# Optimizing a Trainium2 kernel written in Bass

```python
import numpy as np
import jax
import jax.numpy as jnp

def _softmax(x, axis=-1):
    return jax.nn.softmax(x, axis=axis)

def _gelu(x):
    return jax.nn.gelu(x, approximate=True)

def _silu(x):
    return jax.nn.silu(x)

def _sigmoid(x):
    return jax.nn.sigmoid(x)

def _layernorm(x, axis=-1, eps=1e-05):
    m = jnp.mean(x, axis=axis, keepdims=True)
    v = jnp.var(x, axis=axis, keepdims=True)
    return (x - m) / jnp.sqrt(v + eps)

def _scatter_add(tgt, idx, src, axis=0):
    return tgt.at[idx].add(src)

def _segment_sum(src, seg, n):
    return jax.ops.segment_sum(src, seg, n)
kernel_name = 'mk_gnn_resnorm_d2_gnn_r32_c30186'

def setup_inputs(seed: int=0):
    np.random.seed(seed)
    _w = jnp.asarray

    def _rec_inputs():
        import jax
        import jax.numpy as jnp
        _gk = jax.random.key(seed)
        x = -0.0001006 + 1 * jax.random.normal(jax.random.fold_in(_gk, 1), (50000, 96), jnp.float32)
        src = jax.random.randint(jax.random.fold_in(_gk, 2), (50000,), 0, 50000, jnp.int32)
        dst = jax.random.randint(jax.random.fold_in(_gk, 3), (50000,), 0, 50000, jnp.int32)
        _o = jnp.argsort(dst, stable=True)
        src = src[_o]
        dst = dst[_o]
        edge_attr_4 = 0.000714719 + 1.00021 * jax.random.normal(jax.random.fold_in(_gk, 11), (50000, 4), jnp.float32)
        return (x, src, dst, edge_attr_4)
    x, src, dst, edge_attr_4 = _rec_inputs()

    def _L0_gnn_setup():
        import jax, jax.numpy as jnp
        import numpy as np
        EPS = 1e-05

        def _mlp(h, W, b, gamma, beta):
            h = jax.nn.relu(h @ W + b)
            mu = jnp.mean(h, axis=0)
            var = jnp.mean(jnp.square(h - mu), axis=0)
            return gamma * (h - mu) * jax.lax.rsqrt(var + EPS) + beta
        key = jax.random.key(seed)
        ks = jax.random.split(key, 10)
        N, E, C_in, C_out, E_dim = (50000, 25000, 96, 96, 4)
        x = jax.random.normal(ks[0], (N, C_in), dtype=jnp.float32)
        edge_index = jax.random.randint(ks[1], (2, E), 0, N, dtype=jnp.int64)
        edge_attr = jax.random.normal(ks[2], (E, E_dim), dtype=jnp.float32)
        s = lambda fan_in: 1.0 / np.sqrt(fan_in)
        W_node = jax.random.uniform(ks[3], (C_in, C_out), jnp.float32, -s(C_in), s(C_in))
        b_node = jnp.zeros((C_out,), jnp.float32)
        g_node = jnp.ones((C_out,), jnp.float32)
        beta_node = jnp.zeros((C_out,), jnp.float32)
        W_edge = jax.random.uniform(ks[4], (E_dim, C_out), jnp.float32, -s(E_dim), s(E_dim))
        b_edge = jnp.zeros((C_out,), jnp.float32)
        g_edge = jnp.ones((C_out,), jnp.float32)
        beta_edge = jnp.zeros((C_out,), jnp.float32)
        M_in = 2 * C_in + C_out
        W_msg = jax.random.uniform(ks[5], (M_in, C_out), jnp.float32, -s(M_in), s(M_in))
        b_msg = jnp.zeros((C_out,), jnp.float32)
        g_msg = jnp.ones((C_out,), jnp.float32)
        beta_msg = jnp.zeros((C_out,), jnp.float32)
        return dict(x=x, edge_index=edge_index, edge_attr=edge_attr, W_node=W_node, b_node=b_node, g_node=g_node, beta_node=beta_node, W_edge=W_edge, b_edge=b_edge, g_edge=g_edge, beta_edge=beta_edge, W_msg=W_msg, b_msg=b_msg, g_msg=g_msg, beta_msg=beta_msg)
    _L0_gnn_all = _L0_gnn_setup()
    _L0_gnn_in = {k: v for k, v in _L0_gnn_all.items() if k in ('W_node', 'b_node', 'g_node', 'beta_node', 'W_edge', 'b_edge', 'g_edge', 'beta_edge', 'W_msg', 'b_msg', 'g_msg', 'beta_msg')}
    del _L0_gnn_all

    def _L1_gnn_setup():
        import jax, jax.numpy as jnp
        import numpy as np
        N_NODES = 50000

        def gcn_conv(x, src, dst, W, b):
            n = x.shape[0]
            ew = jnp.ones(src.shape[0], dtype=x.dtype)
            deg = jax.ops.segment_sum(ew, dst, num_segments=n)
            dinv = jnp.where(deg > 0, jax.lax.rsqrt(deg), 0.0).astype(x.dtype)
            norm = dinv[src] * dinv[dst]
            xw = x @ W
            msg = xw[src] * norm[:, None]
            out = jax.ops.segment_sum(msg, dst, num_segments=n)
            return out + b

        def prelu(x, a):
            return jnp.where(x > 0, x, a * x)
        key = jax.random.key(seed)
        k1, k2, k3, k4 = jax.random.split(key, 4)
        in_dim = z_dim = 96
        n_edges = 25000
        x = jax.random.normal(k1, (N_NODES, in_dim), dtype=jnp.float32)
        edge_index = jax.random.randint(k2, (2, n_edges), 0, N_NODES, dtype=jnp.int32)
        s1 = 1.0 / np.sqrt(in_dim)
        W1 = jax.random.uniform(k3, (in_dim, z_dim), jnp.float32, -s1, s1)
        W2 = jax.random.uniform(k4, (z_dim, z_dim), jnp.float32, -s1, s1)
        b1 = jnp.zeros((z_dim,), jnp.float32)
        b2 = jnp.zeros((z_dim,), jnp.float32)
        prelu_a = jnp.full((z_dim,), 0.25, jnp.float32)
        return {'x': x, 'edge_index': edge_index, 'W1': W1, 'b1': b1, 'W2': W2, 'b2': b2, 'prelu_a': prelu_a}
    _L1_gnn_all = _L1_gnn_setup()
    _L1_gnn_in = {k: v for k, v in _L1_gnn_all.items() if k in ('W1', 'b1', 'W2', 'b2', 'prelu_a')}
    del _L1_gnn_all
    return {'x': x, 'src': src, 'dst': dst, 'edge_attr_4': edge_attr_4, 'L0_gnn_W_node': _L0_gnn_in['W_node'], 'L0_gnn_b_node': _L0_gnn_in['b_node'], 'L0_gnn_g_node': _L0_gnn_in['g_node'], 'L0_gnn_beta_node': _L0_gnn_in['beta_node'], 'L0_gnn_W_edge': _L0_gnn_in['W_edge'], 'L0_gnn_b_edge': _L0_gnn_in['b_edge'], 'L0_gnn_g_edge': _L0_gnn_in['g_edge'], 'L0_gnn_beta_edge': _L0_gnn_in['beta_edge'], 'L0_gnn_W_msg': _L0_gnn_in['W_msg'], 'L0_gnn_b_msg': _L0_gnn_in['b_msg'], 'L0_gnn_g_msg': _L0_gnn_in['g_msg'], 'L0_gnn_beta_msg': _L0_gnn_in['beta_msg'], 'L1_gnn_W1': _L1_gnn_in['W1'], 'L1_gnn_b1': _L1_gnn_in['b1'], 'L1_gnn_W2': _L1_gnn_in['W2'], 'L1_gnn_b2': _L1_gnn_in['b2'], 'L1_gnn_prelu_a': _L1_gnn_in['prelu_a']}

def reference(x, src, dst, edge_attr_4, L0_gnn_W_node, L0_gnn_b_node, L0_gnn_g_node, L0_gnn_beta_node, L0_gnn_W_edge, L0_gnn_b_edge, L0_gnn_g_edge, L0_gnn_beta_edge, L0_gnn_W_msg, L0_gnn_b_msg, L0_gnn_g_msg, L0_gnn_beta_msg, L1_gnn_W1, L1_gnn_b1, L1_gnn_W2, L1_gnn_b2, L1_gnn_prelu_a):
    import jax
    import jax.numpy as jnp

    def _L0_gnn_ref(x, edge_index, edge_attr, W_node, b_node, g_node, beta_node, W_edge, b_edge, g_edge, beta_edge, W_msg, b_msg, g_msg, beta_msg):
        import jax, jax.numpy as jnp
        import numpy as np
        EPS = 1e-05

        def _mlp(h, W, b, gamma, beta):
            h = jax.nn.relu(h @ W + b)
            mu = jnp.mean(h, axis=0)
            var = jnp.mean(jnp.square(h - mu), axis=0)
            return gamma * (h - mu) * jax.lax.rsqrt(var + EPS) + beta
        node_feat = _mlp(x, W_node, b_node, g_node, beta_node)
        edge_feat = _mlp(edge_attr, W_edge, b_edge, g_edge, beta_edge)
        row, col = (edge_index[0], edge_index[1])
        message = jnp.concatenate([x[row], x[col], edge_feat], axis=1)
        message = _mlp(message, W_msg, b_msg, g_msg, beta_msg)
        agg = jax.ops.segment_sum(message, col, num_segments=node_feat.shape[0])
        return agg + node_feat

    def _L1_gnn_ref(x, edge_index, W1, b1, W2, b2, prelu_a):
        import jax, jax.numpy as jnp
        import numpy as np
        N_NODES = 50000

        def gcn_conv(x, src, dst, W, b):
            n = x.shape[0]
            ew = jnp.ones(src.shape[0], dtype=x.dtype)
            deg = jax.ops.segment_sum(ew, dst, num_segments=n)
            dinv = jnp.where(deg > 0, jax.lax.rsqrt(deg), 0.0).astype(x.dtype)
            norm = dinv[src] * dinv[dst]
            xw = x @ W
            msg = xw[src] * norm[:, None]
            out = jax.ops.segment_sum(msg, dst, num_segments=n)
            return out + b

        def prelu(x, a):
            return jnp.where(x > 0, x, a * x)
        n = x.shape[0]
        loop = jnp.arange(n, dtype=edge_index.dtype)
        src = jnp.concatenate([edge_index[0], loop])
        dst = jnp.concatenate([edge_index[1], loop])
        h = prelu(gcn_conv(x, src, dst, W1, b1), prelu_a)
        h = prelu(gcn_conv(h, src, dst, W2, b2), prelu_a)
        return h
    edge_index = jnp.stack([src, dst])
    x = _layernorm(x + _L0_gnn_ref(x, edge_index, edge_attr_4, L0_gnn_W_node, L0_gnn_b_node, L0_gnn_g_node, L0_gnn_beta_node, L0_gnn_W_edge, L0_gnn_b_edge, L0_gnn_g_edge, L0_gnn_beta_edge, L0_gnn_W_msg, L0_gnn_b_msg, L0_gnn_g_msg, L0_gnn_beta_msg), axis=-1)
    x = _layernorm(x + _L1_gnn_ref(x, edge_index, L1_gnn_W1, L1_gnn_b1, L1_gnn_W2, L1_gnn_b2, L1_gnn_prelu_a), axis=-1)
    return x

_drawn_inputs = setup_inputs


def setup_inputs(seed=0):
    import zlib

    import numpy as np

    out = dict(_drawn_inputs(seed))
    spreads = {'L0_gnn_b_node': (0.0, 0.1),
     'L0_gnn_g_node': (1.0, 0.2),
     'L0_gnn_beta_node': (0.0, 0.1),
     'L0_gnn_b_edge': (0.0, 0.1),
     'L0_gnn_g_edge': (1.0, 0.2),
     'L0_gnn_beta_edge': (0.0, 0.437),
     'L0_gnn_b_msg': (0.0, 0.1),
     'L0_gnn_g_msg': (1.0, 0.2),
     'L0_gnn_beta_msg': (0.0, 0.1),
     'L1_gnn_b1': (0.0, 0.1),
     'L1_gnn_b2': (0.0, 0.1),
     'L1_gnn_prelu_a': (0.25, 0.6)}
    factors = {}
    for name, (base, spread) in spreads.items():
        noise = np.random.default_rng([zlib.crc32(name.encode()), seed]).standard_normal(out[name].shape)
        drawn = base * np.exp(spread * noise) if base else spread * noise
        out[name] = jnp.asarray(drawn.astype(out[name].dtype))
    for name, factor in factors.items():
        out[name] = (out[name] * factor).astype(out[name].dtype)
    return out
```

```python
from contextlib import ExitStack

import concourse.bass as bass
from concourse import mybir

P = 128
C = 96
R = C + 2
CNT, DST = C, C + 1
HALF = 4
COLS = HALF * P
WINDOW = 3
WIN = WINDOW * P
EPS = 1e-5

F32 = mybir.dt.float32
BF16 = mybir.dt.bfloat16
I32 = mybir.dt.int32
ALU = mybir.AluOpType
ACT = mybir.ActivationFunctionType


def rounds(eng, n, body, ahead=1):
    for it in range(min(ahead, n)):
        body(it)
    if n > ahead:
        with eng.Fori(ahead, n) as it:
            body(it)


def peeled(it):
    return isinstance(it, int)


def later(it):
    return not (peeled(it) and it == 0)


def wide(ap, n):
    return ap.unsqueeze(2).to_broadcast([ap.shape[0], ap.shape[1], n])


def rowwise(ap, k):
    return ap.unsqueeze(1).to_broadcast([ap.shape[0], k, ap.shape[1]])


def build_program(nc, n, a, out):
    n_pad = out.shape[0]
    groups = n_pad // (2 * COLS)
    chunks = n_pad // P
    full = n // P
    rest = n - full * P
    last_cols = n - (2 * groups - 1) * COLS
    his = -(-chunks // P)
    area = n_pad + WIN
    assert 0 < last_cols <= COLS and rest > 0 and full <= 512

    rows = nc.dram_tensor("rows", [area + chunks // 2 * WIN, R], F32, kind="Internal").ap()
    z_tab = [nc.dram_tensor(f"z{i}", [n_pad, C], F32, kind="Internal").ap() for i in (1, 2)]
    x1_tab = nc.dram_tensor("x1", [n_pad, C], F32, kind="Internal").ap()
    lo_tab = nc.dram_tensor("lo", [his * P, 2], I32, kind="Internal").ap()

    with ExitStack() as ctx:
        def maker(c, prefix=""):
            return lambda name, shape, dt=F32: c.enter_context(nc.sbuf_tensor(prefix + name, shape, dt))

        def semaphores(c, prefix=""):
            held = []

            def sem(name):
                held.append(c.enter_context(nc.semaphore(prefix + name)))
                return held[-1]

            c.callback(clear, held)
            return sem, lambda name: [sem(f"{name}_{i}") for i in range(2)]

        def clear(held):
            with nc.Block() as between:
                @between.gpsimd
                def _(pool):
                    for one in held:
                        pool.sem_clear(one)

        gathered_msg = [ctx.enter_context(nc.semaphore(f"gathered_msg{i}")) for i in range(2)]
        pool_sems = {k: [ctx.enter_context(nc.semaphore(f"l{k}_{m}")) for m in ("gathered0", "gathered1", "gathered2", "rows_in")]
                     for k in (1, 2)}

        sb = maker(ctx)
        bank = [ctx.enter_context(nc.psum_tensor(f"bank{i}", [P, 512], F32)) for i in range(8)]

        iota_f = sb("iota_f", [P, P])
        part_f = sb("part_f", [P, 1])
        ident = sb("ident", [P, P])
        base = sb("base", [P, 2 * groups])
        ends_i = sb("ends_i", [P, 2, chunks], I32)
        lo_i = sb("lo_i", [1, his * P * 2], I32)
        flag_i = sb("flag_i", [1, 1], I32)
        w_node = sb("w_node", [C + 1, C])
        w1 = sb("w1", [C, C])
        w2 = sb("w2", [C, C])
        rowp = sb("rowp", [P, 6, C])
        dinv = sb("dinv", [P, chunks])
        w_res = sb("w_res", [C + 1, C])

        with ExitStack() as c1:
            sb1 = maker(c1)
            sem, pair = semaphores(c1, "m_")
            msg = sb1("msg", [P, chunks, R])
            tiles_f = sb1("tiles_f", [P, 2, chunks])
            part_i = sb1("part_i", [P, 1], I32)
            iota_i = sb1("iota_i", [P, P], I32)
            pairs_i = sb1("pairs_i", [P, P + 1], I32)
            same_pair = sb1("same_pair", [P, P + 1])
            base_i = sb1("base_i", [P, 2 * groups], I32)
            idx = sb1("idx", [P, 2, 2, HALF], I32)
            g_rows = sb1("g_rows", [P, 2, 2, HALF, C])
            free = g_rows[:].rearrange("p s w u c -> p (s w u c)")
            ints = free[:, 0:2 * chunks].bitcast(I32).rearrange("p (k n) -> p k n", k=2)
            mst = free[:, 0:6 * C].rearrange("p (c k) -> p c k", k=6)
            mmv = free[:, 6 * C:8 * C].rearrange("p (k c) -> p k c", k=2)
            diag = free[0:C, 10 * C:14 * C].rearrange("p (k c) -> p k c", k=4)
            m_dev, m_tail = free[:, 8 * C:9 * C], free[:, 9 * C:10 * C]
            g_cols = sb1("g_cols", [C, 2, COLS])
            feat = sb1("feat", [C + 1, COLS])
            ea = sb1("ea", [P, 2, COLS])
            xc = sb1("xc", [C + 1, 2, COLS])
            h = sb1("h", [C, 2, COLS])
            st = sb1("st", [C, 2 * groups, 6])
            hot_a = sb1("hot_a", [P, 2, HALF, P], BF16)
            hot_b = sb1("hot_b", [P, 2, HALF, his], BF16)
            ones = sb1("ones", [P, P])
            m_full = sb1("m_full", [P, P])
            m_one = sb1("m_one", [P, P])
            zeros = sb1("zeros", [P, P], BF16)
            before = sb1("before", [P, P])
            pads = sb1("pads", [P, WINDOW, R])
            w_edge = sb1("w_edge", [P, C])
            w_src = sb1("w_src", [C, C])
            w_dst = sb1("w_dst", [C, C])
            w_ef = sb1("w_ef", [C + 1, C])
            b_msg = sb1("b_msg", [1, C])
            gb = sb1("gb", [C, 6])
            mv = sb1("mv", [C, 3, 2])
            sc = sb1("sc", [C, 3, 4])
            tab = sb1("tab", [P, 10, his])
            bad = sb1("bad", [P, 2])
            tab_i = sb1("tab_i", [P, his, 4], I32)
            w_raw = sb1("w_raw", [C, C])

            loaded = sem("loaded"); iotas = sem("iotas"); consts = sem("consts")
            ea_in = pair("ea_in"); ea_used = pair("ea_used"); e_relu = pair("e_relu"); e_stat = pair("e_stat")
            idx_set = pair("idx_set"); gathered = gathered_msg; turned = pair("turned")
            src_cols = pair("src_cols"); dst_cols = pair("dst_cols")
            mea_in = pair("mea_in"); e_layer = pair("e_layer"); feat_set = pair("feat_set")
            xc_in = pair("xc_in"); n_layer = pair("n_layer"); n_relu = pair("n_relu"); n_stat = pair("n_stat")
            pre = pair("pre"); msg_set = pair("msg_set"); stored = sem("stored")
            hot_set = pair("hot_set"); counted = pair("counted")
            steps = sem("steps"); root = sem("root"); m_stat = sem("m_stat"); copied = pair("copied")
            p_shift = sem("p_shift"); p_tab = sem("p_tab"); p_before = sem("p_before"); p_pairs = sem("p_pairs"); p_mean = sem("p_mean")
            p_var = sem("p_var"); passed = sem("passed"); p_rows = sem("p_rows")

            ps_t, ps_f, ps_p, ps_tab, ps_s = bank[0:2], bank[2:4], bank[4:6], bank[6], bank[7]
            loads = [(ends_i[:, 1, :], a["dst"]), (ints[:, 1, 0:chunks], a["dst_next"]), (ends_i[:, 0, :], a["src"]),
                     (w_edge[0:4, :], a["W_edge"]), (w_edge[4:5, :], a["b_edge"]),
                     (w_node[0:C, :], a["W_node"]), (w_node[C:C + 1, :], a["b_node"]),
                     (w_src, a["W_msg"][0:C, :]), (w_dst, a["W_msg"][C:2 * C, :]),
                     (w_ef[0:C, :], a["W_msg"][2 * C:3 * C, :]), (b_msg, a["b_msg"]),
                     (w1, a["W1"]), (w2, a["W2"]), (gb, a["gb"])]
            loads += [(rowp[:, i, :], a[k].to_broadcast([P, C])) for i, k in enumerate(("b1", "b2", "prelu"))]
            all_loaded = 16 * len(loads)

            block = c1.enter_context(nc.Block())
            when = {}

            @block.vector
            def _(dve):
                V = nc.vector
                done = [0]

                def step(ins, name=None):
                    done[0] += 1
                    ins.then_inc(steps, 1)
                    dve.wait_ge(steps, done[0])
                    if name:
                        when[name] = done[0]

                dve.wait_ge(iotas, 4)
                step(V.memset(ea[:], 0.0), "zeros")
                step(V.tensor_copy(part_f[:], part_i[:]))
                step(V.tensor_copy(base[:], base_i[:]))
                step(V.memset(ones[:], 1.0))
                step(V.memset(m_full[:], full / n))
                step(V.memset(m_one[:], 1.0 / n))
                step(V.memset(feat[C:C + 1, :], 1.0))
                step(V.memset(msg[:, :, CNT:CNT + 1], 1.0))
                step(V.memset(pads[:], 0.0))
                step(V.memset(pads[:, :, DST:DST + 1], float(n_pad - 1)), "pads")
                step(V.memset(zeros[:], 0.0))
                step(V.tensor_copy(iota_f[:], iota_i[:]))
                step(V.tensor_scalar(ident[:], iota_f[:], part_f[:, 0:1], None, ALU.is_equal))
                step(V.tensor_copy(w_res[0:C, :], ident[0:C, 0:C]))
                step(V.tensor_scalar(before[:], iota_f[:], part_f[:, 0:1], None, ALU.is_gt))
                step(V.tensor_scalar(pairs_i[:, 0:P], iota_i[:], 1, None, ALU.arith_shift_right))
                step(V.tensor_scalar(pairs_i[:, P:], part_i[:], 1, None, ALU.arith_shift_right))
                step(V.tensor_copy(same_pair[:], pairs_i[:]))
                step(V.tensor_scalar(same_pair[:, 0:P], same_pair[:, 0:P], same_pair[:, P:P + 1], None, ALU.is_equal))
                dve.wait_ge(loaded, all_loaded)
                step(V.tensor_copy(msg[:, :, DST], ends_i[:, 1, :]))
                step(V.tensor_tensor(tiles_f[:, 0, :], ints[:, 1, 0:chunks], msg[:, :, DST], ALU.is_lt))
                step(V.tensor_reduce(bad[:, 1:2], tiles_f[:, 0, :], mybir.AxisListType.X, ALU.add))
                step(V.tensor_scalar(ints[:, 0, 0:chunks], ends_i[:, 1, :], 7, 127, ALU.arith_shift_right, ALU.bitwise_and))
                step(V.tensor_scalar(ints[:, 1, 0:chunks], ends_i[:, 1, :], 14, None, ALU.arith_shift_right))
                step(V.tensor_copy(tiles_f[:], ints[:, :, 0:chunks]))
                step(V.tensor_copy(w_raw[:], w_ef[0:C, :]), "consts")

                def edge_stats(it):
                    for s in range(2):
                        dve.wait_ge(e_relu[s], it + 1)
                        V.bn_stats(st[:, bass.ds(it * 2 + s, 1), :].rearrange("p a k -> p (a k)"),
                                   h[:, s, :]).then_inc(e_stat[s], 1)
                rounds(dve, groups, edge_stats)

                def scale_shift(k):
                    step(V.tensor_tensor(sc[:, k, 2:3], sc[:, k, 1:2], gb[:, 2 * k:2 * k + 1], ALU.mult))
                    step(V.tensor_tensor(sc[:, k, 0:1], mv[:, k, 0:1], sc[:, k, 2:3], ALU.mult))
                    step(V.tensor_tensor(sc[:, k, 3:4], gb[:, 2 * k + 1:2 * k + 2], sc[:, k, 0:1], ALU.subtract), f"shift{k}")

                for s in range(2):
                    dve.wait_ge(e_stat[s], groups)
                step(V.bn_stats(st[:, 2 * groups - 1, :], h[:, 1, 0:last_cols]), "e_stats")
                step(V.bn_aggr(mv[:, 0, :], st[:].rearrange("p a k -> p (a k)")))
                step(V.tensor_scalar(sc[:, 0, 0:1], mv[:, 0, 1:2], EPS, None, ALU.add))
                step(V.reciprocal(sc[:, 0, 0:1], sc[:, 0, 0:1]), "e_var")
                dve.wait_ge(root, 1)
                scale_shift(0)
                step(V.tensor_scalar(w_ef[0:C, :], w_raw[:], sc[:, 0, 2:3], None, ALU.mult))
                dve.wait_ge(p_shift, 1)
                step(V.tensor_tensor(w_ef[C:C + 1, :], ps_s[0:1, 0:C], b_msg[:], ALU.add), "w_ef")

                def messages(it):
                    first = peeled(it)
                    for s in range(2):
                        at = it * (2 * HALF) + s * HALF
                        if not first:
                            dve.wait_ge(counted[s], it)
                        V.tensor_tensor(hot_a[:, s], wide(tiles_f[:, 0, bass.ds(at, HALF)], P),
                                        rowwise(iota_f[:], HALF), ALU.is_equal).then_inc(hot_set[s], 1)
                        V.tensor_tensor(hot_b[:, s], wide(tiles_f[:, 1, bass.ds(at, HALF)], his),
                                        rowwise(iota_f[:, 0:his], HALF), ALU.is_equal).then_inc(hot_set[s], 1)
                        dve.wait_ge(turned[s], it * 2 + 2)
                        if not first or s:
                            dve.wait_ge(pre[1 - s], it + s)
                        V.tensor_copy(g_cols[:, 1, :], ps_t[1][0:C, :]).then_inc(dst_cols[s], 1)
                        dve.wait_ge(n_relu[s], it + 1)
                        V.bn_stats(st[:, bass.ds(it * 2 + s, 1), :].rearrange("p a k -> p (a k)"),
                                   h[:, s, :]).then_inc(n_stat[s], 1)
                rounds(dve, groups, messages)
                for s in range(2):
                    dve.wait_ge(n_stat[s], groups)
                step(V.bn_stats(st[:, 2 * groups - 1, :], h[:, 1, 0:last_cols]))
                step(V.bn_aggr(mv[:, 2, :], st[:].rearrange("p a k -> p (a k)")))

                dve.wait_ge(p_tab, 1)
                step(V.tensor_copy(tab[:, 0, :], ps_tab[:, 0:his]), "counts")
                dve.wait_ge(p_pairs, 1)
                step(V.tensor_scalar(tab[:, 1, :], ps_s[:, 0:his], float(WIN), None, ALU.is_gt))
                step(V.tensor_reduce(bad[:, 0:1], tab[:, 1, :], mybir.AxisListType.X, ALU.add))
                step(V.tensor_tensor(bad[:, 0:1], bad[:, 0:1], bad[:, 1:2], ALU.add), "bad")
                dve.wait_ge(p_before, 1)
                step(V.memset(tab[:, 2, :], 0.0))
                for b in range(1, his):
                    step(V.tensor_tensor(tab[:, 2, b:b + 1], tab[:, 2, b - 1:b], ps_s[:, 8 + b - 1:8 + b], ALU.add))
                step(V.tensor_tensor(tab[:, 3, :], tab[:, 2, :], ps_s[:, 0:his], ALU.add))
                step(V.tensor_scalar(bad[:, 0:1], ps_s[:, 16:17], 1.0, None, ALU.min))
                step(V.tensor_copy(flag_i[:], bad[0:1, 0:1]))
                for b in range(his):
                    step(V.tensor_scalar(tab[:, 4, b:b + 1], part_f[:], float(WIN // 2), float(area + b * P * WIN // 2), ALU.mult, ALU.add))
                step(V.tensor_tensor(tab[:, 5, :], tab[:, 4, :], tab[:, 3, :], ALU.subtract))
                step(V.scalar_tensor_tensor(tab[:, 6, :], tab[:, 5, :], bad[:, 0:1], tab[:, 3, :], ALU.mult, ALU.add))
                step(V.tensor_copy(tab_i[:, :, 2], tab[:, 6, :]))
                step(V.tensor_scalar(tab[:, 7, :], tab[:, 3, :], float(WIN - 1), None, ALU.add))
                step(V.tensor_copy(tab_i[:, :, 0], tab[:, 7, :]))
                step(V.tensor_scalar(tab_i[:, :, 1], tab_i[:, :, 0], 10, None, ALU.arith_shift_right))
                step(V.tensor_copy(tab[:, 8, :], tab_i[:, :, 1]))
                step(V.tensor_scalar(tab[:, 8, :], tab[:, 8, :], float(groups - 1), 16.0, ALU.min, ALU.mult))
                step(V.tensor_scalar(tab[:, 8, :], tab[:, 8, :], 16.0, None, ALU.add))
                step(V.tensor_copy(tab_i[:, :, 3], tab[:, 8, :]), "windows")

                for s in range(2):
                    dve.wait_ge(msg_set[s], groups)
                with dve.Fori(0, C) as c:
                    V.bn_stats(mst[:, bass.ds(c, 1), :].rearrange("p a k -> p (a k)"),
                               msg[:, 0:full, bass.ds(c, 1)].rearrange("p e a -> p (e a)")).then_inc(m_stat, 1)
                dve.wait_ge(m_stat, C)
                even, odd = (full + 1) // 2, full // 2
                step(V.tensor_scalar(mmv[:, 0, :], mst[:, :, 4], odd / full, None, ALU.mult))
                step(V.scalar_tensor_tensor(mmv[:, 0, :], mst[:, :, 1], even / full, mmv[:, 0, :], ALU.mult, ALU.add), "m_means")
                step(V.tensor_tensor(m_dev[:], mst[:, :, 1], mst[:, :, 4], ALU.subtract))
                step(V.tensor_tensor(m_dev[:], m_dev[:], m_dev[:], ALU.mult))
                step(V.tensor_tensor(mmv[:, 1, :], mst[:, :, 2], mst[:, :, 5], ALU.add))
                step(V.scalar_tensor_tensor(mmv[:, 1, :], m_dev[:], even * odd / full, mmv[:, 1, :], ALU.mult, ALU.add))
                step(V.tensor_scalar(mmv[:, 1, :], mmv[:, 1, :], 1.0 / full, None, ALU.mult))
                step(V.tensor_copy(m_dev[:], mmv[:, 0, :]))
                dve.wait_ge(p_mean, 1)
                step(V.tensor_tensor(m_dev[:], m_dev[:], ps_p[0][:, 0:C], ALU.subtract))
                step(V.tensor_tensor(m_dev[:], m_dev[:], m_dev[:], ALU.mult))
                step(V.tensor_tensor(m_dev[:], m_dev[:], mmv[:, 1, :], ALU.add))
                step(V.tensor_tensor(m_tail[0:rest, :], msg[0:rest, full, 0:C], ps_p[0][0:rest, 0:C], ALU.subtract))
                step(V.tensor_tensor(m_tail[0:rest, :], m_tail[0:rest, :], m_tail[0:rest, :], ALU.mult), "m_devs")
                dve.wait_ge(p_var, 1)
                step(V.tensor_copy(mv[:, 1, 0:1], ps_p[1][0:C, 0:1]))
                step(V.tensor_copy(mv[:, 1, 1:2], ps_p[1][0:C, 2:3]))
                step(V.tensor_scalar(sc[:, 1:3, 0], mv[:, 1:3, 1], EPS, None, ALU.add))
                step(V.reciprocal(sc[:, 1:3, 0], sc[:, 1:3, 0]), "mn_var")
                dve.wait_ge(root, 2)
                scale_shift(1)
                scale_shift(2)
                for i, (k, w) in enumerate(((2, 2), (1, 2), (1, 3), (2, 3))):
                    step(V.tensor_scalar(diag[:, i, :], ident[0:C, 0:C], sc[:, k, w:w + 1], None, ALU.mult), "diags")
                dve.wait_ge(p_rows, 1)
                step(V.tensor_copy(rowp[:, 3:6, :], ps_s[:, 0:3 * C].rearrange("p (k c) -> p k c", k=3)))
                step(V.tensor_copy(w_res[C:C + 1, :], ps_s[C:C + 1, 3 * C:4 * C]))

            @block.sync
            def _(sp):
                sp.wait_ge(iotas, 4)
                for to, of in loads:
                    sp.dma_start(to[:], of).then_inc(loaded, 16)

                sp.wait_ge(steps, when["zeros"])

                def edge_stats(it):
                    at = [it * (2 * COLS) + s * COLS if peeled(it) else sp.snap(it * (2 * COLS) + s * COLS) for s in range(2)]
                    for s in range(2):
                        if not peeled(it):
                            sp.wait_ge(ea_used[s], it)
                        sp.dma_start(ea[0:5, s, :], a["eaT"][:, bass.ds(at[s], COLS)]).then_inc(ea_in[s], 16)
                rounds(sp, groups, edge_stats)

                def messages(it):
                    at = [it * (2 * COLS) + s * COLS if peeled(it) else sp.snap(it * (2 * COLS) + s * COLS) for s in range(2)]
                    for s in range(2):
                        if peeled(it):
                            sp.wait_ge(ea_used[s], groups)
                        else:
                            sp.wait_ge(e_layer[s], it)
                        sp.dma_start(ea[0:5, s, :], a["eaT"][:, bass.ds(at[s], COLS)]).then_inc(mea_in[s], 16)
                        if not peeled(it):
                            sp.wait_ge(n_layer[s], it)
                        sp.dma_start(xc[:, s, :], a["xT"][:, bass.ds(at[s], COLS)]).then_inc(xc_in[s], 16)
                rounds(sp, groups, messages)
            @block.gpsimd
            def _(pool):
                nc.gpsimd.memset(w_edge[:], 0.0).then_inc(iotas, 1)
                nc.gpsimd.iota(iota_i[:], [[1, P]], base=0, channel_multiplier=0).then_inc(iotas, 1)
                nc.gpsimd.iota(part_i[:], [[0, 1]], base=0, channel_multiplier=1).then_inc(iotas, 1)
                nc.gpsimd.iota(base_i[:], [[COLS, 2 * groups]], base=0, channel_multiplier=0).then_inc(iotas, 1)
                pool.wait_ge(steps, when["consts"])

                def indices(it, s):
                    nc.gpsimd.tensor_copy(idx[:, s], ends_i[:, :, bass.ds(it * (2 * HALF) + s * HALF, HALF)]).then_inc(copied[s], 1)

                def gathers(it, last=False):
                    for s in range(2):
                        if later(it):
                            pool.wait_ge(turned[s], it * 2)
                        pool.wait_ge(copied[s], it + 1)
                        if not peeled(it):
                            pool.sem_inc(passed, 1)
                        for w in range(2):
                            for u in range(HALF):
                                nc.gpsimd.indirect_dma_start(
                                    g_rows[:, s, w, u, :], None, a["x"],
                                    bass.IndirectOffsetOnAxis(idx[:, s, w, u:u + 1], axis=0),
                                ).then_inc(gathered[s], 16)
                            if w == 0 and not (last and s):
                                if s or later(it):
                                    pool.wait_ge(gathered[1 - s], (it + s) * (16 * 2 * HALF))
                                    if not peeled(it):
                                        pool.sem_inc(passed, 1)
                                indices(it + s, 1 - s)
                indices(0, 0)
                rounds(pool, groups - 1, gathers)
                gathers(groups - 1, last=True)

            @block.tensor
            def _(pe):
                T = nc.tensor
                pe.wait_ge(steps, when["consts"])

                def edge_stats(it):
                    for s in range(2):
                        pe.wait_ge(ea_in[s], it * 16 + 16)
                        if not peeled(it):
                            pe.wait_ge(e_relu[s], it)
                        T.matmul(ps_f[s][0:C, :], w_edge[:], ea[:, s, :], start=True, stop=True).then_inc(ea_used[s], 1)
                rounds(pe, groups, edge_stats)

                pe.wait_ge(steps, when["shift0"])
                T.matmul(ps_s[0:1, 0:C], sc[:, 0, 3:4], w_raw[:], start=True, stop=True).then_inc(p_shift, 1)

                def messages(it):
                    first = peeled(it)
                    for s in range(2):
                        pe.wait_ge(gathered[s], it * (16 * 2 * HALF) + 16 * 2 * HALF)
                        if not first or s:
                            pe.wait_ge(src_cols[1 - s], it + s)
                        for u in range(HALF):
                            last = T.transpose(ps_t[0][0:C, u * P:(u + 1) * P], g_rows[:, s, 0, u, :], ident[:])
                        last.then_inc(turned[s], 1)
                        if not first or s:
                            pe.wait_ge(dst_cols[1 - s], it + s)
                        for u in range(HALF):
                            last = T.transpose(ps_t[1][0:C, u * P:(u + 1) * P], g_rows[:, s, 1, u, :], ident[:])
                        last.then_inc(turned[s], 1)
                        pe.wait_ge(mea_in[s], it * 16 + 16)
                        if first and s == 0:
                            pe.wait_ge(e_relu[0], groups)
                        else:
                            pe.wait_ge(feat_set[1 - s], it + s)
                        T.matmul(ps_f[0][0:C, :], w_edge[:], ea[:, s, :], start=True, stop=True).then_inc(e_layer[s], 1)
                        pe.wait_ge(xc_in[s], it * 16 + 16)
                        if first and s == 0:
                            pe.wait_ge(e_relu[1], groups)
                        else:
                            pe.wait_ge(n_relu[1 - s], it + s)
                        T.matmul(ps_f[1][0:C, :], w_node[:], xc[:, s, :], start=True, stop=True).then_inc(n_layer[s], 1)
                        pe.wait_ge(hot_set[s], it * 2 + 2)
                        for u in range(HALF):
                            last = T.matmul(ps_tab[:, 0:his], hot_a[:, s, u, :], hot_b[:, s, u, :],
                                            start=(first and s == 0 and u == 0), stop=False)
                        last.then_inc(counted[s], 1)
                        pe.wait_ge(src_cols[s], it + 1)
                        pe.wait_ge(dst_cols[s], it + 1)
                        pe.wait_ge(feat_set[s], it + 1)
                        if first and s == 0:
                            pe.wait_ge(steps, when["w_ef"])
                        if not first:
                            pe.wait_ge(msg_set[s], it)
                        for u in range(HALF):
                            o = ps_p[s][:, u * C:(u + 1) * C]
                            e = slice(u * P, (u + 1) * P)
                            T.matmul(o, g_cols[:, 0, e], w_src[:], start=True, stop=False)
                            T.matmul(o, g_cols[:, 1, e], w_dst[:], start=False, stop=False)
                            last = T.matmul(o, feat[:, e], w_ef[:], start=False, stop=True)
                        last.then_inc(pre[s], 1)
                rounds(pe, groups, messages)
                T.matmul(ps_tab[:, 0:his], zeros[:], zeros[:, 0:his], start=False, stop=True).then_inc(p_tab, 1)
                pe.wait_ge(steps, when["counts"])
                T.matmul(ps_s[:, 0:his], same_pair[:, 0:P], tab[:, 0, :], start=True, stop=True).then_inc(p_pairs, 1)
                pe.wait_ge(steps, when["bad"])
                T.matmul(ps_s[:, 0:his], before[:], tab[:, 0, :], start=True, stop=True)
                T.matmul(ps_s[:, 8:8 + his], ones[:], tab[:, 0, :], start=True, stop=True)
                T.matmul(ps_s[:, 16:17], ones[:], bad[:, 0:1], start=True, stop=True).then_inc(p_before, 1)
                pe.wait_ge(steps, when["m_means"])
                for s in range(2):
                    pe.wait_ge(msg_set[s], groups)
                T.matmul(ps_p[0][:, 0:C], m_full[:], mmv[:, 0, :], start=True, stop=False)
                T.matmul(ps_p[0][:, 0:C], m_one[0:rest, :], msg[0:rest, full, 0:C], start=False, stop=True)
                T.matmul(ps_p[1][0:C, 0:1], mmv[:, 0, :], m_full[:, 0:1], start=True, stop=False)
                T.matmul(ps_p[1][0:C, 0:1], msg[0:rest, full, 0:C], m_one[0:rest, 0:1], start=False, stop=True).then_inc(p_mean, 1)
                pe.wait_ge(steps, when["m_devs"])
                T.matmul(ps_p[1][0:C, 2:3], m_dev[:], m_full[:, 0:1], start=True, stop=False)
                T.matmul(ps_p[1][0:C, 2:3], m_tail[0:rest, :], m_one[0:rest, 0:1], start=False, stop=True).then_inc(p_var, 1)
                pe.wait_ge(steps, when["diags"])
                T.matmul(ps_s[:, 0:4 * C], ones[0:C, :], diag.rearrange("p k c -> p (k c)"), start=True, stop=True).then_inc(p_rows, 1)

            @block.scalar
            def _(act):
                def edge_stats(it):
                    for s in range(2):
                        act.wait_ge(ea_used[s], it + 1)
                        if not peeled(it):
                            act.wait_ge(e_stat[s], it)
                        nc.scalar.activation(h[:, s, :], ps_f[s][0:C, :], ACT.Relu).then_inc(e_relu[s], 1)
                rounds(act, groups, edge_stats)
                act.wait_ge(steps, when["e_var"])
                nc.scalar.activation(sc[:, 0, 1:2], sc[:, 0, 0:1], ACT.Sqrt).then_inc(root, 1)

                def messages(it):
                    first = peeled(it)
                    for s in range(2):
                        act.wait_ge(turned[s], it * 2 + 1)
                        if not first or s:
                            act.wait_ge(pre[1 - s], it + s)
                        nc.scalar.copy(g_cols[:, 0, :], ps_t[0][0:C, :]).then_inc(src_cols[s], 1)
                        act.wait_ge(e_layer[s], it + 1)
                        nc.scalar.activation(feat[0:C, :], ps_f[0][0:C, :], ACT.Relu).then_inc(feat_set[s], 1)
                        act.wait_ge(n_layer[s], it + 1)
                        if first:
                            act.wait_ge(steps, when["e_stats"])
                        else:
                            act.wait_ge(n_stat[s], it)
                        nc.scalar.activation(h[:, s, :], ps_f[1][0:C, :], ACT.Relu).then_inc(n_relu[s], 1)
                        act.wait_ge(pre[s], it + 1)
                        nc.scalar.activation(
                            msg[:, bass.ds(it * (2 * HALF) + s * HALF, HALF), 0:C],
                            ps_p[s][:, 0:HALF * C].rearrange("p (u c) -> p u c", u=HALF), ACT.Relu).then_inc(msg_set[s], 1)
                    for s in range(2):
                        act.wait_ge(msg_set[s], it + 1)
                    act.dma_start(rows[bass.ds(it * (2 * COLS), 2 * COLS), :].rearrange("(u p) c -> p u c", p=P),
                                  msg[:, bass.ds(it * (2 * HALF), 2 * HALF), :]).then_inc(stored, 16)
                act.wait_ge(steps, when["consts"])
                rounds(act, groups, messages)
                act.dma_start(rows[n_pad:area, :].rearrange("(p w) c -> p w c", w=WINDOW), pads[:]).then_inc(stored, 16)
                act.wait_ge(steps, when["windows"])
                with nc.allow_non_contiguous_dma(reason="a table of some hundred words"):
                    act.dma_start(lo_tab.rearrange("(b p) k -> p b k", p=P), tab_i[:, :, 2:4]).then_inc(stored, 16)
                act.wait_ge(stored, 16 * (groups + 2))
                act.dma_start(lo_i[:], lo_tab.rearrange("(o t) k -> o (t k)", o=1)).then_inc(stored, 16)
                act.wait_ge(steps, when["mn_var"])
                nc.scalar.activation(sc[:, 1:3, 1], sc[:, 1:3, 0], ACT.Sqrt).then_inc(root, 1)
                act.wait_ge(stored, 16 * (groups + 3))

        for layer in range(3):
            with ExitStack() as c2:
                node_layer(nc, maker(c2, f"l{layer}_"), *semaphores(c2, f"l{layer}_"), c2, layer, groups, chunks,
                           a, out, rows, area, z_tab, x1_tab, bank, iota_f, part_f, ident, base, ends_i, lo_i,
                           pool_sems.get(layer), flag_i, w_node, (w1, w2), rowp, dinv, w_res)


def before(s, it, steps):
    q = s - steps
    return q % 2, it + q // 2


def node_layer(nc, sb, sem, pair, ctx, layer, groups, chunks, a, out, rows, area, z_tab, x1_tab, bank, iota_f,
               part_f, ident, base, ends_i, lo_i, pool_sems, flag_i, w_node, w_conv, rowp, dinv, w_res):
    n_pad = chunks * P
    slope, node_scale, msg_scale, msg_shift = (rowp[:, i, :] for i in range(2, 6))
    width = C if layer else C + 1
    slots = 3
    has_z = layer < 2
    has_ln = layer != 1
    turn_lag = 3 if has_ln else 2
    win = sb("win", [P, 2, 2, WINDOW, R])
    hot = sb("hot", [P, 2, 2 * WINDOW, 2, P])
    numbers = sb("numbers", [P, 2, WINDOW, 2, P])
    acc = sb("acc", [P, 2, 3, HALF, C])
    if layer == 0:
        deg = sb("deg", [P, 2, HALF])
        xc = sb("xc", [C + 1, 2, COLS])
    else:
        zr = sb("zr", [P, 2, HALF, C])
        g_rows = sb("g_rows", [P, slots, 2 * HALF, C])
        idx = sb("idx", [P, slots, 2 * HALF], I32)
    if has_ln:
        xr = sb("xr", [P, 2, HALF, C])
        ln = sb("ln", [P, 2, HALF, 6])
        mv = sb("mv", [P, 2, 6, HALF])
        inv = sb("inv", [P, 2, 3, 2 * HALF])
        lift = sb("lift", [P, 2, HALF])
        o_rows = sb("o_rows", [P, 2, HALF, C])
    if has_z:
        o_cols = sb("o_cols", [C, COLS])
        z_out = sb("z_out", [P, 2, HALF, C])
    big = sb("big", [P, 2 * HALF, R])
    sums = sb("sums", [P, WINDOW, R])
    first_node = sb("first_node", [P, 1])

    win_in = pair("win_in")
    z_in, res_in, xc_in = pair("z_in"), pair("res_in"), pair("xc_in")
    hot_set, summed, own, own_x, shifts = (pair(k) for k in ("hot_set", "summed", "own", "own_x", "shifts"))
    own_relu, own_scaled, own_set = pair("own_relu"), pair("own_scaled"), pair("own_set")
    y1, y2, y3, y4, deg_set, deg_used, y_set = (pair(k) for k in ("y1", "y2", "y3", "y4", "deg_set", "deg_used", "y_set"))
    ln_set, mv_set, var_set, inv_set, roots = (pair(k) for k in ("ln_set", "mv_set", "var_set", "inv_set", "roots"))
    lifted, o_set, turned, cols_set, z_ps, z_set = (pair(k) for k in ("lifted", "o_set", "turned", "cols_set", "z_ps", "z_set"))
    o_out, z_st, dinv_set = pair("o_out"), pair("z_st"), pair("dinv_set")
    idx_set = [sem(f"idx_set{i}") for i in range(slots)]
    passed, numbered = sem("passed"), sem("numbered")
    big_in, big_hot, big_sum, big_acc, big_zero, big_key, big_out = (
        sem(k) for k in ("big_in", "big_hot", "big_sum", "big_acc", "big_zero", "big_key", "big_out"))
    if layer:
        gathered, rows_in = pool_sems[0:slots], pool_sems[slots]

    ps_a, ps_h, ps_y, ps_t, ps_z = bank[0:2], bank[2:4], bank[4:6], bank[6], bank[7]
    z_of = z_tab[layer - 1] if layer else None
    z_to = z_tab[layer] if has_z else None

    block = ctx.enter_context(nc.Block())

    def tiles_of(table, at):
        return table[bass.ds(at, COLS), :].rearrange("(j p t) c -> p j (t c)", p=P, t=2)

    def by_pair(rows_of):
        return rows_of.rearrange("p (j t) c -> p j (t c)", t=2)

    def tile(s, k):
        return k * (2 * HALF) + s * HALF

    def exists(half):
        return not peeled(half[1]) or 0 <= half[1] < groups

    def all_steps(eng, step, snapped=False):
        def both(it):
            for s in range(2):
                step(s, it)
        rounds(eng, groups, both, ahead=3)
        for h in range(turn_lag):
            step(h % 2, groups + h // 2)

    if layer:
        @block.gpsimd
        def _(pool):
            def indices(it, s):
                nc.gpsimd.tensor_copy(idx[:, s], ends_i[:, 0, bass.ds(it * (slots * 2 * HALF) + s * 2 * HALF, 2 * HALF)]).then_inc(idx_set[s], 1)

            def store(it, s):
                pool.wait_ge(gathered[s], it * (16 * 2 * HALF) + 16 * 2 * HALF)
                if later(it) or s:
                    pool.wait_ge(rows_in, it * (16 * slots) + 16 * s)
                pool.dma_start(rows[bass.ds(it * (slots * 2 * COLS) + s * 2 * COLS, 2 * COLS), 0:C].rearrange("(u p) c -> p u c", p=P),
                               g_rows[:, s]).then_inc(rows_in, 16)

            def group(it, s, last=False):
                if not last:
                    indices(it + 1 if s == slots - 1 else it, (s + 1) % slots)
                pool.wait_ge(idx_set[s], it + 1)
                if not peeled(it):
                    pool.sem_inc(passed, 1)
                for u in range(2 * HALF):
                    nc.gpsimd.indirect_dma_start(
                        g_rows[:, s, u, :], None, z_of, bass.IndirectOffsetOnAxis(idx[:, s, u:u + 1], axis=0),
                    ).then_inc(gathered[s], 16)
                if s:
                    store(it, s - 1)
                elif later(it):
                    store(it - 1, slots - 1)

            def three(it):
                for s in range(slots):
                    group(it, s)
            indices(0, 0)
            whole = (groups - 1) // slots
            rounds(pool, whole, three)
            for s in range(groups - whole * slots):
                group(whole, s, last=s == groups - whole * slots - 1)
            store(whole, groups - whole * slots - 1)
    else:
        @block.gpsimd
        def _(pool):
            def own_rows(s, k):
                A = acc[:, s]
                pool.wait_ge(own_relu[s], k + 1)
                if later(k):
                    pool.wait_ge(y_set[s], k)
                nc.gpsimd.tensor_tensor(A[:, 1], A[:, 0], rowwise(node_scale, HALF), ALU.mult).then_inc(own_scaled[s], 1)
                pool.wait_ge(deg_set[s], k + 1)
                nc.gpsimd.tensor_tensor(xr[:, s], wide(deg[:, s], C), rowwise(msg_shift, HALF), ALU.mult).then_inc(shifts[s], 1)
                pool.wait_ge(own_scaled[s], k + 1)
                pool.wait_ge(shifts[s], k + 1)
                nc.gpsimd.tensor_tensor(A[:, 1], A[:, 1], xr[:, s], ALU.add).then_inc(own_set[s], 1)

            def both(it):
                for s in range(2):
                    own_rows(s, it)
            rounds(pool, groups, both)

    @block.sync
    def _(sp):
        flag = sp.value_load(flag_i[0:1, 0:1], min_val=0, max_val=1)
        with sp.If(flag == 1):
            if layer:
                sp.wait_ge(rows_in, 16 * groups)
            with sp.Fori(0, chunks // 2) as t:
                with sp.Fori(0, groups) as k:
                    free = sp.snap(t * groups + k + 1)
                    at = sp.snap(k * (2 * COLS))
                    sp.wait_ge(big_acc, free)
                    sp.dma_start(big[:], rows[bass.ds(at, 2 * COLS), :].rearrange("(p u) c -> p u c", p=P)).then_inc(big_in, 16)
                summed_all = sp.snap(t * groups + (groups + 1))
                to = sp.snap(t * WIN + area)
                sp.wait_ge(big_acc, summed_all)
                sp.dma_start(rows[bass.ds(to, WIN), :].rearrange("(p w) c -> p w c", w=WINDOW), sums[:]).then_inc(big_out, 16)
            sp.wait_ge(big_out, 16 * (chunks // 2))

        def loads(it):
            for s in range(2):
                at = it * (2 * COLS) + s * COLS
                used = it
                if not peeled(it):
                    at, used = sp.snap(at), sp.snap(used)
                entry = [(tile(s, it) + 2 * j) * 2 for j in range(2)]
                lows = [sp.value_load(lo_i[0:1, bass.ds(e, 1)], min_val=0, max_val=area + (chunks // 2 - 1) * WIN) for e in entry]
                if layer:
                    need = sp.value_load(lo_i[0:1, bass.ds(entry[1] + 1, 1)], min_val=16, max_val=16 * groups)
                if later(it):
                    sp.wait_ge(summed[s], used)
                if layer:
                    sp.wait_ge(rows_in, need)
                for j, low in enumerate(lows):
                    sp.dma_start(win[:, s, j], rows[bass.ds(low, WIN), :].rearrange("(p w) c -> p w c", w=WINDOW)).then_inc(win_in[s], 16)
                if layer == 0:
                    if later(it):
                        sp.wait_ge(own_x[s], used)
                    sp.dma_start(xc[:, s, :], a["xT"][:, bass.ds(at, COLS)]).then_inc(xc_in[s], 16)
                else:
                    sp.dma_start(by_pair(zr[:, s]), tiles_of(z_of, at)).then_inc(z_in[s], 16)
                if layer == 2:
                    if later(it):
                        sp.wait_ge(y_set[s], used)
                    sp.dma_start(by_pair(xr[:, s]), tiles_of(x1_tab, at)).then_inc(res_in[s], 16)
        rounds(sp, groups, loads)

    @block.vector
    def _(dve):
        V = nc.vector
        for v in range(2):
            V.tensor_scalar(numbers[:, 0, 0, v], iota_f[:], 2.0, float(v), ALU.mult, ALU.add).then_inc(numbered, 1)
        dve.wait_ge(numbered, 2)
        for w in range(1, WINDOW):
            V.tensor_copy(numbers[:, 0, w], numbers[:, 0, 0]).then_inc(numbered, 1)
        for w in range(WINDOW):
            V.tensor_scalar(numbers[:, 1, w], numbers[:, 0, 0], 2.0 * P, None, ALU.add).then_inc(numbered, 1)
        dve.wait_ge(numbered, 2 * WINDOW + 1)
        flag = dve.value_load(flag_i[0:1, 0:1], min_val=0, max_val=1)
        with dve.If(flag == 1):
            every = hot[:].rearrange("p s w t m -> p (s w t m)")[:, 0:4 * HALF * P].rearrange("p (u t m) -> p u t m", t=2, m=P)
            V.memset(sums[:], 0.0).then_inc(big_zero, 1)
            V.memset(first_node[:], -2.0 * P).then_inc(big_zero, 1)
            dve.wait_ge(big_zero, 2)
            V.memset(sums[:, 2, DST:DST + 1], float(n_pad - 1)).then_inc(big_zero, 1)
            dve.wait_ge(big_zero, 3)
            V.memset(sums[:, 0, 0:1], 0.0).then_inc(big_acc, 1)
            with dve.Fori(0, chunks // 2) as t:
                dve.wait_ge(big_acc, t * groups + 1)
                V.tensor_scalar(first_node[:], first_node[:], 2.0 * P, None, ALU.add).then_inc(big_zero, 1)
                V.memset(sums[:, 0:2, 0:DST], 0.0).then_inc(big_zero, 1)
                dve.wait_ge(big_zero, t * 4 + 5)
                for v in range(2):
                    V.tensor_scalar(sums[:, v, DST:DST + 1], part_f[:], 2.0, float(v), ALU.mult, ALU.add).then_inc(big_zero, 1)
                dve.wait_ge(big_zero, t * 4 + 7)
                V.tensor_scalar(sums[:, 0:2, DST], sums[:, 0:2, DST], first_node[:, 0:1], None, ALU.add).then_inc(big_key, 1)
                with dve.Fori(0, groups) as k:
                    dve.wait_ge(big_key, t + 1)
                    dve.wait_ge(big_in, t * (16 * groups) + k * 16 + 16)
                    V.scalar_tensor_tensor(every.rearrange("p u t m -> p u (t m)"), wide(big[:, :, DST], 2 * P), first_node[:, 0:1],
                                           rowwise(numbers[:, 0, 0].rearrange("p t m -> p (t m)"), 2 * HALF),
                                           ALU.subtract, ALU.is_equal).then_inc(big_hot, 1)
                    dve.wait_ge(big_sum, t * groups + k + 1)
                    V.tensor_tensor(sums[:, 0:2, 0:DST], sums[:, 0:2, 0:DST],
                                    ps_a[0][:, 0:2 * DST].rearrange("p (t c) -> p t c", t=2), ALU.add).then_inc(big_acc, 1)
                    dve.wait_ge(big_acc, t * groups + k + 2)
                dve.wait_ge(big_out, t * 16 + 16)

        def one_hots(s, it):
            if later(it):
                dve.wait_ge(summed[s], it)
            dve.wait_ge(win_in[s], it * 32 + 32)
            V.scalar_tensor_tensor(hot[:, s].rearrange("p w t m -> p w (t m)"),
                                   wide(win[:, s, :, :, DST].rearrange("p j w -> p (j w)"), 2 * P),
                                   base[:, bass.ds(it * 2 + s, 1)], numbers[:].rearrange("p j w t m -> p (j w) (t m)"),
                                   ALU.subtract, ALU.is_equal).then_inc(hot_set[s], 1)

        def norm_statistics(s, it, y, width):
            for u in range(HALF):
                V.bn_stats(ln[:, s, u], y[:, u]).then_inc(ln_set[s], 1)
            dve.wait_ge(ln_set[s], it * HALF + HALF)
            V.tensor_tensor(mv[:, s, 0], ln[:, s, :, 1], ln[:, s, :, 4], ALU.add).then_inc(mv_set[s], 1)
            V.tensor_tensor(mv[:, s, 1], ln[:, s, :, 1], ln[:, s, :, 4], ALU.subtract).then_inc(mv_set[s], 1)
            V.tensor_tensor(mv[:, s, 3], ln[:, s, :, 2], ln[:, s, :, 5], ALU.add).then_inc(mv_set[s], 1)
            dve.wait_ge(mv_set[s], it * 5 + 3)
            V.tensor_tensor(mv[:, s, 2], mv[:, s, 1], mv[:, s, 1], ALU.mult).then_inc(mv_set[s], 1)
            V.tensor_scalar(mv[:, s, 5], mv[:, s, 0], 0.5, None, ALU.mult).then_inc(mv_set[s], 1)
            dve.wait_ge(mv_set[s], it * 5 + 5)
            V.scalar_tensor_tensor(mv[:, s, 4], mv[:, s, 2], C / 4, mv[:, s, 3], ALU.mult, ALU.add).then_inc(var_set[s], 1)
            dve.wait_ge(var_set[s], it * 2 + 1)
            V.tensor_scalar(inv[:, s, 0, 0:HALF], mv[:, s, 4], 1.0 / C, EPS, ALU.mult, ALU.add).then_inc(var_set[s], 1)
            dve.wait_ge(var_set[s], it * 2 + 2)
            V.reciprocal(inv[:, s, 1, 0:width], inv[:, s, 0, 0:width]).then_inc(inv_set[s], 1)

        def norm_shift(s, k):
            dve.wait_ge(roots[s], k + 1)
            if layer == 0:
                V.tensor_copy(dinv[:, bass.ds(tile(s, k), HALF)], inv[:, s, 2, HALF:2 * HALF]).then_inc(dinv_set[s], 1)
            V.scalar_tensor_tensor(lift[:, s], mv[:, s, 5], -1.0, inv[:, s, 2, 0:HALF], ALU.mult, ALU.mult).then_inc(lifted[s], 1)

        def nodes_0(s, k):
            A = acc[:, s]
            four = lambda bank, n: bank[s][:, 0:HALF * n].rearrange("p (t c) -> p t c", t=HALF)
            dve.wait_ge(deg_set[s], k + 1)
            V.tensor_scalar(inv[:, s, 0, HALF:2 * HALF], deg[:, s], 1.0, None, ALU.add).then_inc(deg_used[s], 1)
            if later(k):
                dve.wait_ge(o_set[s], k * HALF)
            V.tensor_tensor(A[:, 2], four(ps_a, C + 1)[:, :, 0:C], rowwise(msg_scale, HALF), ALU.mult).then_inc(y1[s], 1)
            dve.wait_ge(own_x[s], k + 1)
            dve.wait_ge(y1[s], k + 1)
            V.tensor_tensor(A[:, 2], four(ps_y, C), A[:, 2], ALU.add).then_inc(y2[s], 1)
            dve.wait_ge(own_set[s], k + 1)
            dve.wait_ge(y2[s], k + 1)
            V.tensor_tensor(A[:, 2], A[:, 2], A[:, 1], ALU.add).then_inc(y_set[s], 1)
            dve.wait_ge(y_set[s], k + 1)
            dve.wait_ge(deg_used[s], k + 1)
            norm_statistics(s, k, A[:, 2], 2 * HALF)

        def nodes_12(s, k):
            A = acc[:, s]
            dve.wait_ge(y1[s], k * HALF + HALF)
            V.tensor_tensor(A[:, 0], A[:, 0], rowwise(rowp[:, layer - 1, :], HALF), ALU.add).then_inc(y2[s], 1)
            if layer == 2 and later(k):
                dve.wait_ge(o_set[s], k * HALF)
            dve.wait_ge(y2[s], k + 1)
            V.scalar_tensor_tensor(A[:, 1], A[:, 0], 0.0, rowwise(slope, HALF), ALU.min, ALU.mult).then_inc(y3[s], 1)
            if layer == 1 and later(k):
                dve.wait_ge(turned[s], k)
            dve.wait_ge(y3[s], k + 1)
            V.scalar_tensor_tensor(A[:, 2], A[:, 0], 0.0, A[:, 1], ALU.max, ALU.add).then_inc(y4[s], 1)
            if layer == 2:
                dve.wait_ge(res_in[s], k * 16 + 16)
                dve.wait_ge(y4[s], k + 1)
                V.tensor_tensor(A[:, 1], A[:, 2], xr[:, s], ALU.add).then_inc(y_set[s], 1)
                dve.wait_ge(y_set[s], k + 1)
                norm_statistics(s, k, A[:, 1], HALF)

        def step(s, it):
            here, one, two = ((s, it) if j == 0 else before(s, it, j) for j in range(3))
            if exists(here):
                one_hots(*here)
            if has_ln and exists(two):
                norm_shift(*two)
            if exists(one):
                (nodes_12 if layer else nodes_0)(*one)
        all_steps(dve, step)

    @block.tensor
    def _(pe):
        T = nc.tensor
        flag = pe.value_load(flag_i[0:1, 0:1], min_val=0, max_val=1)
        with pe.If(flag == 1):
            with pe.Fori(0, chunks // 2) as t:
                with pe.Fori(0, groups) as k:
                    pe.wait_ge(big_hot, t * groups + k + 1)
                    every = hot[:].rearrange("p s w t m -> p (s w t m)")[:, 0:4 * HALF * P].rearrange("p (u t m) -> p u t m", t=2, m=P)
                    for v in range(2):
                        for u in range(2 * HALF):
                            last = T.matmul(ps_a[0][:, v * DST:(v + 1) * DST], every[:, u, v], big[:, u, 0:DST],
                                            start=(u == 0), stop=(u == 2 * HALF - 1))
                    last.then_inc(big_sum, 1)

        def turn(s, k):
            of = acc[:, s, 2] if layer else o_rows[:, s]
            pe.wait_ge(y4[s] if layer else o_set[s], k + 1 if layer else k * HALF + HALF)
            if s:
                pe.wait_ge(cols_set[0], k + 1)
            elif later(k):
                pe.wait_ge(cols_set[1], k)
            for u in range(HALF):
                last = T.transpose(ps_t[0:C, u * P:(u + 1) * P], of[:, u, :], ident[:])
            last.then_inc(turned[s], 1)

        def product(s, k):
            pe.wait_ge(cols_set[s], k + 1)
            if s:
                pe.wait_ge(z_set[0], k * HALF + HALF)
            elif later(k):
                pe.wait_ge(z_set[1], k * HALF)
            for u in range(HALF):
                last = T.matmul(ps_z[:, u * C:(u + 1) * C], o_cols[:, u * P:(u + 1) * P], w_conv[layer][:], start=True, stop=True)
            last.then_inc(z_ps[s], 1)

        def sum_edges(s, k):
            pe.wait_ge(hot_set[s], k + 1)
            if later(k):
                pe.wait_ge(y1[s], k * HALF if layer else k)
                if layer == 0:
                    pe.wait_ge(deg_set[s], k)
            if layer:
                pe.wait_ge(z_in[s], k * 16 + 16)
            for u in range(HALF):
                to = ps_a[s][:, u * width:(u + 1) * width]
                for w in range(WINDOW):
                    last = T.matmul(to, hot[:, s, u // 2 * WINDOW + w, u % 2, :], win[:, s, u // 2, w, 0:width],
                                    start=(w == 0), stop=(layer == 0 and w == WINDOW - 1))
                if layer:
                    last = T.matmul(to, ident[:], zr[:, s, u, :], start=False, stop=True)
            last.then_inc(summed[s], 1)

        def own_features(s, k):
            pe.wait_ge(xc_in[s], k * 16 + 16)
            if later(k):
                pe.wait_ge(own_relu[s], k)
            for u in range(HALF):
                T.matmul(ps_h[s][:, u * C:(u + 1) * C], xc[:, s, u // 2 * 2 * P + u % 2:(u // 2 + 1) * 2 * P:2], w_node[:], start=True, stop=True).then_inc(own[s], 1)
            if later(k):
                pe.wait_ge(y2[s], k)
            for u in range(HALF):
                last = T.matmul(ps_y[s][:, u * C:(u + 1) * C], xc[:, s, u // 2 * 2 * P + u % 2:(u // 2 + 1) * 2 * P:2], w_res[:], start=True, stop=True)
            last.then_inc(own_x[s], 1)

        def step(s, it):
            here, old = (s, it), before(s, it, turn_lag)
            if exists(here):
                if layer == 0:
                    own_features(*here)
                sum_edges(*here)
            if has_z and exists(old):
                turn(*old)
            if has_z and exists(old):
                product(*old)
        all_steps(pe, step)

    @block.scalar
    def _(act):
        def own_features(s, k):
            act.wait_ge(own[s], k * HALF + HALF)
            if later(k):
                act.wait_ge(own_scaled[s], k)
            nc.scalar.activation(acc[:, s, 0], ps_h[s][:, 0:HALF * C].rearrange("p (t c) -> p t c", t=HALF), ACT.Relu).then_inc(own_relu[s], 1)

        def sums_out(s, k):
            act.wait_ge(summed[s], k + 1)
            if layer == 0:
                if later(k):
                    act.wait_ge(shifts[s], k)
                    act.wait_ge(deg_used[s], k)
                nc.scalar.copy(deg[:, s], ps_a[s][:, 0:HALF * (C + 1)].rearrange("p (t c) -> p t c", t=HALF)[:, :, C]).then_inc(deg_set[s], 1)
                return
            if later(k):
                act.wait_ge(y4[s], k)
            for u in range(HALF):
                nc.scalar.activation(acc[:, s, 0, u], ps_a[s][:, u * C:(u + 1) * C], ACT.Copy,
                                     scale=dinv[:, bass.ds(tile(s, k) + u, 1)]).then_inc(y1[s], 1)

        def square_roots(s, k):
            act.wait_ge(inv_set[s], k + 1)
            if layer == 0 and later(k):
                act.wait_ge(dinv_set[s], k)
            if later(k):
                act.wait_ge(lifted[s], k)
            width = HALF if layer else 2 * HALF
            nc.scalar.activation(inv[:, s, 2, 0:width], inv[:, s, 1, 0:width], ACT.Sqrt).then_inc(roots[s], 1)

        def norm(s, k):
            act.wait_ge(lifted[s], k + 1)
            if later(k):
                act.wait_ge(o_out[s], k * 16)
                if layer == 0:
                    act.wait_ge(turned[s], k)
            for u in range(HALF):
                nc.scalar.activation(o_rows[:, s, u], acc[:, s, 1 if layer else 2, u], ACT.Identity,
                                     bias=lift[:, s, u:u + 1], scale=inv[:, s, 2, u:u + 1]).then_inc(o_set[s], 1)
            act.wait_ge(o_set[s], k * HALF + HALF)
            act.dma_start(tiles_of(out if layer else x1_tab, k * (2 * COLS) + s * COLS), by_pair(o_rows[:, s])).then_inc(o_out[s], 16)

        def columns(s, k):
            act.wait_ge(turned[s], k + 1)
            if s:
                act.wait_ge(z_ps[0], k + 1)
            elif later(k):
                act.wait_ge(z_ps[1], k)
            nc.scalar.copy(o_cols[:], ps_t[0:C, :]).then_inc(cols_set[s], 1)

        def next_rows(s, k):
            act.wait_ge(z_ps[s], k + 1)
            if layer == 0:
                act.wait_ge(dinv_set[s], k + 1)
            if later(k):
                act.wait_ge(z_st[s], k * 16)
            for u in range(HALF):
                nc.scalar.activation(z_out[:, s, u], ps_z[:, u * C:(u + 1) * C], ACT.Copy,
                                     scale=dinv[:, bass.ds(tile(s, k) + u, 1)]).then_inc(z_set[s], 1)
            act.wait_ge(z_set[s], k * HALF + HALF)
            act.dma_start(tiles_of(z_to, k * (2 * COLS) + s * COLS), by_pair(z_out[:, s])).then_inc(z_st[s], 16)

        def step(s, it):
            here, one, two, old = (s, it), before(s, it, 1), before(s, it, 2), before(s, it, turn_lag)
            if exists(here):
                if layer == 0:
                    own_features(*here)
                sums_out(*here)
            if has_z and exists(old):
                columns(*old)
            if has_ln and exists(one):
                square_roots(*one)
            if has_ln and exists(two):
                norm(*two)
            if has_z and exists(old):
                next_rows(*old)
        all_steps(act, step)
        for s in range(2):
            if has_ln:
                act.wait_ge(o_out[s], 16 * groups)
            if has_z:
                act.wait_ge(z_st[s], 16 * groups)


_SHAPE_ROWS = 2 * COLS


def lay_out(inputs):
    import numpy as np

    g = {k: np.asarray(v) for k, v in inputs.items()}
    n = g["x"].shape[0]
    n_pad = -(-n // _SHAPE_ROWS) * _SHAPE_ROWS
    more = n_pad - n

    def by_chunk(v):
        return np.ascontiguousarray(v.reshape(-1, P).T)

    src = np.concatenate([g["src"], np.zeros(more, np.int32)])
    dst = np.concatenate([g["dst"], np.full(more, n_pad - 1, np.int32)])
    nxt = np.concatenate([dst[1:], np.full(1, n_pad - 1, np.int32)])
    x = np.concatenate([g["x"], np.zeros((more, C), np.float32)])
    ea = np.concatenate([g["edge_attr_4"], np.zeros((more, 4), np.float32)])
    one = np.ones((1, n_pad), np.float32)
    row = lambda k: g[k].reshape(1, C)
    a = {
        "x": x, "xT": np.concatenate([x.T, one]), "eaT": np.concatenate([ea.T, one]),
        "src": by_chunk(src), "dst": by_chunk(dst), "dst_next": by_chunk(nxt),
        "W_edge": g["L0_gnn_W_edge"], "b_edge": row("L0_gnn_b_edge"),
        "W_node": g["L0_gnn_W_node"], "b_node": row("L0_gnn_b_node"),
        "W_msg": g["L0_gnn_W_msg"], "b_msg": row("L0_gnn_b_msg"),
        "gb": np.stack([g[f"L0_gnn_{k}_{w}"] for w in ("edge", "msg", "node") for k in ("g", "beta")], 1),
        "W1": g["L1_gnn_W1"], "W2": g["L1_gnn_W2"],
        "b1": row("L1_gnn_b1"), "b2": row("L1_gnn_b2"), "prelu": row("L1_gnn_prelu_a"),
    }
    return n, n_pad, {k: np.ascontiguousarray(v) for k, v in a.items()}


def kernel(**inputs):
    import concourse.bacc as _bacc
    from concourse.bass_utils import run_bass_kernel_spmd as _run

    n, n_pad, arrays = lay_out(inputs)
    nc = _bacc.Bacc("TRN2", target_bir_lowering=False, num_devices=1)
    args = {k: nc.dram_tensor(f"in_{k}", v.shape, mybir.dt.from_np(v.dtype), kind="ExternalInput").ap()
            for k, v in arrays.items()}
    out = nc.dram_tensor("out_0", (n_pad, C), F32, kind="ExternalOutput").ap()
    build_program(nc, n, args, out)
    r = _run(nc, [{f"in_{k}": v for k, v in arrays.items()}], core_ids=[0])
    return r.results[0]["out_0"][:n]
```

```python
from contextlib import ExitStack

import concourse.bass as bass
from concourse import mybir

P = 128
C = 96
R = C + 2
CNT, DST = C, C + 1
HALF = 4
COLS = HALF * P
WINDOW = 3
WIN = WINDOW * P
SLOTS = 4
EPS = 1e-5

F32 = mybir.dt.float32
BF16 = mybir.dt.bfloat16
I32 = mybir.dt.int32
ALU = mybir.AluOpType
ACT = mybir.ActivationFunctionType


def rounds(eng, n, body, ahead=1):
    for it in range(min(ahead, n)):
        body(it)
    if n > ahead:
        with eng.Fori(ahead, n) as it:
            body(it)


def peeled(it):
    return isinstance(it, int)


def later(it):
    return not (peeled(it) and it == 0)


def wide(ap, n):
    return ap.unsqueeze(2).to_broadcast([ap.shape[0], ap.shape[1], n])


def rowwise(ap, k):
    return ap.unsqueeze(1).to_broadcast([ap.shape[0], k, ap.shape[1]])


def build_program(nc, n, a, out):
    n_pad = out.shape[0]
    groups = n_pad // (2 * COLS)
    chunks = n_pad // P
    full = n // P
    rest = n - full * P
    last_cols = n - (2 * groups - 1) * COLS
    his = -(-chunks // P)
    area = n_pad + WIN
    assert 0 < last_cols <= COLS and rest > 0 and full <= 512

    rows = nc.dram_tensor("rows", [area + chunks // 2 * WIN, R], F32, kind="Internal").ap()
    z_tab = [nc.dram_tensor(f"z{i}", [n_pad, C], F32, kind="Internal").ap() for i in (1, 2)]
    x1_tab = nc.dram_tensor("x1", [n_pad, C], F32, kind="Internal").ap()
    lo_tab = nc.dram_tensor("lo", [his * P, 2], I32, kind="Internal").ap()

    with ExitStack() as ctx:
        def maker(c, prefix=""):
            return lambda name, shape, dt=F32: c.enter_context(nc.sbuf_tensor(prefix + name, shape, dt))

        def semaphores(c, prefix=""):
            held = []

            def sem(name):
                held.append(c.enter_context(nc.semaphore(prefix + name)))
                return held[-1]

            c.callback(clear, held)
            return sem, lambda name, n=2: [sem(f"{name}_{i}") for i in range(n)]

        def clear(held):
            with nc.Block() as between:
                @between.gpsimd
                def _(pool):
                    for one in held:
                        pool.sem_clear(one)

        gathered_msg = [ctx.enter_context(nc.semaphore(f"gathered_msg{i}")) for i in range(2)]
        pool_sems = {k: [ctx.enter_context(nc.semaphore(f"l{k}_{m}")) for m in ("gathered0", "gathered1", "gathered2", "rows_in")]
                     for k in (1, 2)}

        sb = maker(ctx)
        bank = [ctx.enter_context(nc.psum_tensor(f"bank{i}", [P, 512], F32)) for i in range(8)]

        iota_f = sb("iota_f", [P, P])
        part_f = sb("part_f", [P, 1])
        ident = sb("ident", [P, P])
        base = sb("base", [P, 2 * groups])
        ends_i = sb("ends_i", [P, 2, chunks], I32)
        lo_i = sb("lo_i", [1, his * P * 2], I32)
        flag_i = sb("flag_i", [1, 1], I32)
        w_node = sb("w_node", [C + 1, 2, C])
        w1 = sb("w1", [C, C])
        w2 = sb("w2", [C, C])
        rowp = sb("rowp", [P, 6, C])
        dinv = sb("dinv", [P, chunks])

        with ExitStack() as c1:
            sb1 = maker(c1)
            sem, pair = semaphores(c1, "m_")
            msg = sb1("msg", [P, chunks, R])
            tiles_f = sb1("tiles_f", [P, 2, chunks])
            part_i = sb1("part_i", [P, 1], I32)
            iota_i = sb1("iota_i", [P, P], I32)
            pairs_i = sb1("pairs_i", [P, P + 1], I32)
            same_pair = sb1("same_pair", [P, P + 1])
            base_i = sb1("base_i", [P, 2 * groups], I32)
            idx = sb1("idx", [P, 2, 2, HALF], I32)
            g_rows = sb1("g_rows", [P, 2, 2, HALF, C])
            free = g_rows[:].rearrange("p s w u c -> p (s w u c)")
            ints = free[:, 0:2 * chunks].bitcast(I32).rearrange("p (k n) -> p k n", k=2)
            mst = free[:, 0:6 * C].rearrange("p (c k) -> p c k", k=6)
            mmv = free[:, 6 * C:8 * C].rearrange("p (k c) -> p k c", k=2)
            diag = free[0:C, 10 * C:14 * C].rearrange("p (k c) -> p k c", k=4)
            m_dev, m_tail = free[:, 8 * C:9 * C], free[:, 9 * C:10 * C]
            g_cols = sb1("g_cols", [C, 2, COLS])
            feat = sb1("feat", [C + 1, COLS])
            ea = sb1("ea", [P, 2, COLS])
            xc = sb1("xc", [C + 1, 2, COLS])
            h = sb1("h", [C, 2, COLS])
            st = sb1("st", [C, 2 * groups, 6])
            hot_a = sb1("hot_a", [P, 2, HALF, P], BF16)
            hot_b = sb1("hot_b", [P, 2, HALF, his], BF16)
            ones = sb1("ones", [P, P])
            m_full = sb1("m_full", [P, P])
            m_one = sb1("m_one", [P, P])
            zeros = sb1("zeros", [P, P], BF16)
            before = sb1("before", [P, P])
            pads = sb1("pads", [P, WINDOW, R])
            w_edge = sb1("w_edge", [P, C])
            w_src = sb1("w_src", [C, C])
            w_dst = sb1("w_dst", [C, C])
            w_ef = sb1("w_ef", [C + 1, C])
            b_msg = sb1("b_msg", [1, C])
            gb = sb1("gb", [C, 6])
            mv = sb1("mv", [C, 3, 2])
            sc = sb1("sc", [C, 3, 4])
            tab = sb1("tab", [P, 10, his])
            bad = sb1("bad", [P, 2])
            tab_i = sb1("tab_i", [P, his, 4], I32)
            w_raw = sb1("w_raw", [C, C])

            loaded = sem("loaded"); iotas = sem("iotas"); consts = sem("consts")
            ea_in = pair("ea_in"); ea_used = pair("ea_used"); e_relu = pair("e_relu"); e_stat = pair("e_stat")
            idx_set = pair("idx_set"); gathered = gathered_msg; turned = pair("turned")
            src_cols = pair("src_cols"); dst_cols = pair("dst_cols")
            mea_in = pair("mea_in"); e_layer = pair("e_layer"); feat_set = pair("feat_set")
            xc_in = pair("xc_in"); n_layer = pair("n_layer"); n_relu = pair("n_relu"); n_stat = pair("n_stat")
            pre = pair("pre"); msg_set = pair("msg_set"); stored = sem("stored")
            hot_set = pair("hot_set"); counted = pair("counted")
            steps = sem("steps"); root = sem("root"); m_stat = sem("m_stat"); copied = pair("copied")
            p_shift = sem("p_shift"); p_tab = sem("p_tab"); p_before = sem("p_before"); p_pairs = sem("p_pairs"); p_mean = sem("p_mean")
            p_var = sem("p_var"); passed = sem("passed"); p_rows = sem("p_rows")

            ps_t, ps_f, ps_p, ps_tab, ps_s = bank[0:2], bank[2:4], bank[4:6], bank[6], bank[7]
            loads = [(ends_i[:, 1, :], a["dst"]), (ints[:, 1, 0:chunks], a["dst_next"]), (ends_i[:, 0, :], a["src"]),
                     (w_edge[0:4, :], a["W_edge"]), (w_edge[4:5, :], a["b_edge"]),
                     (w_node[0:C, 0, :], a["W_node"]), (w_node[C:C + 1, 0, :], a["b_node"]),
                     (w_src[:], a["W_msg"][0:C, :]), (w_dst[:], a["W_msg"][C:2 * C, :]),
                     (w_ef[0:C, :], a["W_msg"][2 * C:3 * C, :]), (b_msg[:], a["b_msg"]),
                     (w1[:], a["W1"]), (w2[:], a["W2"]), (gb[:], a["gb"])]
            loads += [(rowp[:, i, :], a[k].to_broadcast([P, C])) for i, k in enumerate(("b1", "b2", "prelu"))]
            all_loaded = 16 * len(loads)

            block = c1.enter_context(nc.Block())
            when = {}

            @block.vector
            def _(dve):
                V = nc.vector
                done = [0]

                def step(ins, name=None):
                    done[0] += 1
                    ins.then_inc(steps, 1)
                    dve.wait_ge(steps, done[0])
                    if name:
                        when[name] = done[0]

                dve.wait_ge(iotas, 4)
                step(V.memset(ea[:], 0.0), "zeros")
                step(V.tensor_copy(part_f[:], part_i[:]))
                step(V.tensor_copy(base[:], base_i[:]))
                step(V.memset(ones[:], 1.0))
                step(V.memset(m_full[:], full / n))
                step(V.memset(m_one[:], 1.0 / n))
                step(V.memset(feat[C:C + 1, :], 1.0))
                step(V.memset(msg[:, :, CNT:CNT + 1], 1.0))
                step(V.memset(pads[:], 0.0))
                step(V.memset(pads[:, :, DST:DST + 1], float(n_pad - 1)), "pads")
                step(V.memset(zeros[:], 0.0))
                step(V.tensor_copy(iota_f[:], iota_i[:]))
                step(V.tensor_scalar(ident[:], iota_f[:], part_f[:, 0:1], None, ALU.is_equal))
                step(V.tensor_copy(w_node[0:C, 1, :], ident[0:C, 0:C]))
                step(V.tensor_scalar(before[:], iota_f[:], part_f[:, 0:1], None, ALU.is_gt))
                step(V.tensor_scalar(pairs_i[:, 0:P], iota_i[:], 1, None, ALU.arith_shift_right))
                step(V.tensor_scalar(pairs_i[:, P:], part_i[:], 1, None, ALU.arith_shift_right))
                step(V.tensor_copy(same_pair[:], pairs_i[:]))
                step(V.tensor_scalar(same_pair[:, 0:P], same_pair[:, 0:P], same_pair[:, P:P + 1], None, ALU.is_equal))
                dve.wait_ge(loaded, all_loaded)
                step(V.tensor_copy(msg[:, :, DST], ends_i[:, 1, :]))
                step(V.tensor_tensor(tiles_f[:, 0, :], ints[:, 1, 0:chunks], msg[:, :, DST], ALU.is_lt))
                step(V.tensor_reduce(bad[:, 1:2], tiles_f[:, 0, :], mybir.AxisListType.X, ALU.add))
                step(V.tensor_scalar(ints[:, 0, 0:chunks], ends_i[:, 1, :], 7, 127, ALU.arith_shift_right, ALU.bitwise_and))
                step(V.tensor_scalar(ints[:, 1, 0:chunks], ends_i[:, 1, :], 14, None, ALU.arith_shift_right))
                step(V.tensor_copy(tiles_f[:], ints[:, :, 0:chunks]))
                step(V.tensor_copy(w_raw[:], w_ef[0:C, :]), "consts")

                def edge_stats(it):
                    for s in range(2):
                        dve.wait_ge(e_relu[s], it + 1)
                        V.bn_stats(st[:, bass.ds(it * 2 + s, 1), :].rearrange("p a k -> p (a k)"),
                                   h[:, s, :]).then_inc(e_stat[s], 1)
                rounds(dve, groups, edge_stats)

                def scale_shift(k):
                    step(V.tensor_tensor(sc[:, k, 2:3], sc[:, k, 1:2], gb[:, 2 * k:2 * k + 1], ALU.mult))
                    step(V.tensor_tensor(sc[:, k, 0:1], mv[:, k, 0:1], sc[:, k, 2:3], ALU.mult))
                    step(V.tensor_tensor(sc[:, k, 3:4], gb[:, 2 * k + 1:2 * k + 2], sc[:, k, 0:1], ALU.subtract), f"shift{k}")

                for s in range(2):
                    dve.wait_ge(e_stat[s], groups)
                step(V.bn_stats(st[:, 2 * groups - 1, :], h[:, 1, 0:last_cols]), "e_stats")
                step(V.bn_aggr(mv[:, 0, :], st[:].rearrange("p a k -> p (a k)")))
                step(V.tensor_scalar(sc[:, 0, 0:1], mv[:, 0, 1:2], EPS, None, ALU.add))
                step(V.reciprocal(sc[:, 0, 0:1], sc[:, 0, 0:1]), "e_var")
                dve.wait_ge(root, 1)
                scale_shift(0)
                step(V.tensor_scalar(w_ef[0:C, :], w_raw[:], sc[:, 0, 2:3], None, ALU.mult))
                dve.wait_ge(p_shift, 1)
                step(V.tensor_tensor(w_ef[C:C + 1, :], ps_s[0:1, 0:C], b_msg[:], ALU.add), "w_ef")

                def messages(it):
                    first = peeled(it)
                    for s in range(2):
                        at = it * (2 * HALF) + s * HALF
                        if not first:
                            dve.wait_ge(counted[s], it)
                        V.tensor_tensor(hot_a[:, s], wide(tiles_f[:, 0, bass.ds(at, HALF)], P),
                                        rowwise(iota_f[:], HALF), ALU.is_equal).then_inc(hot_set[s], 1)
                        V.tensor_tensor(hot_b[:, s], wide(tiles_f[:, 1, bass.ds(at, HALF)], his),
                                        rowwise(iota_f[:, 0:his], HALF), ALU.is_equal).then_inc(hot_set[s], 1)
                        dve.wait_ge(turned[s], it * 2 + 2)
                        if not first or s:
                            dve.wait_ge(pre[1 - s], it + s)
                        V.tensor_copy(g_cols[:, 1, :], ps_t[1][0:C, :]).then_inc(dst_cols[s], 1)
                        dve.wait_ge(n_relu[s], it + 1)
                        V.bn_stats(st[:, bass.ds(it * 2 + s, 1), :].rearrange("p a k -> p (a k)"),
                                   h[:, s, :]).then_inc(n_stat[s], 1)
                rounds(dve, groups, messages)
                for s in range(2):
                    dve.wait_ge(n_stat[s], groups)
                step(V.bn_stats(st[:, 2 * groups - 1, :], h[:, 1, 0:last_cols]))
                step(V.bn_aggr(mv[:, 2, :], st[:].rearrange("p a k -> p (a k)")))

                dve.wait_ge(p_tab, 1)
                step(V.tensor_copy(tab[:, 0, :], ps_tab[:, 0:his]), "counts")
                dve.wait_ge(p_pairs, 1)
                step(V.tensor_scalar(tab[:, 1, :], ps_s[:, 0:his], float(WIN), None, ALU.is_gt))
                step(V.tensor_reduce(bad[:, 0:1], tab[:, 1, :], mybir.AxisListType.X, ALU.add))
                step(V.tensor_tensor(bad[:, 0:1], bad[:, 0:1], bad[:, 1:2], ALU.add), "bad")
                dve.wait_ge(p_before, 1)
                step(V.memset(tab[:, 2, :], 0.0))
                for b in range(1, his):
                    step(V.tensor_tensor(tab[:, 2, b:b + 1], tab[:, 2, b - 1:b], ps_s[:, 8 + b - 1:8 + b], ALU.add))
                step(V.tensor_tensor(tab[:, 3, :], tab[:, 2, :], ps_s[:, 0:his], ALU.add))
                step(V.tensor_scalar(bad[:, 0:1], ps_s[:, 16:17], 1.0, None, ALU.min))
                step(V.tensor_copy(flag_i[:], bad[0:1, 0:1]))
                for b in range(his):
                    step(V.tensor_scalar(tab[:, 4, b:b + 1], part_f[:], float(WIN // 2), float(area + b * P * WIN // 2), ALU.mult, ALU.add))
                step(V.tensor_tensor(tab[:, 5, :], tab[:, 4, :], tab[:, 3, :], ALU.subtract))
                step(V.scalar_tensor_tensor(tab[:, 6, :], tab[:, 5, :], bad[:, 0:1], tab[:, 3, :], ALU.mult, ALU.add))
                step(V.tensor_copy(tab_i[:, :, 2], tab[:, 6, :]))
                step(V.tensor_scalar(tab[:, 7, :], tab[:, 3, :], float(WIN - 1), None, ALU.add))
                step(V.tensor_copy(tab_i[:, :, 0], tab[:, 7, :]))
                step(V.tensor_scalar(tab_i[:, :, 1], tab_i[:, :, 0], 10, None, ALU.arith_shift_right))
                step(V.tensor_copy(tab[:, 8, :], tab_i[:, :, 1]))
                step(V.tensor_scalar(tab[:, 8, :], tab[:, 8, :], float(groups - 1), 16.0, ALU.min, ALU.mult))
                step(V.tensor_scalar(tab[:, 8, :], tab[:, 8, :], 16.0, None, ALU.add))
                step(V.tensor_copy(tab_i[:, :, 3], tab[:, 8, :]), "windows")

                for s in range(2):
                    dve.wait_ge(msg_set[s], groups)
                with dve.Fori(0, C) as c:
                    V.bn_stats(mst[:, bass.ds(c, 1), :].rearrange("p a k -> p (a k)"),
                               msg[:, 0:full, bass.ds(c, 1)].rearrange("p e a -> p (e a)")).then_inc(m_stat, 1)
                dve.wait_ge(m_stat, C)
                even, odd = (full + 1) // 2, full // 2
                step(V.tensor_scalar(mmv[:, 0, :], mst[:, :, 4], odd / full, None, ALU.mult))
                step(V.scalar_tensor_tensor(mmv[:, 0, :], mst[:, :, 1], even / full, mmv[:, 0, :], ALU.mult, ALU.add), "m_means")
                step(V.tensor_tensor(m_dev[:], mst[:, :, 1], mst[:, :, 4], ALU.subtract))
                step(V.tensor_tensor(m_dev[:], m_dev[:], m_dev[:], ALU.mult))
                step(V.tensor_tensor(mmv[:, 1, :], mst[:, :, 2], mst[:, :, 5], ALU.add))
                step(V.scalar_tensor_tensor(mmv[:, 1, :], m_dev[:], even * odd / full, mmv[:, 1, :], ALU.mult, ALU.add))
                step(V.tensor_scalar(mmv[:, 1, :], mmv[:, 1, :], 1.0 / full, None, ALU.mult))
                step(V.tensor_copy(m_dev[:], mmv[:, 0, :]))
                dve.wait_ge(p_mean, 1)
                step(V.tensor_tensor(m_dev[:], m_dev[:], ps_p[0][:, 0:C], ALU.subtract))
                step(V.tensor_tensor(m_dev[:], m_dev[:], m_dev[:], ALU.mult))
                step(V.tensor_tensor(m_dev[:], m_dev[:], mmv[:, 1, :], ALU.add))
                step(V.tensor_tensor(m_tail[0:rest, :], msg[0:rest, full, 0:C], ps_p[0][0:rest, 0:C], ALU.subtract))
                step(V.tensor_tensor(m_tail[0:rest, :], m_tail[0:rest, :], m_tail[0:rest, :], ALU.mult), "m_devs")
                dve.wait_ge(p_var, 1)
                step(V.tensor_copy(mv[:, 1, 0:1], ps_p[1][0:C, 0:1]))
                step(V.tensor_copy(mv[:, 1, 1:2], ps_p[1][0:C, 2:3]))
                step(V.tensor_scalar(sc[:, 1:3, 0], mv[:, 1:3, 1], EPS, None, ALU.add))
                step(V.reciprocal(sc[:, 1:3, 0], sc[:, 1:3, 0]), "mn_var")
                dve.wait_ge(root, 2)
                scale_shift(1)
                scale_shift(2)
                for i, (k, w) in enumerate(((2, 2), (1, 2), (1, 3), (2, 3))):
                    step(V.tensor_scalar(diag[:, i, :], ident[0:C, 0:C], sc[:, k, w:w + 1], None, ALU.mult), "diags")
                dve.wait_ge(p_rows, 1)
                step(V.tensor_copy(rowp[:, 3:6, :], ps_s[:, 0:3 * C].rearrange("p (k c) -> p k c", k=3)))
                step(V.tensor_copy(w_node[C:C + 1, 1, :], ps_s[C:C + 1, 3 * C:4 * C]))

            @block.sync
            def _(sp):
                sp.wait_ge(iotas, 4)
                for to, of in loads:
                    sp.dma_start(to, of).then_inc(loaded, 16)

                sp.wait_ge(steps, when["zeros"])

                def edge_stats(it):
                    at = [it * (2 * COLS) + s * COLS if peeled(it) else sp.snap(it * (2 * COLS) + s * COLS) for s in range(2)]
                    for s in range(2):
                        if not peeled(it):
                            sp.wait_ge(ea_used[s], it)
                        sp.dma_start(ea[0:5, s, :], a["eaT"][:, bass.ds(at[s], COLS)]).then_inc(ea_in[s], 16)
                rounds(sp, groups, edge_stats)

                def messages(it):
                    at = [it * (2 * COLS) + s * COLS if peeled(it) else sp.snap(it * (2 * COLS) + s * COLS) for s in range(2)]
                    for s in range(2):
                        if peeled(it):
                            sp.wait_ge(ea_used[s], groups)
                        else:
                            sp.wait_ge(e_layer[s], it)
                        sp.dma_start(ea[0:5, s, :], a["eaT"][:, bass.ds(at[s], COLS)]).then_inc(mea_in[s], 16)
                        if not peeled(it):
                            sp.wait_ge(n_layer[s], it)
                        sp.dma_start(xc[:, s, :], a["xT"][:, bass.ds(at[s], COLS)]).then_inc(xc_in[s], 16)
                rounds(sp, groups, messages)
            @block.gpsimd
            def _(pool):
                nc.gpsimd.memset(w_edge[:], 0.0).then_inc(iotas, 1)
                nc.gpsimd.iota(iota_i[:], [[1, P]], base=0, channel_multiplier=0).then_inc(iotas, 1)
                nc.gpsimd.iota(part_i[:], [[0, 1]], base=0, channel_multiplier=1).then_inc(iotas, 1)
                nc.gpsimd.iota(base_i[:], [[COLS, 2 * groups]], base=0, channel_multiplier=0).then_inc(iotas, 1)
                pool.wait_ge(steps, when["consts"])

                def indices(it, s):
                    nc.gpsimd.tensor_copy(idx[:, s], ends_i[:, :, bass.ds(it * (2 * HALF) + s * HALF, HALF)]).then_inc(copied[s], 1)

                def gathers(it, last=False):
                    for s in range(2):
                        if later(it):
                            pool.wait_ge(turned[s], it * 2)
                        pool.wait_ge(copied[s], it + 1)
                        if not peeled(it):
                            pool.sem_inc(passed, 1)
                        for w in range(2):
                            for u in range(HALF):
                                nc.gpsimd.indirect_dma_start(
                                    g_rows[:, s, w, u, :], None, a["x"],
                                    bass.IndirectOffsetOnAxis(idx[:, s, w, u:u + 1], axis=0),
                                ).then_inc(gathered[s], 16)
                            if w == 0 and not (last and s):
                                if s or later(it):
                                    pool.wait_ge(gathered[1 - s], (it + s) * (16 * 2 * HALF))
                                    if not peeled(it):
                                        pool.sem_inc(passed, 1)
                                indices(it + s, 1 - s)
                indices(0, 0)
                rounds(pool, groups - 1, gathers)
                gathers(groups - 1, last=True)

            @block.tensor
            def _(pe):
                T = nc.tensor
                pe.wait_ge(steps, when["consts"])

                def edge_stats(it):
                    for s in range(2):
                        pe.wait_ge(ea_in[s], it * 16 + 16)
                        if not peeled(it):
                            pe.wait_ge(e_relu[s], it)
                        T.matmul(ps_f[s][0:C, :], w_edge[:], ea[:, s, :], start=True, stop=True).then_inc(ea_used[s], 1)
                rounds(pe, groups, edge_stats)

                pe.wait_ge(steps, when["shift0"])
                T.matmul(ps_s[0:1, 0:C], sc[:, 0, 3:4], w_raw[:], start=True, stop=True).then_inc(p_shift, 1)

                def messages(it):
                    first = peeled(it)
                    for s in range(2):
                        pe.wait_ge(gathered[s], it * (16 * 2 * HALF) + 16 * 2 * HALF)
                        if not first or s:
                            pe.wait_ge(src_cols[1 - s], it + s)
                        for u in range(HALF):
                            last = T.transpose(ps_t[0][0:C, u * P:(u + 1) * P], g_rows[:, s, 0, u, :], ident[:])
                        last.then_inc(turned[s], 1)
                        if not first or s:
                            pe.wait_ge(dst_cols[1 - s], it + s)
                        for u in range(HALF):
                            last = T.transpose(ps_t[1][0:C, u * P:(u + 1) * P], g_rows[:, s, 1, u, :], ident[:])
                        last.then_inc(turned[s], 1)
                        pe.wait_ge(mea_in[s], it * 16 + 16)
                        if first and s == 0:
                            pe.wait_ge(e_relu[0], groups)
                        else:
                            pe.wait_ge(feat_set[1 - s], it + s)
                        T.matmul(ps_f[0][0:C, :], w_edge[:], ea[:, s, :], start=True, stop=True).then_inc(e_layer[s], 1)
                        pe.wait_ge(xc_in[s], it * 16 + 16)
                        if first and s == 0:
                            pe.wait_ge(e_relu[1], groups)
                        else:
                            pe.wait_ge(n_relu[1 - s], it + s)
                        T.matmul(ps_f[1][0:C, :], w_node[:, 0, :], xc[:, s, :], start=True, stop=True).then_inc(n_layer[s], 1)
                        pe.wait_ge(hot_set[s], it * 2 + 2)
                        for u in range(HALF):
                            last = T.matmul(ps_tab[:, 0:his], hot_a[:, s, u, :], hot_b[:, s, u, :],
                                            start=(first and s == 0 and u == 0), stop=False)
                        last.then_inc(counted[s], 1)
                        pe.wait_ge(src_cols[s], it + 1)
                        pe.wait_ge(dst_cols[s], it + 1)
                        pe.wait_ge(feat_set[s], it + 1)
                        if first and s == 0:
                            pe.wait_ge(steps, when["w_ef"])
                        if not first:
                            pe.wait_ge(msg_set[s], it)
                        for u in range(HALF):
                            o = ps_p[s][:, u * C:(u + 1) * C]
                            e = slice(u * P, (u + 1) * P)
                            T.matmul(o, g_cols[:, 0, e], w_src[:], start=True, stop=False)
                            T.matmul(o, g_cols[:, 1, e], w_dst[:], start=False, stop=False)
                            last = T.matmul(o, feat[:, e], w_ef[:], start=False, stop=True)
                        last.then_inc(pre[s], 1)
                rounds(pe, groups, messages)
                T.matmul(ps_tab[:, 0:his], zeros[:], zeros[:, 0:his], start=False, stop=True).then_inc(p_tab, 1)
                pe.wait_ge(steps, when["counts"])
                T.matmul(ps_s[:, 0:his], same_pair[:, 0:P], tab[:, 0, :], start=True, stop=True).then_inc(p_pairs, 1)
                pe.wait_ge(steps, when["bad"])
                T.matmul(ps_s[:, 0:his], before[:], tab[:, 0, :], start=True, stop=True)
                T.matmul(ps_s[:, 8:8 + his], ones[:], tab[:, 0, :], start=True, stop=True)
                T.matmul(ps_s[:, 16:17], ones[:], bad[:, 0:1], start=True, stop=True).then_inc(p_before, 1)
                pe.wait_ge(steps, when["m_means"])
                for s in range(2):
                    pe.wait_ge(msg_set[s], groups)
                T.matmul(ps_p[0][:, 0:C], m_full[:], mmv[:, 0, :], start=True, stop=False)
                T.matmul(ps_p[0][:, 0:C], m_one[0:rest, :], msg[0:rest, full, 0:C], start=False, stop=True)
                T.matmul(ps_p[1][0:C, 0:1], mmv[:, 0, :], m_full[:, 0:1], start=True, stop=False)
                T.matmul(ps_p[1][0:C, 0:1], msg[0:rest, full, 0:C], m_one[0:rest, 0:1], start=False, stop=True).then_inc(p_mean, 1)
                pe.wait_ge(steps, when["m_devs"])
                T.matmul(ps_p[1][0:C, 2:3], m_dev[:], m_full[:, 0:1], start=True, stop=False)
                T.matmul(ps_p[1][0:C, 2:3], m_tail[0:rest, :], m_one[0:rest, 0:1], start=False, stop=True).then_inc(p_var, 1)
                pe.wait_ge(steps, when["diags"])
                T.matmul(ps_s[:, 0:4 * C], ones[0:C, :], diag.rearrange("p k c -> p (k c)"), start=True, stop=True).then_inc(p_rows, 1)

            @block.scalar
            def _(act):
                def edge_stats(it):
                    for s in range(2):
                        act.wait_ge(ea_used[s], it + 1)
                        if not peeled(it):
                            act.wait_ge(e_stat[s], it)
                        nc.scalar.activation(h[:, s, :], ps_f[s][0:C, :], ACT.Relu).then_inc(e_relu[s], 1)
                rounds(act, groups, edge_stats)
                act.wait_ge(steps, when["e_var"])
                nc.scalar.activation(sc[:, 0, 1:2], sc[:, 0, 0:1], ACT.Sqrt).then_inc(root, 1)

                def messages(it):
                    first = peeled(it)
                    for s in range(2):
                        act.wait_ge(turned[s], it * 2 + 1)
                        if not first or s:
                            act.wait_ge(pre[1 - s], it + s)
                        nc.scalar.copy(g_cols[:, 0, :], ps_t[0][0:C, :]).then_inc(src_cols[s], 1)
                        act.wait_ge(e_layer[s], it + 1)
                        nc.scalar.activation(feat[0:C, :], ps_f[0][0:C, :], ACT.Relu).then_inc(feat_set[s], 1)
                        act.wait_ge(n_layer[s], it + 1)
                        if first:
                            act.wait_ge(steps, when["e_stats"])
                        else:
                            act.wait_ge(n_stat[s], it)
                        nc.scalar.activation(h[:, s, :], ps_f[1][0:C, :], ACT.Relu).then_inc(n_relu[s], 1)
                        act.wait_ge(pre[s], it + 1)
                        nc.scalar.activation(
                            msg[:, bass.ds(it * (2 * HALF) + s * HALF, HALF), 0:C],
                            ps_p[s][:, 0:HALF * C].rearrange("p (u c) -> p u c", u=HALF), ACT.Relu).then_inc(msg_set[s], 1)
                    for s in range(2):
                        act.wait_ge(msg_set[s], it + 1)
                    act.dma_start(rows[bass.ds(it * (2 * COLS), 2 * COLS), :].rearrange("(u p) c -> p u c", p=P),
                                  msg[:, bass.ds(it * (2 * HALF), 2 * HALF), :]).then_inc(stored, 16)
                act.wait_ge(steps, when["consts"])
                rounds(act, groups, messages)
                act.dma_start(rows[n_pad:area, :].rearrange("(p w) c -> p w c", w=WINDOW), pads[:]).then_inc(stored, 16)
                act.wait_ge(steps, when["windows"])
                with nc.allow_non_contiguous_dma(reason="a table of some hundred words"):
                    act.dma_start(lo_tab.rearrange("(b p) k -> p b k", p=P), tab_i[:, :, 2:4]).then_inc(stored, 16)
                act.wait_ge(stored, 16 * (groups + 2))
                act.dma_start(lo_i[:], lo_tab.rearrange("(o t) k -> o (t k)", o=1)).then_inc(stored, 16)
                act.wait_ge(steps, when["mn_var"])
                nc.scalar.activation(sc[:, 1:3, 1], sc[:, 1:3, 0], ACT.Sqrt).then_inc(root, 1)
                act.wait_ge(stored, 16 * (groups + 3))

        for layer in range(3):
            with ExitStack() as c2:
                node_layer(nc, maker(c2, f"l{layer}_"), *semaphores(c2, f"l{layer}_"), c2, layer, groups, chunks,
                           a, out, rows, area, z_tab, x1_tab, bank, iota_f, part_f, ident, base, ends_i, lo_i,
                           pool_sems.get(layer), flag_i, w_node, (w1, w2), rowp, dinv)


def before(s, it, steps):
    q = s - steps
    return q % SLOTS, it + q // SLOTS


def node_layer(nc, sb, sem, pair, ctx, layer, groups, chunks, a, out, rows, area, z_tab, x1_tab, bank, iota_f,
               part_f, ident, base, ends_i, lo_i, pool_sems, flag_i, w_node, w_conv, rowp, dinv):
    n_pad = chunks * P
    halves = 2 * groups
    assert halves % SLOTS
    slope, node_scale, msg_scale, msg_shift = (rowp[:, i, :] for i in range(2, 6))
    width = C if layer else C + 1
    slots = 3
    has_z = layer < 2
    has_ln = layer != 1
    turn_lag = 4 if has_ln else 2
    last_lag = 4 if layer == 0 else 3 if has_ln else 2
    win = sb("win", [P, SLOTS, 2, WINDOW, R])
    hot = sb("hot", [P, SLOTS, 2 * WINDOW, 2, P])
    numbers = sb("numbers", [P, 2, WINDOW, 2, P])
    acc = sb("acc", [P, SLOTS, 3, HALF, C])
    if layer == 0:
        deg = sb("deg", [P, SLOTS, HALF])
        xc = sb("xc", [C + 1, SLOTS, COLS])
    else:
        zr = sb("zr", [P, SLOTS, HALF, C])
        g_rows = sb("g_rows", [P, slots, 2 * HALF, C])
        idx = sb("idx", [P, slots, 2 * HALF], I32)
    if has_ln:
        xr = sb("xr", [P, SLOTS, HALF, C])
        ln = sb("ln", [P, SLOTS, HALF, 6])
        mv = sb("mv", [P, SLOTS, 5, HALF])
        dev = sb("dev", [P, SLOTS, 2, HALF])
        inv = sb("inv", [P, SLOTS, HALF])
        offsets = sb("offsets", [P, 2])
        lift = sb("lift", [P, SLOTS, HALF])
        o_rows = sb("o_rows", [P, SLOTS, HALF, C])
    if has_z:
        o_cols = sb("o_cols", [C, COLS])
        z_out = sb("z_out", [P, SLOTS, HALF, C])
    big = sb("big", [P, 2 * HALF, R])
    sums = sb("sums", [P, WINDOW, R])
    first_node = sb("first_node", [P, 1])

    def each(name):
        return pair(name, SLOTS)

    win_in, z_in, res_in, xc_in = each("win_in"), each("z_in"), each("res_in"), each("xc_in")
    hot_set, summed, own_x, shifts = (each(k) for k in ("hot_set", "summed", "own_x", "shifts"))
    own_relu, own_scaled, own_set = each("own_relu"), each("own_scaled"), each("own_set")
    y1, y2, y3, y4, deg_set, y_set = (each(k) for k in ("y1", "y2", "y3", "y4", "deg_set", "y_set"))
    ln_set, mv_set, var_set, roots = (each(k) for k in ("ln_set", "mv_set", "var_set", "roots"))
    deg_root, rstd_set = each("deg_root"), each("rstd_set")
    lifted, o_set, turned, cols_set, z_ps, z_set = (each(k) for k in ("lifted", "o_set", "turned", "cols_set", "z_ps", "z_set"))
    o_out, z_st, dinv_set = each("o_out"), each("z_st"), each("dinv_set")
    idx_set = [sem(f"idx_set{i}") for i in range(slots)]
    passed, act_passed, numbered = sem("passed"), sem("act_passed"), sem("numbered")
    big_in, big_hot, big_sum, big_acc, big_zero, big_key, big_out = (
        sem(k) for k in ("big_in", "big_hot", "big_sum", "big_acc", "big_zero", "big_key", "big_out"))
    if layer:
        gathered, rows_in = pool_sems[0:slots], pool_sems[slots]

    ps_a, ps_own, ps_t, ps_z = bank[0:2], (bank[2:4], bank[4:6]), bank[6], bank[7]
    z_of = z_tab[layer - 1] if layer else None
    z_to = z_tab[layer] if has_z else None

    block = ctx.enter_context(nc.Block())

    def tiles_of(table, at):
        return table[bass.ds(at, COLS), :].rearrange("(j p t) c -> p j (t c)", p=P, t=2)

    def by_pair(rows_of):
        return rows_of.rearrange("p (j t) c -> p j (t c)", t=2)

    def own_part(s, j, part):
        return ps_own[j][s % 2][:, 0:4 * C].rearrange("p (t k c) -> p t k c", t=2, k=2)[:, :, part, :]

    def tile(s, k):
        return k * (SLOTS * HALF) + s * HALF

    def exists(half):
        s, k = half
        return not peeled(k) or 0 <= k * SLOTS + s < halves

    def all_steps(eng, step, more=0):
        def body(it):
            for s in range(SLOTS):
                step(s, it)
        rounds(eng, halves // SLOTS, body, ahead=2)
        for h in range(halves // SLOTS * SLOTS, halves + more):
            step(h % SLOTS, h // SLOTS)

    def all_of(eng, signal, times):
        for s in range(SLOTS):
            eng.wait_ge(signal[s], times * ((halves - s + SLOTS - 1) // SLOTS))

    if layer:
        @block.gpsimd
        def _(pool):
            def indices(it, s):
                nc.gpsimd.tensor_copy(idx[:, s], ends_i[:, 0, bass.ds(it * (slots * 2 * HALF) + s * 2 * HALF, 2 * HALF)]).then_inc(idx_set[s], 1)

            def store(it, s):
                pool.wait_ge(gathered[s], it * (16 * 2 * HALF) + 16 * 2 * HALF)
                if later(it) or s:
                    pool.wait_ge(rows_in, it * (16 * slots) + 16 * s)
                pool.dma_start(rows[bass.ds(it * (slots * 2 * COLS) + s * 2 * COLS, 2 * COLS), 0:C].rearrange("(u p) c -> p u c", p=P),
                               g_rows[:, s]).then_inc(rows_in, 16)

            def group(it, s, last=False):
                if not last:
                    indices(it + 1 if s == slots - 1 else it, (s + 1) % slots)
                pool.wait_ge(idx_set[s], it + 1)
                if not peeled(it):
                    pool.sem_inc(passed, 1)
                for u in range(2 * HALF):
                    nc.gpsimd.indirect_dma_start(
                        g_rows[:, s, u, :], None, z_of, bass.IndirectOffsetOnAxis(idx[:, s, u:u + 1], axis=0),
                    ).then_inc(gathered[s], 16)
                if s:
                    store(it, s - 1)
                elif later(it):
                    store(it - 1, slots - 1)

            def three(it):
                for s in range(slots):
                    group(it, s)
            indices(0, 0)
            whole = (groups - 1) // slots
            rounds(pool, whole, three)
            for s in range(groups - whole * slots):
                group(whole, s, last=s == groups - whole * slots - 1)
            store(whole, groups - whole * slots - 1)
    else:
        @block.gpsimd
        def _(pool):
            def own_rows(s, k):
                A = acc[:, s]
                pool.wait_ge(own_relu[s], k * 2 + 2)
                if later(k):
                    pool.wait_ge(y_set[s], k)
                nc.gpsimd.tensor_tensor(A[:, 1], A[:, 0], rowwise(node_scale, HALF), ALU.mult).then_inc(own_scaled[s], 1)
                pool.wait_ge(deg_set[s], k + 1)
                nc.gpsimd.tensor_tensor(xr[:, s], wide(deg[:, s], C), rowwise(msg_shift, HALF), ALU.mult).then_inc(shifts[s], 1)
                pool.wait_ge(own_scaled[s], k + 1)
                pool.wait_ge(shifts[s], k + 1)
                nc.gpsimd.tensor_tensor(A[:, 1], A[:, 1], xr[:, s], ALU.add).then_inc(own_set[s], 1)

            all_steps(pool, own_rows)

    @block.sync
    def _(sp):
        flag = sp.value_load(flag_i[0:1, 0:1], min_val=0, max_val=1)
        with sp.If(flag == 1):
            if layer:
                sp.wait_ge(rows_in, 16 * groups)
            with sp.Fori(0, chunks // 2) as t:
                with sp.Fori(0, groups) as k:
                    free = sp.snap(t * groups + k + 1)
                    at = sp.snap(k * (2 * COLS))
                    sp.wait_ge(big_acc, free)
                    sp.dma_start(big[:], rows[bass.ds(at, 2 * COLS), :].rearrange("(p u) c -> p u c", p=P)).then_inc(big_in, 16)
                summed_all = sp.snap(t * groups + (groups + 1))
                to = sp.snap(t * WIN + area)
                sp.wait_ge(big_acc, summed_all)
                sp.dma_start(rows[bass.ds(to, WIN), :].rearrange("(p w) c -> p w c", w=WINDOW), sums[:]).then_inc(big_out, 16)
            sp.wait_ge(big_out, 16 * (chunks // 2))

        def loads(s, it):
            at = tile(s, it) * P
            used = it
            if not peeled(it):
                at, used = sp.snap(at), sp.snap(used)
            entry = [(tile(s, it) + 2 * j) * 2 for j in range(2)]
            lows = [sp.value_load(lo_i[0:1, bass.ds(e, 1)], min_val=0, max_val=area + (chunks // 2 - 1) * WIN) for e in entry]
            if layer:
                need = sp.value_load(lo_i[0:1, bass.ds(entry[1] + 1, 1)], min_val=16, max_val=16 * groups)
            if later(it):
                sp.wait_ge(summed[s], used)
            if layer:
                sp.wait_ge(rows_in, need)
            for j, low in enumerate(lows):
                sp.dma_start(win[:, s, j], rows[bass.ds(low, WIN), :].rearrange("(p w) c -> p w c", w=WINDOW)).then_inc(win_in[s], 16)
            if layer == 0:
                if later(it):
                    sp.wait_ge(own_x[s], used)
                sp.dma_start(xc[:, s, :], a["xT"][:, bass.ds(at, COLS)]).then_inc(xc_in[s], 16)
            else:
                sp.dma_start(by_pair(zr[:, s]), tiles_of(z_of, at)).then_inc(z_in[s], 16)
            if layer == 2:
                if later(it):
                    sp.wait_ge(y_set[s], used)
                sp.dma_start(by_pair(xr[:, s]), tiles_of(x1_tab, at)).then_inc(res_in[s], 16)
        all_steps(sp, loads)

    @block.vector
    def _(dve):
        V = nc.vector
        for v in range(2):
            V.tensor_scalar(numbers[:, 0, 0, v], iota_f[:], 2.0, float(v), ALU.mult, ALU.add).then_inc(numbered, 1)
        dve.wait_ge(numbered, 2)
        for w in range(1, WINDOW):
            V.tensor_copy(numbers[:, 0, w], numbers[:, 0, 0]).then_inc(numbered, 1)
        for w in range(WINDOW):
            V.tensor_scalar(numbers[:, 1, w], numbers[:, 0, 0], 2.0 * P, None, ALU.add).then_inc(numbered, 1)
        dve.wait_ge(numbered, 2 * WINDOW + 1)
        if has_ln:
            V.memset(offsets[:, 0:1], EPS).then_inc(numbered, 1)
            V.memset(offsets[:, 1:2], 1.0).then_inc(numbered, 1)
        flag = dve.value_load(flag_i[0:1, 0:1], min_val=0, max_val=1)
        with dve.If(flag == 1):
            every = hot[:].rearrange("p s w t m -> p (s w t m)")[:, 0:4 * HALF * P].rearrange("p (u t m) -> p u t m", t=2, m=P)
            V.memset(sums[:], 0.0).then_inc(big_zero, 1)
            V.memset(first_node[:], -2.0 * P).then_inc(big_zero, 1)
            dve.wait_ge(big_zero, 2)
            V.memset(sums[:, 2, DST:DST + 1], float(n_pad - 1)).then_inc(big_zero, 1)
            dve.wait_ge(big_zero, 3)
            V.memset(sums[:, 0, 0:1], 0.0).then_inc(big_acc, 1)
            with dve.Fori(0, chunks // 2) as t:
                dve.wait_ge(big_acc, t * groups + 1)
                V.tensor_scalar(first_node[:], first_node[:], 2.0 * P, None, ALU.add).then_inc(big_zero, 1)
                V.memset(sums[:, 0:2, 0:DST], 0.0).then_inc(big_zero, 1)
                dve.wait_ge(big_zero, t * 4 + 5)
                for v in range(2):
                    V.tensor_scalar(sums[:, v, DST:DST + 1], part_f[:], 2.0, float(v), ALU.mult, ALU.add).then_inc(big_zero, 1)
                dve.wait_ge(big_zero, t * 4 + 7)
                V.tensor_scalar(sums[:, 0:2, DST], sums[:, 0:2, DST], first_node[:, 0:1], None, ALU.add).then_inc(big_key, 1)
                with dve.Fori(0, groups) as k:
                    dve.wait_ge(big_key, t + 1)
                    dve.wait_ge(big_in, t * (16 * groups) + k * 16 + 16)
                    V.scalar_tensor_tensor(every.rearrange("p u t m -> p u (t m)"), wide(big[:, :, DST], 2 * P), first_node[:, 0:1],
                                           rowwise(numbers[:, 0, 0].rearrange("p t m -> p (t m)"), 2 * HALF),
                                           ALU.subtract, ALU.is_equal).then_inc(big_hot, 1)
                    dve.wait_ge(big_sum, t * groups + k + 1)
                    V.tensor_tensor(sums[:, 0:2, 0:DST], sums[:, 0:2, 0:DST],
                                    ps_a[0][:, 0:2 * DST].rearrange("p (t c) -> p t c", t=2), ALU.add).then_inc(big_acc, 1)
                    dve.wait_ge(big_acc, t * groups + k + 2)
                dve.wait_ge(big_out, t * 16 + 16)

        def one_hots(j, s, k):
            if later(k):
                dve.wait_ge(summed[s], k)
            dve.wait_ge(win_in[s], k * 32 + 32)
            V.scalar_tensor_tensor(hot[:, s, j * WINDOW:(j + 1) * WINDOW].rearrange("p w t m -> p w (t m)"),
                                   wide(win[:, s, j, :, DST], 2 * P),
                                   base[:, bass.ds(k * SLOTS + s, 1)], numbers[:, j].rearrange("p w t m -> p w (t m)"),
                                   ALU.subtract, ALU.is_equal).then_inc(hot_set[s], 1)

        def norm_1(s, k):
            dve.wait_ge(ln_set[s], k * HALF + HALF)
            V.tensor_tensor(mv[:, s, 0], ln[:, s, :, 1], ln[:, s, :, 4], ALU.add).then_inc(mv_set[s], 1)
            V.tensor_tensor(mv[:, s, 1], ln[:, s, :, 1], ln[:, s, :, 4], ALU.subtract).then_inc(mv_set[s], 1)
            V.tensor_tensor(mv[:, s, 2], ln[:, s, :, 2], ln[:, s, :, 5], ALU.add).then_inc(mv_set[s], 1)

        def norm_2(s, k):
            dve.wait_ge(mv_set[s], k * 4 + 3)
            V.scalar_tensor_tensor(mv[:, s, 3], mv[:, s, 1], 0.25, mv[:, s, 1], ALU.mult, ALU.mult).then_inc(mv_set[s], 1)

        def norm_3(s, k):
            if later(k):
                dve.wait_ge(roots[s], k)
            dve.wait_ge(mv_set[s], k * 4 + 4)
            V.scalar_tensor_tensor(mv[:, s, 4], mv[:, s, 2], 1.0 / C, mv[:, s, 3], ALU.mult, ALU.add).then_inc(var_set[s], 1)

        def norm_4(s, k):
            if later(k):
                dve.wait_ge(o_set[s], k * HALF)
            dve.wait_ge(roots[s], k + 1)
            V.reciprocal(inv[:, s], dev[:, s, 0]).then_inc(rstd_set[s], 1)
            if layer == 0:
                dve.wait_ge(deg_root[s], k + 1)
                V.reciprocal(dinv[:, bass.ds(tile(s, k), HALF)], dev[:, s, 1]).then_inc(dinv_set[s], 1)

        def norm_5(s, k):
            dve.wait_ge(rstd_set[s], k + 1)
            V.scalar_tensor_tensor(lift[:, s], mv[:, s, 0], -0.5, inv[:, s], ALU.mult, ALU.mult).then_inc(lifted[s], 1)

        def statistics(s, k, y):
            dve.wait_ge(y_set[s], k + 1)
            for u in range(HALF):
                V.bn_stats(ln[:, s, u], y[:, u]).then_inc(ln_set[s], 1)

        def nodes_0(s, k):
            A = acc[:, s]

            def one():
                if later(k):
                    dve.wait_ge(o_set[s], k * HALF)
                dve.wait_ge(deg_set[s], k + 1)
                V.tensor_tensor(A[:, 2], ps_a[s % 2][:, 0:HALF * (C + 1)].rearrange("p (t c) -> p t c", t=HALF)[:, :, 0:C],
                                rowwise(msg_scale, HALF), ALU.mult).then_inc(y1[s], 1)

            def two():
                dve.wait_ge(own_relu[s], k * 2 + 2)
                dve.wait_ge(y1[s], k + 1)
                for j in range(2):
                    V.tensor_tensor(A[:, 2, 2 * j:2 * j + 2], own_part(s, j, 1), A[:, 2, 2 * j:2 * j + 2], ALU.add).then_inc(y2[s], 1)

            def three():
                dve.wait_ge(own_set[s], k + 1)
                dve.wait_ge(y2[s], k * 2 + 2)
                V.tensor_tensor(A[:, 2], A[:, 2], A[:, 1], ALU.add).then_inc(y_set[s], 1)

            return one, two, three, lambda: statistics(s, k, A[:, 2])

        def nodes_12(s, k):
            A = acc[:, s]

            def one():
                dve.wait_ge(y1[s], k * HALF + HALF)
                V.tensor_tensor(A[:, 0], A[:, 0], rowwise(rowp[:, layer - 1, :], HALF), ALU.add).then_inc(y2[s], 1)

            def two():
                if layer == 2 and later(k):
                    dve.wait_ge(o_set[s], k * HALF)
                dve.wait_ge(y2[s], k + 1)
                V.scalar_tensor_tensor(A[:, 1], A[:, 0], 0.0, rowwise(slope, HALF), ALU.min, ALU.mult).then_inc(y3[s], 1)

            def three():
                if layer == 1 and later(k):
                    dve.wait_ge(turned[s], k)
                dve.wait_ge(y3[s], k + 1)
                V.scalar_tensor_tensor(A[:, 2], A[:, 0], 0.0, A[:, 1], ALU.max, ALU.add).then_inc(y4[s], 1)

            def four():
                if layer == 2:
                    dve.wait_ge(res_in[s], k * 16 + 16)
                    dve.wait_ge(y4[s], k + 1)
                    V.tensor_tensor(A[:, 1], A[:, 2], xr[:, s], ALU.add).then_inc(y_set[s], 1)
                    statistics(s, k, A[:, 1])

            return one, two, three, four

        def step(s, it):
            following, one, two = (before(s, it, j) for j in (-1, 1, 2))
            values = (nodes_12 if layer else nodes_0)(*one) if exists(one) else ()
            norms = (norm_1, norm_2, norm_3, norm_4, norm_5) if has_ln and exists(two) else ()
            for j in range(5):
                if j < len(norms):
                    norms[j](*two)
                if j < len(values):
                    values[j]()
                if j < 2 and exists(following):
                    one_hots(j, *following)
        for j in range(2):
            one_hots(j, 0, 0)
        all_steps(dve, step, last_lag)

    @block.tensor
    def _(pe):
        T = nc.tensor
        flag = pe.value_load(flag_i[0:1, 0:1], min_val=0, max_val=1)
        with pe.If(flag == 1):
            with pe.Fori(0, chunks // 2) as t:
                with pe.Fori(0, groups) as k:
                    pe.wait_ge(big_hot, t * groups + k + 1)
                    every = hot[:].rearrange("p s w t m -> p (s w t m)")[:, 0:4 * HALF * P].rearrange("p (u t m) -> p u t m", t=2, m=P)
                    for v in range(2):
                        for u in range(2 * HALF):
                            last = T.matmul(ps_a[0][:, v * DST:(v + 1) * DST], every[:, u, v], big[:, u, 0:DST],
                                            start=(u == 0), stop=(u == 2 * HALF - 1))
                    last.then_inc(big_sum, 1)

        def turn(s, k):
            of = acc[:, s, 2] if layer else o_rows[:, s]
            pe.wait_ge(y4[s] if layer else o_set[s], k + 1 if layer else k * HALF + HALF)
            last_one = before(s, k, 1)
            if exists(last_one):
                pe.wait_ge(cols_set[last_one[0]], last_one[1] + 1)
            for u in range(HALF):
                last = T.transpose(ps_t[0:C, u * P:(u + 1) * P], of[:, u, :], ident[:])
            last.then_inc(turned[s], 1)

        def product(s, k):
            pe.wait_ge(cols_set[s], k + 1)
            last_one = before(s, k, 1)
            if exists(last_one):
                pe.wait_ge(z_set[last_one[0]], last_one[1] * HALF + HALF)
            for u in range(HALF):
                last = T.matmul(ps_z[:, u * C:(u + 1) * C], o_cols[:, u * P:(u + 1) * P], w_conv[layer][:], start=True, stop=True)
            last.then_inc(z_ps[s], 1)

        def sum_edges(s, k):
            pe.wait_ge(hot_set[s], k * 2 + 2)
            two = before(s, k, 2)
            if exists(two):
                pe.wait_ge(y1[two[0]], two[1] * HALF + HALF if layer else two[1] + 1)
                if layer == 0:
                    pe.wait_ge(deg_set[two[0]], two[1] + 1)
            if layer:
                pe.wait_ge(z_in[s], k * 16 + 16)
                T.matmul(ps_a[s % 2][:, 0:HALF * C], ident[:], zr[:, s].rearrange("p t c -> p (t c)"), start=True, stop=False)
            for u in range(HALF):
                for w in range(WINDOW):
                    last = T.matmul(ps_a[s % 2][:, u * width:(u + 1) * width], hot[:, s, u // 2 * WINDOW + w, u % 2, :],
                                    win[:, s, u // 2, w, 0:width], start=(layer == 0 and w == 0),
                                    stop=(w == WINDOW - 1 and (layer == 0 or u == HALF - 1)))
            last.then_inc(summed[s], 1)

        def own_features(s, k):
            pe.wait_ge(xc_in[s], k * 16 + 16)
            two = before(s, k, 2)
            if exists(two):
                pe.wait_ge(own_relu[two[0]], two[1] * 2 + 2)
                pe.wait_ge(y2[two[0]], two[1] * 2 + 2)
            for u in range(HALF):
                to = ps_own[u // 2][s % 2][:, (u % 2) * 2 * C:(u % 2 + 1) * 2 * C]
                last = T.matmul(to, xc[:, s, u // 2 * 2 * P + u % 2:(u // 2 + 1) * 2 * P:2],
                                w_node[:].rearrange("p k c -> p (k c)"), start=True, stop=True)
            last.then_inc(own_x[s], 1)

        def step(s, it):
            here, old = (s, it), before(s, it, turn_lag)
            if has_z and exists(old):
                turn(*old)
            if exists(here):
                if layer == 0:
                    own_features(*here)
                sum_edges(*here)
            if has_z and exists(old):
                product(*old)
        all_steps(pe, step, last_lag)

    @block.scalar
    def _(act):
        def own_features(s, k):
            act.wait_ge(own_x[s], k + 1)
            if later(k):
                act.wait_ge(own_scaled[s], k)
            for j in range(2):
                nc.scalar.activation(acc[:, s, 0, 2 * j:2 * j + 2], own_part(s, j, 0), ACT.Relu).then_inc(own_relu[s], 1)

        def sums_out(s, k):
            act.wait_ge(summed[s], k + 1)
            if layer == 0:
                if later(k):
                    act.wait_ge(shifts[s], k)
                    act.wait_ge(deg_root[s], k)
                nc.scalar.copy(deg[:, s], ps_a[s % 2][:, 0:HALF * (C + 1)].rearrange("p (t c) -> p t c", t=HALF)[:, :, C]).then_inc(deg_set[s], 1)
                return
            if later(k):
                act.wait_ge(y4[s], k)
            for u in range(HALF):
                nc.scalar.activation(acc[:, s, 0, u], ps_a[s % 2][:, u * C:(u + 1) * C], ACT.Copy,
                                     scale=dinv[:, bass.ds(tile(s, k) + u, 1)]).then_inc(y1[s], 1)

        def square_roots(s, k):
            act.wait_ge(var_set[s], k + 1)
            if later(k):
                act.wait_ge(rstd_set[s], k)
            nc.scalar.activation(dev[:, s, 0], mv[:, s, 4], ACT.Sqrt, bias=offsets[:, 0:1]).then_inc(roots[s], 1)

        def degree_roots(s, k):
            act.wait_ge(deg_set[s], k + 1)
            if later(k):
                act.wait_ge(dinv_set[s], k)
            nc.scalar.activation(dev[:, s, 1], deg[:, s], ACT.Sqrt, bias=offsets[:, 1:2]).then_inc(deg_root[s], 1)

        def norm(s, k):
            act.wait_ge(lifted[s], k + 1)
            if later(k):
                act.wait_ge(o_out[s], k * 16)
                if layer == 0:
                    act.wait_ge(turned[s], k)
            for u in range(HALF):
                nc.scalar.activation(o_rows[:, s, u], acc[:, s, 1 if layer else 2, u], ACT.Identity,
                                     bias=lift[:, s, u:u + 1], scale=inv[:, s, u:u + 1]).then_inc(o_set[s], 1)
            act.wait_ge(o_set[s], k * HALF + HALF)
            act.dma_start(tiles_of(out if layer else x1_tab, tile(s, k) * P), by_pair(o_rows[:, s])).then_inc(o_out[s], 16)

        def columns(s, k):
            act.wait_ge(turned[s], k + 1)
            last_one = before(s, k, 1)
            if exists(last_one):
                act.wait_ge(z_ps[last_one[0]], last_one[1] + 1)
            nc.scalar.copy(o_cols[:], ps_t[0:C, :]).then_inc(cols_set[s], 1)

        def next_rows(s, k):
            act.wait_ge(z_ps[s], k + 1)
            if layer == 0:
                act.wait_ge(dinv_set[s], k + 1)
            if later(k):
                act.wait_ge(z_st[s], k * 16)
            if not peeled(k):
                act.sem_inc(act_passed, 1)
            for u in range(HALF):
                nc.scalar.activation(z_out[:, s, u], ps_z[:, u * C:(u + 1) * C], ACT.Copy,
                                     scale=dinv[:, bass.ds(tile(s, k) + u, 1)]).then_inc(z_set[s], 1)
            act.wait_ge(z_set[s], k * HALF + HALF)
            act.dma_start(tiles_of(z_to, tile(s, k) * P), by_pair(z_out[:, s])).then_inc(z_st[s], 16)

        def step(s, it):
            here, one, two, three, old = (s, it), *(before(s, it, j) for j in (1, 2, 3, turn_lag))
            if has_z and exists(old):
                columns(*old)
            if has_ln and exists(three):
                norm(*three)
            if layer == 0 and exists(one):
                degree_roots(*one)
            if layer == 0 and exists(here):
                own_features(*here)
            if has_ln and exists(two):
                square_roots(*two)
            if exists(here):
                sums_out(*here)
            if has_z and exists(old):
                next_rows(*old)
        if has_ln:
            act.wait_ge(numbered, 2 * WINDOW + 3)
        all_steps(act, step, last_lag)
        if has_ln:
            all_of(act, o_out, 16)
        if has_z:
            all_of(act, z_st, 16)


_SHAPE_ROWS = 2 * COLS


def lay_out(inputs):
    import numpy as np

    g = {k: np.asarray(v) for k, v in inputs.items()}
    n = g["x"].shape[0]
    n_pad = -(-n // _SHAPE_ROWS) * _SHAPE_ROWS
    more = n_pad - n

    def by_chunk(v):
        return np.ascontiguousarray(v.reshape(-1, P).T)

    src = np.concatenate([g["src"], np.zeros(more, np.int32)])
    dst = np.concatenate([g["dst"], np.full(more, n_pad - 1, np.int32)])
    nxt = np.concatenate([dst[1:], np.full(1, n_pad - 1, np.int32)])
    x = np.concatenate([g["x"], np.zeros((more, C), np.float32)])
    ea = np.concatenate([g["edge_attr_4"], np.zeros((more, 4), np.float32)])
    one = np.ones((1, n_pad), np.float32)
    row = lambda k: g[k].reshape(1, C)
    a = {
        "x": x, "xT": np.concatenate([x.T, one]), "eaT": np.concatenate([ea.T, one]),
        "src": by_chunk(src), "dst": by_chunk(dst), "dst_next": by_chunk(nxt),
        "W_edge": g["L0_gnn_W_edge"], "b_edge": row("L0_gnn_b_edge"),
        "W_node": g["L0_gnn_W_node"], "b_node": row("L0_gnn_b_node"),
        "W_msg": g["L0_gnn_W_msg"], "b_msg": row("L0_gnn_b_msg"),
        "gb": np.stack([g[f"L0_gnn_{k}_{w}"] for w in ("edge", "msg", "node") for k in ("g", "beta")], 1),
        "W1": g["L1_gnn_W1"], "W2": g["L1_gnn_W2"],
        "b1": row("L1_gnn_b1"), "b2": row("L1_gnn_b2"), "prelu": row("L1_gnn_prelu_a"),
    }
    return n, n_pad, {k: np.ascontiguousarray(v) for k, v in a.items()}


def kernel(**inputs):
    import concourse.bacc as _bacc
    from concourse.bass_utils import run_bass_kernel_spmd as _run

    n, n_pad, arrays = lay_out(inputs)
    nc = _bacc.Bacc("TRN2", target_bir_lowering=False, num_devices=1)
    args = {k: nc.dram_tensor(f"in_{k}", v.shape, mybir.dt.from_np(v.dtype), kind="ExternalInput").ap()
            for k, v in arrays.items()}
    out = nc.dram_tensor("out_0", (n_pad, C), F32, kind="ExternalOutput").ap()
    build_program(nc, n, args, out)
    r = _run(nc, [{f"in_{k}": v for k, v in arrays.items()}], core_ids=[0])
    return r.results[0]["out_0"][:n]
```

```python
from contextlib import ExitStack

import concourse.bass as bass
from concourse import mybir

P = 128
C = 96
R = C + 2
CNT, DST = C, C + 1
HALF = 4
COLS = HALF * P
WINDOW = 3
WIN = WINDOW * P
SLOTS = 4
EPS = 1e-5

F32 = mybir.dt.float32
BF16 = mybir.dt.bfloat16
I32 = mybir.dt.int32
ALU = mybir.AluOpType
ACT = mybir.ActivationFunctionType


def rounds(eng, n, body, ahead=1):
    for it in range(min(ahead, n)):
        body(it)
    if n > ahead:
        with eng.Fori(ahead, n) as it:
            body(it)


def peeled(it):
    return isinstance(it, int)


def later(it):
    return not (peeled(it) and it == 0)


def wide(ap, n):
    return ap.unsqueeze(2).to_broadcast([ap.shape[0], ap.shape[1], n])


def rowwise(ap, k):
    return ap.unsqueeze(1).to_broadcast([ap.shape[0], k, ap.shape[1]])


def build_program(nc, n, a, out):
    n_pad = out.shape[0]
    groups = n_pad // (2 * COLS)
    chunks = n_pad // P
    full = n // P
    rest = n - full * P
    last_cols = n - (2 * groups - 1) * COLS
    his = -(-chunks // P)
    area = n_pad + WIN
    assert 0 < last_cols <= COLS and rest > 0 and full <= 512

    rows = nc.dram_tensor("rows", [area + chunks // 2 * WIN, R], F32, kind="Internal").ap()
    z_tab = [nc.dram_tensor(f"z{i}", [n_pad, C], F32, kind="Internal").ap() for i in (1, 2)]
    x1_tab = nc.dram_tensor("x1", [n_pad, C], F32, kind="Internal").ap()
    lo_tab = nc.dram_tensor("lo", [his * P, 2], I32, kind="Internal").ap()

    with ExitStack() as ctx:
        def maker(c, prefix=""):
            return lambda name, shape, dt=F32: c.enter_context(nc.sbuf_tensor(prefix + name, shape, dt))

        def semaphores(c, prefix=""):
            held = []

            def sem(name):
                held.append(c.enter_context(nc.semaphore(prefix + name)))
                return held[-1]

            c.callback(clear, held)
            return sem, lambda name, n=2: [sem(f"{name}_{i}") for i in range(n)]

        def clear(held):
            with nc.Block() as between:
                @between.gpsimd
                def _(pool):
                    for one in held:
                        pool.sem_clear(one)

        gathered_msg = [ctx.enter_context(nc.semaphore(f"gathered_msg{i}")) for i in range(3)]
        pool_sems = {k: [ctx.enter_context(nc.semaphore(f"l{k}_{m}")) for m in ("gathered0", "gathered1", "gathered2", "rows_in")]
                     for k in (1, 2)}

        sb = maker(ctx)
        bank = [ctx.enter_context(nc.psum_tensor(f"bank{i}", [P, 512], F32)) for i in range(8)]

        iota_f = sb("iota_f", [P, P])
        part_f = sb("part_f", [P, 1])
        ident = sb("ident", [P, P])
        base = sb("base", [P, 2 * groups])
        ends_i = sb("ends_i", [P, 2, chunks], I32)
        shared = sb("shared", [P, max(his * P * 2, 2 * WINDOW * C + chunks // 2)])
        lo_i = shared[0:1, 0:his * P * 2].bitcast(I32)
        flag_i = sb("flag_i", [1, 1], I32)
        w_node = sb("w_node", [C + 1, 2, C])
        w1 = sb("w1", [C, C])
        w2 = sb("w2", [C, C])
        rowp = sb("rowp", [P, 6, C])
        dinv = sb("dinv", [P, chunks])

        with ExitStack() as c1:
            sb1 = maker(c1)
            sem, pair = semaphores(c1, "m_")
            msg = sb1("msg", [P, chunks, R])
            tiles_f = sb1("tiles_f", [P, 2, chunks])
            part_i = sb1("part_i", [P, 1], I32)
            same_pair = sb1("same_pair", [P, P + 1])
            base_i = sb1("base_i", [P, 2 * groups], I32)
            idx = sb1("idx", [P, 2, 2, HALF], I32)
            g_rows = sb1("g_rows", [P, 2, 2, HALF, C])
            free = g_rows[:].rearrange("p s w u c -> p (s w u c)")
            iota_i = free[:, 2 * chunks:2 * chunks + P].bitcast(I32)
            pairs_i = free[:, 2 * chunks + P:2 * chunks + 2 * P + 1].bitcast(I32)
            ints = free[:, 0:2 * chunks].bitcast(I32).rearrange("p (k n) -> p k n", k=2)
            mst = free[:, 0:6 * C].rearrange("p (c k) -> p c k", k=6)
            mmv = free[:, 6 * C:8 * C].rearrange("p (k c) -> p k c", k=2)
            diag = free[0:C, 10 * C:14 * C].rearrange("p (k c) -> p k c", k=4)
            m_dev, m_tail = free[:, 8 * C:9 * C], free[:, 9 * C:10 * C]
            g_cols = sb1("g_cols", [C, 2, COLS])
            feat = sb1("feat", [C + 1, COLS])
            ea = sb1("ea", [P, 2, COLS])
            xc = sb1("xc", [C + 1, 2, COLS])
            h = sb1("h", [C, 2, COLS])
            h4 = [h[:, 0, :], h[:, 1, :], g_cols[:, 0, :], g_cols[:, 1, :]]
            st = sb1("st", [C, 2 * groups, 6])
            hot_a = sb1("hot_a", [P, 2, HALF, P], BF16)
            hot_b = sb1("hot_b", [P, 2, HALF, his], BF16)
            ones = sb1("ones", [P, P])
            zeros = sb1("zeros", [P, P], BF16)
            x_words = 2 * WINDOW * C
            x_win = shared[:, 0:x_words].rearrange("p (j w c) -> p j w c", j=2, w=WINDOW)
            firsts_i = shared[:, x_words:x_words + chunks // 2].bitcast(I32)
            firsts = dinv[:, 0:chunks // 2]
            dst_i = sb1("dst_i", [P, COLS], I32)
            dst_rel = dst_i[:].bitcast(F32)
            hot_x = sb1("hot_x", [P, WINDOW, COLS])
            node_0 = sb1("node_0", [P, 1])
            far = sb1("far", [P, 1])
            far_i = sb1("far_i", [1, 1], I32)
            ea4 = [ea[:, 0, :], ea[:, 1, :], hot_x[:, 0, :], hot_x[:, 1, :]]
            m_full, m_one, before = (hot_x[:, 0, i * P:(i + 1) * P] for i in range(3))
            pads = hot_x[:, 1, 0:WINDOW * R].rearrange("p (w c) -> p w c", w=WINDOW)
            w_edge = sb1("w_edge", [P, C])
            w_src = sb1("w_src", [C, C])
            w_dst = sb1("w_dst", [C, C])
            w_ef = sb1("w_ef", [C + 1, C])
            b_msg = sb1("b_msg", [1, C])
            gb = sb1("gb", [C, 6])
            mv = sb1("mv", [C, 3, 2])
            sc = sb1("sc", [C, 3, 4])
            tab = sb1("tab", [P, 10, his])
            bad = sb1("bad", [P, 2])
            tab_i = sb1("tab_i", [P, his, 4], I32)
            w_raw = sb1("w_raw", [C, C])

            loaded = sem("loaded"); iotas = sem("iotas")
            ea_in, ea_used, e_relu, e_stat = (pair(k, SLOTS) for k in ("ea_in", "ea_used", "e_relu", "e_stat"))
            gathered = gathered_msg; turned = pair("turned")
            src_cols = pair("src_cols"); dst_cols = pair("dst_cols")
            mea_in = pair("mea_in"); e_layer = pair("e_layer"); feat_set = pair("feat_set")
            xc_in = pair("xc_in"); n_layer = pair("n_layer"); n_relu = pair("n_relu"); n_stat = pair("n_stat")
            pre = pair("pre"); msg_set = pair("msg_set"); stored = sem("stored")
            gathered_far = gathered_msg[2]
            x_win_in, dst_in, rel_set, hot_x_set, p_far = (sem(k) for k in ("x_win_in", "dst_in", "rel_set", "hot_x_set", "p_far"))
            hot_set = pair("hot_set"); counted = pair("counted")
            steps = sem("steps"); root = sem("root"); m_stat = sem("m_stat"); copied = pair("copied")
            p_shift = sem("p_shift"); p_tab = sem("p_tab"); p_before = sem("p_before"); p_pairs = sem("p_pairs"); p_mean = sem("p_mean")
            p_var = sem("p_var"); passed = sem("passed"); sp_passed = sem("sp_passed"); p_rows = sem("p_rows")

            ps_t, ps_f, ps_p, ps_tab, ps_s = bank[0:2], bank[2:4], bank[4:6], bank[6], bank[7]
            loads = [(firsts_i, a["dst_first"]), (ends_i[:, 1, :], a["dst"]), (ints[:, 1, 0:chunks], a["dst_next"]),
                     (ends_i[:, 0, :], a["src"]),
                     (w_edge[0:4, :], a["W_edge"]), (w_edge[4:5, :], a["b_edge"]),
                     (w_node[0:C, 0, :], a["W_node"]), (w_node[C:C + 1, 0, :], a["b_node"]),
                     (w_src[:], a["W_msg"][0:C, :]), (w_dst[:], a["W_msg"][C:2 * C, :]),
                     (w_ef[0:C, :], a["W_msg"][2 * C:3 * C, :]), (b_msg[:], a["b_msg"]),
                     (w1[:], a["W1"]), (w2[:], a["W2"]), (gb[:], a["gb"])]
            loads += [(rowp[:, i, :], a[k].to_broadcast([P, C])) for i, k in enumerate(("b1", "b2", "prelu"))]
            all_loaded = 16 * len(loads)

            def all_halves(eng, step):
                def body(it):
                    for s in range(SLOTS):
                        step(s, it)
                rounds(eng, 2 * groups // SLOTS, body)
                for h in range(2 * groups // SLOTS * SLOTS, 2 * groups):
                    step(h % SLOTS, h // SLOTS)

            def in_all(s):
                return (2 * groups - s + SLOTS - 1) // SLOTS

            block = c1.enter_context(nc.Block())
            when = {}

            @block.vector
            def _(dve):
                V = nc.vector
                done = [0]

                def step(ins, name=None):
                    done[0] += 1
                    ins.then_inc(steps, 1)
                    dve.wait_ge(steps, done[0])
                    if name:
                        when[name] = done[0]

                dve.wait_ge(iotas, 4)
                step(V.memset(ea[:], 0.0))
                step(V.memset(hot_x[:], 0.0), "zeros")
                step(V.tensor_copy(part_f[:], part_i[:]))
                step(V.tensor_copy(base[:], base_i[:]))
                step(V.memset(ones[:], 1.0))
                step(V.memset(feat[C:C + 1, :], 1.0))
                step(V.memset(msg[:, :, CNT:CNT + 1], 1.0))
                step(V.memset(zeros[:], 0.0))
                step(V.tensor_copy(iota_f[:], iota_i))
                step(V.tensor_scalar(ident[:], iota_f[:], part_f[:, 0:1], None, ALU.is_equal))
                step(V.tensor_copy(w_node[0:C, 1, :], ident[0:C, 0:C]))
                step(V.tensor_scalar(pairs_i[:, 0:P], iota_i, 1, None, ALU.arith_shift_right))
                step(V.tensor_scalar(pairs_i[:, P:], part_i[:], 1, None, ALU.arith_shift_right))
                step(V.tensor_copy(same_pair[:], pairs_i))
                step(V.tensor_scalar(same_pair[:, 0:P], same_pair[:, 0:P], same_pair[:, P:P + 1], None, ALU.is_equal))
                dve.wait_ge(loaded, all_loaded)
                step(V.tensor_copy(msg[:, :, DST], ends_i[:, 1, :]))
                step(V.tensor_tensor(tiles_f[:, 0, :], ints[:, 1, 0:chunks], msg[:, :, DST], ALU.is_lt))
                step(V.tensor_reduce(bad[:, 1:2], tiles_f[:, 0, :], mybir.AxisListType.X, ALU.add))
                step(V.tensor_scalar(node_0[:], part_f[:], float(WINDOW), None, ALU.mult))
                step(V.tensor_copy(firsts, firsts_i))
                step(V.tensor_tensor(tiles_f[:, 0, :].rearrange("p (j u) -> p j u", u=2), msg[:, :, DST].rearrange("p (j u) -> p j u", u=2),
                                     wide(firsts, 2), ALU.subtract))
                step(V.tensor_scalar(tiles_f[:, 1, :], tiles_f[:, 0, :], 0.0, None, ALU.is_lt))
                step(V.tensor_scalar(tiles_f[:, 0, :], tiles_f[:, 0, :], float(WIN - 1), None, ALU.is_gt))
                step(V.tensor_tensor(tiles_f[:, 0, :], tiles_f[:, 0, :], tiles_f[:, 1, :], ALU.add))
                step(V.tensor_reduce(far[:], tiles_f[:, 0, :], mybir.AxisListType.X, ALU.add), "far")
                dve.wait_ge(p_far, 1)
                step(V.tensor_scalar(far[:], ps_s[:, 0:1], 1.0, None, ALU.min))
                step(V.tensor_copy(far_i[:], far[0:1, :]))
                step(V.tensor_scalar(ints[:, 0, 0:chunks], ends_i[:, 1, :], 7, 127, ALU.arith_shift_right, ALU.bitwise_and))
                step(V.tensor_scalar(ints[:, 1, 0:chunks], ends_i[:, 1, :], 14, None, ALU.arith_shift_right))
                step(V.tensor_copy(tiles_f[:], ints[:, :, 0:chunks]))
                step(V.tensor_copy(w_raw[:], w_ef[0:C, :]), "consts")

                def edge_stats(s, it):
                    dve.wait_ge(e_relu[s], it + 1)
                    V.bn_stats(st[:, bass.ds(it * SLOTS + s, 1), :].rearrange("p a k -> p (a k)"), h4[s]).then_inc(e_stat[s], 1)
                all_halves(dve, edge_stats)

                def scale_shift(k):
                    step(V.tensor_tensor(sc[:, k, 2:3], sc[:, k, 1:2], gb[:, 2 * k:2 * k + 1], ALU.mult))
                    step(V.tensor_tensor(sc[:, k, 0:1], mv[:, k, 0:1], sc[:, k, 2:3], ALU.mult))
                    step(V.tensor_tensor(sc[:, k, 3:4], gb[:, 2 * k + 1:2 * k + 2], sc[:, k, 0:1], ALU.subtract), f"shift{k}")

                for s in range(SLOTS):
                    dve.wait_ge(e_stat[s], in_all(s))
                step(V.bn_stats(st[:, 2 * groups - 1, :], h4[(2 * groups - 1) % SLOTS][:, 0:last_cols]), "e_stats")
                step(V.bn_aggr(mv[:, 0, :], st[:].rearrange("p a k -> p (a k)")))
                step(V.tensor_scalar(sc[:, 0, 0:1], mv[:, 0, 1:2], EPS, None, ALU.add))
                step(V.reciprocal(sc[:, 0, 0:1], sc[:, 0, 0:1]), "e_var")
                dve.wait_ge(root, 1)
                scale_shift(0)
                step(V.tensor_scalar(w_ef[0:C, :], w_raw[:], sc[:, 0, 2:3], None, ALU.mult))
                dve.wait_ge(p_shift, 1)
                step(V.tensor_tensor(w_ef[C:C + 1, :], ps_s[0:1, 0:C], b_msg[:], ALU.add), "w_ef")

                def messages(it):
                    first = peeled(it)
                    for s in range(2):
                        at = it * (2 * HALF) + s * HALF
                        if not first:
                            dve.wait_ge(counted[s], it)
                        V.tensor_tensor(hot_a[:, s], wide(tiles_f[:, 0, bass.ds(at, HALF)], P),
                                        rowwise(iota_f[:], HALF), ALU.is_equal).then_inc(hot_set[s], 1)
                        V.tensor_tensor(hot_b[:, s], wide(tiles_f[:, 1, bass.ds(at, HALF)], his),
                                        rowwise(iota_f[:, 0:his], HALF), ALU.is_equal).then_inc(hot_set[s], 1)
                        dve.wait_ge(turned[s], it * 2 + 2)
                        if not first or s:
                            dve.wait_ge(pre[1 - s], it + s)
                        V.tensor_copy(g_cols[:, 1, :], ps_t[1][0:C, :]).then_inc(dst_cols[s], 1)
                        if s == 0:
                            dve.wait_ge(dst_in, it * 16 + 16)
                            for j in range(2):
                                V.tensor_scalar(dst_rel[:, j * 2 * P:(j + 1) * 2 * P], dst_i[:, j * 2 * P:(j + 1) * 2 * P],
                                                firsts[:, bass.ds(it * 4 + 2 + j, 1)], node_0[:, 0:1],
                                                ALU.subtract, ALU.subtract).then_inc(rel_set, 1)
                            if not first:
                                dve.wait_ge(turned[1], it * 2)
                            dve.wait_ge(rel_set, it * 2 + 2)
                            for w in range(WINDOW):
                                V.tensor_scalar(hot_x[:, w, :], dst_rel, float(w), None, ALU.is_equal).then_inc(hot_x_set, 1)
                        dve.wait_ge(n_relu[s], it + 1)
                        V.bn_stats(st[:, bass.ds(it * 2 + s, 1), :].rearrange("p a k -> p (a k)"),
                                   h[:, s, :]).then_inc(n_stat[s], 1)
                rounds(dve, groups, messages)
                step(V.memset(m_full, full / n))
                step(V.memset(m_one, 1.0 / n))
                step(V.memset(pads, 0.0))
                step(V.memset(pads[:, :, DST:DST + 1], float(n_pad - 1)), "pads")
                step(V.tensor_scalar(before, iota_f[:], part_f[:, 0:1], None, ALU.is_gt))
                for s in range(2):
                    dve.wait_ge(n_stat[s], groups)
                step(V.bn_stats(st[:, 2 * groups - 1, :], h[:, 1, 0:last_cols]))
                step(V.bn_aggr(mv[:, 2, :], st[:].rearrange("p a k -> p (a k)")))

                dve.wait_ge(p_tab, 1)
                step(V.tensor_copy(tab[:, 0, :], ps_tab[:, 0:his]), "counts")
                dve.wait_ge(p_pairs, 1)
                step(V.tensor_scalar(tab[:, 1, :], ps_s[:, 0:his], float(WIN), None, ALU.is_gt))
                step(V.tensor_reduce(bad[:, 0:1], tab[:, 1, :], mybir.AxisListType.X, ALU.add))
                step(V.tensor_tensor(bad[:, 0:1], bad[:, 0:1], bad[:, 1:2], ALU.add), "bad")
                dve.wait_ge(p_before, 1)
                step(V.memset(tab[:, 2, :], 0.0))
                for b in range(1, his):
                    step(V.tensor_tensor(tab[:, 2, b:b + 1], tab[:, 2, b - 1:b], ps_s[:, 8 + b - 1:8 + b], ALU.add))
                step(V.tensor_tensor(tab[:, 3, :], tab[:, 2, :], ps_s[:, 0:his], ALU.add))
                step(V.tensor_scalar(bad[:, 0:1], ps_s[:, 16:17], 1.0, None, ALU.min))
                step(V.tensor_copy(flag_i[:], bad[0:1, 0:1]))
                for b in range(his):
                    step(V.tensor_scalar(tab[:, 4, b:b + 1], part_f[:], float(WIN // 2), float(area + b * P * WIN // 2), ALU.mult, ALU.add))
                step(V.tensor_tensor(tab[:, 5, :], tab[:, 4, :], tab[:, 3, :], ALU.subtract))
                step(V.scalar_tensor_tensor(tab[:, 6, :], tab[:, 5, :], bad[:, 0:1], tab[:, 3, :], ALU.mult, ALU.add))
                step(V.tensor_copy(tab_i[:, :, 2], tab[:, 6, :]))
                step(V.tensor_scalar(tab[:, 7, :], tab[:, 3, :], float(WIN - 1), None, ALU.add))
                step(V.tensor_copy(tab_i[:, :, 0], tab[:, 7, :]))
                step(V.tensor_scalar(tab_i[:, :, 1], tab_i[:, :, 0], 10, None, ALU.arith_shift_right))
                step(V.tensor_copy(tab[:, 8, :], tab_i[:, :, 1]))
                step(V.tensor_scalar(tab[:, 8, :], tab[:, 8, :], float(groups - 1), 16.0, ALU.min, ALU.mult))
                step(V.tensor_scalar(tab[:, 8, :], tab[:, 8, :], 16.0, None, ALU.add))
                step(V.tensor_copy(tab_i[:, :, 3], tab[:, 8, :]), "windows")

                for s in range(2):
                    dve.wait_ge(msg_set[s], groups)
                with dve.Fori(0, C) as c:
                    V.bn_stats(mst[:, bass.ds(c, 1), :].rearrange("p a k -> p (a k)"),
                               msg[:, 0:full, bass.ds(c, 1)].rearrange("p e a -> p (e a)")).then_inc(m_stat, 1)
                dve.wait_ge(m_stat, C)
                even, odd = (full + 1) // 2, full // 2
                step(V.tensor_scalar(mmv[:, 0, :], mst[:, :, 4], odd / full, None, ALU.mult))
                step(V.scalar_tensor_tensor(mmv[:, 0, :], mst[:, :, 1], even / full, mmv[:, 0, :], ALU.mult, ALU.add), "m_means")
                step(V.tensor_tensor(m_dev[:], mst[:, :, 1], mst[:, :, 4], ALU.subtract))
                step(V.tensor_tensor(m_dev[:], m_dev[:], m_dev[:], ALU.mult))
                step(V.tensor_tensor(mmv[:, 1, :], mst[:, :, 2], mst[:, :, 5], ALU.add))
                step(V.scalar_tensor_tensor(mmv[:, 1, :], m_dev[:], even * odd / full, mmv[:, 1, :], ALU.mult, ALU.add))
                step(V.tensor_scalar(mmv[:, 1, :], mmv[:, 1, :], 1.0 / full, None, ALU.mult))
                step(V.tensor_copy(m_dev[:], mmv[:, 0, :]))
                dve.wait_ge(p_mean, 1)
                step(V.tensor_tensor(m_dev[:], m_dev[:], ps_p[0][:, 0:C], ALU.subtract))
                step(V.tensor_tensor(m_dev[:], m_dev[:], m_dev[:], ALU.mult))
                step(V.tensor_tensor(m_dev[:], m_dev[:], mmv[:, 1, :], ALU.add))
                step(V.tensor_tensor(m_tail[0:rest, :], msg[0:rest, full, 0:C], ps_p[0][0:rest, 0:C], ALU.subtract))
                step(V.tensor_tensor(m_tail[0:rest, :], m_tail[0:rest, :], m_tail[0:rest, :], ALU.mult), "m_devs")
                dve.wait_ge(p_var, 1)
                step(V.tensor_copy(mv[:, 1, 0:1], ps_p[1][0:C, 0:1]))
                step(V.tensor_copy(mv[:, 1, 1:2], ps_p[1][0:C, 2:3]))
                step(V.tensor_scalar(sc[:, 1:3, 0], mv[:, 1:3, 1], EPS, None, ALU.add))
                step(V.reciprocal(sc[:, 1:3, 0], sc[:, 1:3, 0]), "mn_var")
                dve.wait_ge(root, 2)
                scale_shift(1)
                scale_shift(2)
                for i, (k, w) in enumerate(((2, 2), (1, 2), (1, 3), (2, 3))):
                    step(V.tensor_scalar(diag[:, i, :], ident[0:C, 0:C], sc[:, k, w:w + 1], None, ALU.mult), "diags")
                dve.wait_ge(p_rows, 1)
                step(V.tensor_copy(rowp[:, 3:6, :], ps_s[:, 0:3 * C].rearrange("p (k c) -> p k c", k=3)))
                step(V.tensor_copy(w_node[C:C + 1, 1, :], ps_s[C:C + 1, 3 * C:4 * C]))

            @block.sync
            def _(sp):
                sp.wait_ge(iotas, 4)
                for to, of in loads:
                    sp.dma_start(to, of).then_inc(loaded, 16)

                sp.wait_ge(steps, when["zeros"])

                def edge_stats(s, it):
                    at = it * (SLOTS * COLS) + s * COLS
                    if not peeled(it):
                        at = sp.snap(at)
                    if later(it):
                        sp.wait_ge(ea_used[s], it)
                    sp.dma_start(ea4[s][0:5, :], a["eaT"][:, bass.ds(at, COLS)]).then_inc(ea_in[s], 16)
                all_halves(sp, edge_stats)

                def messages(it):
                    at = [it * (2 * COLS) + s * COLS if peeled(it) else sp.snap(it * (2 * COLS) + s * COLS) for s in range(2)]
                    lows = [sp.value_load(firsts_i[0:1, bass.ds(it * 4 + 2 + j, 1)], min_val=0, max_val=n_pad - 1) for j in range(2)]
                    if not peeled(it):
                        sp.wait_ge(hot_x_set, it * WINDOW)
                    sp.dma_start(dst_i[:], a["dst_row"][:, bass.ds(at[1], COLS)].to_broadcast([P, COLS])).then_inc(dst_in, 16)
                    for s in range(2):
                        if peeled(it):
                            sp.wait_ge(ea_used[s], in_all(s))
                        else:
                            sp.wait_ge(e_layer[s], it)
                            sp.sem_inc(sp_passed, 1)
                        sp.dma_start(ea[0:5, s, :], a["eaT"][:, bass.ds(at[s], COLS)]).then_inc(mea_in[s], 16)
                        if not peeled(it):
                            sp.wait_ge(n_layer[s], it)
                        sp.dma_start(xc[:, s, :], a["xT"][:, bass.ds(at[s], COLS)]).then_inc(xc_in[s], 16)
                    if not peeled(it):
                        sp.wait_ge(turned[1], it * 2)
                    for j, low in enumerate(lows):
                        sp.dma_start(x_win[:, j], a["x"][bass.ds(low, WIN), :].rearrange("(p w) c -> p w c", w=WINDOW)).then_inc(x_win_in, 16)
                rounds(sp, groups, messages)
            @block.gpsimd
            def _(pool):
                nc.gpsimd.memset(w_edge[:], 0.0).then_inc(iotas, 1)
                nc.gpsimd.iota(iota_i, [[1, P]], base=0, channel_multiplier=0).then_inc(iotas, 1)
                nc.gpsimd.iota(part_i[:], [[0, 1]], base=0, channel_multiplier=1).then_inc(iotas, 1)
                nc.gpsimd.iota(base_i[:], [[COLS, 2 * groups]], base=0, channel_multiplier=0).then_inc(iotas, 1)
                pool.wait_ge(steps, when["consts"])

                def indices(it, s):
                    nc.gpsimd.tensor_copy(idx[:, s], ends_i[:, :, bass.ds(it * (2 * HALF) + s * HALF, HALF)]).then_inc(copied[s], 1)

                is_far = pool.value_load(far_i[0:1, 0:1], min_val=0, max_val=1)

                def gather(s, w, signal):
                    for u in range(HALF):
                        nc.gpsimd.indirect_dma_start(
                            g_rows[:, s, w, u, :], None, a["x"],
                            bass.IndirectOffsetOnAxis(idx[:, s, w, u:u + 1], axis=0),
                        ).then_inc(signal, 16)

                def wait(it, signal, value):
                    pool.wait_ge(signal, value)
                    if not peeled(it):
                        pool.sem_inc(passed, 1)

                def gathers(it, last=False):
                    for s in range(2):
                        if later(it):
                            pool.wait_ge(turned[s], it * 2 - 1)
                        wait(it, copied[s], it + 1)
                        gather(s, 0, gathered[s])
                        if not (last and s):
                            if s:
                                wait(it, gathered[0], it * (16 * 2 * HALF) + 16 * 2 * HALF)
                            elif later(it):
                                wait(it, gathered[1], it * (16 * HALF))
                                with pool.If(is_far == 1):
                                    wait(it, gathered_far, it * (16 * HALF))
                            indices(it + s, 1 - s)
                        if s:
                            with pool.If(is_far == 1):
                                if later(it):
                                    wait(it, turned[1], it * 2)
                                gather(1, 1, gathered_far)
                        else:
                            if later(it):
                                wait(it, turned[0], it * 2)
                            gather(0, 1, gathered[0])
                indices(0, 0)
                rounds(pool, groups - 1, gathers)
                gathers(groups - 1, last=True)

            @block.tensor
            def _(pe):
                T = nc.tensor
                pe.wait_ge(steps, when["far"])
                T.matmul(ps_s[:, 0:1], ones[:], far[:], start=True, stop=True).then_inc(p_far, 1)
                pe.wait_ge(steps, when["consts"])
                is_far = pe.value_load(far_i[0:1, 0:1], min_val=0, max_val=1)

                ps_e = [*ps_f, *ps_p]

                def edge_stats(s, it):
                    pe.wait_ge(ea_in[s], it * 16 + 16)
                    if later(it):
                        pe.wait_ge(e_relu[s], it)
                    T.matmul(ps_e[s][0:C, :], w_edge[:], ea4[s], start=True, stop=True).then_inc(ea_used[s], 1)
                all_halves(pe, edge_stats)

                pe.wait_ge(steps, when["shift0"])
                T.matmul(ps_s[0:1, 0:C], sc[:, 0, 3:4], w_raw[:], start=True, stop=True).then_inc(p_shift, 1)

                def turn_dst(s):
                    for u in range(HALF):
                        last = T.transpose(ps_t[1][0:C, u * P:(u + 1) * P], g_rows[:, s, 1, u, :], ident[:])
                    last.then_inc(turned[s], 1)

                def messages(it):
                    first = peeled(it)
                    for s in range(2):
                        pe.wait_ge(gathered[s], (it + 1) * (16 * HALF) if s else (it + 1) * (16 * 2 * HALF))
                        if not first or s:
                            pe.wait_ge(src_cols[1 - s], it + s)
                        for u in range(HALF):
                            last = T.transpose(ps_t[0][0:C, u * P:(u + 1) * P], g_rows[:, s, 0, u, :], ident[:])
                        last.then_inc(turned[s], 1)
                        if not first or s:
                            pe.wait_ge(dst_cols[1 - s], it + s)
                        if s == 0:
                            turn_dst(0)
                        else:
                            pe.wait_ge(x_win_in, it * 32 + 32)
                            pe.wait_ge(hot_x_set, it * WINDOW + WINDOW)
                            with pe.If(is_far == 1):
                                pe.wait_ge(gathered_far, (it + 1) * (16 * HALF))
                                turn_dst(1)
                            with pe.If(is_far == 0):
                                for j in range(2):
                                    for w in range(WINDOW):
                                        last = T.matmul(ps_t[1][0:C, j * 2 * P:(j + 1) * 2 * P], x_win[:, j, w, :],
                                                        hot_x[:, w, j * 2 * P:(j + 1) * 2 * P], start=(w == 0), stop=(w == WINDOW - 1))
                                last.then_inc(turned[1], 1)
                        pe.wait_ge(mea_in[s], it * 16 + 16)
                        if first and s == 0:
                            pe.wait_ge(e_relu[0], in_all(0))
                        else:
                            pe.wait_ge(feat_set[1 - s], it + s)
                        T.matmul(ps_f[0][0:C, :], w_edge[:], ea[:, s, :], start=True, stop=True).then_inc(e_layer[s], 1)
                        pe.wait_ge(xc_in[s], it * 16 + 16)
                        if first and s == 0:
                            pe.wait_ge(e_relu[1], in_all(1))
                        else:
                            pe.wait_ge(n_relu[1 - s], it + s)
                        T.matmul(ps_f[1][0:C, :], w_node[:, 0, :], xc[:, s, :], start=True, stop=True).then_inc(n_layer[s], 1)
                        pe.wait_ge(hot_set[s], it * 2 + 2)
                        for u in range(HALF):
                            last = T.matmul(ps_tab[:, 0:his], hot_a[:, s, u, :], hot_b[:, s, u, :],
                                            start=(first and s == 0 and u == 0), stop=False)
                        last.then_inc(counted[s], 1)
                        pe.wait_ge(src_cols[s], it + 1)
                        pe.wait_ge(dst_cols[s], it + 1)
                        pe.wait_ge(feat_set[s], it + 1)
                        if first and s == 0:
                            pe.wait_ge(steps, when["w_ef"])
                        if first:
                            pe.wait_ge(e_relu[2 + s], in_all(2 + s))
                        else:
                            pe.wait_ge(msg_set[s], it)
                        for u in range(HALF):
                            o = ps_p[s][:, u * C:(u + 1) * C]
                            e = slice(u * P, (u + 1) * P)
                            T.matmul(o, g_cols[:, 0, e], w_src[:], start=True, stop=False)
                            T.matmul(o, g_cols[:, 1, e], w_dst[:], start=False, stop=False)
                            last = T.matmul(o, feat[:, e], w_ef[:], start=False, stop=True)
                        last.then_inc(pre[s], 1)
                rounds(pe, groups, messages)
                T.matmul(ps_tab[:, 0:his], zeros[:], zeros[:, 0:his], start=False, stop=True).then_inc(p_tab, 1)
                pe.wait_ge(steps, when["counts"])
                T.matmul(ps_s[:, 0:his], same_pair[:, 0:P], tab[:, 0, :], start=True, stop=True).then_inc(p_pairs, 1)
                pe.wait_ge(steps, when["bad"])
                T.matmul(ps_s[:, 0:his], before, tab[:, 0, :], start=True, stop=True)
                T.matmul(ps_s[:, 8:8 + his], ones[:], tab[:, 0, :], start=True, stop=True)
                T.matmul(ps_s[:, 16:17], ones[:], bad[:, 0:1], start=True, stop=True).then_inc(p_before, 1)
                pe.wait_ge(steps, when["m_means"])
                for s in range(2):
                    pe.wait_ge(msg_set[s], groups)
                T.matmul(ps_p[0][:, 0:C], m_full, mmv[:, 0, :], start=True, stop=False)
                T.matmul(ps_p[0][:, 0:C], m_one[0:rest, :], msg[0:rest, full, 0:C], start=False, stop=True)
                T.matmul(ps_p[1][0:C, 0:1], mmv[:, 0, :], m_full[:, 0:1], start=True, stop=False)
                T.matmul(ps_p[1][0:C, 0:1], msg[0:rest, full, 0:C], m_one[0:rest, 0:1], start=False, stop=True).then_inc(p_mean, 1)
                pe.wait_ge(steps, when["m_devs"])
                T.matmul(ps_p[1][0:C, 2:3], m_dev[:], m_full[:, 0:1], start=True, stop=False)
                T.matmul(ps_p[1][0:C, 2:3], m_tail[0:rest, :], m_one[0:rest, 0:1], start=False, stop=True).then_inc(p_var, 1)
                pe.wait_ge(steps, when["diags"])
                T.matmul(ps_s[:, 0:4 * C], ones[0:C, :], diag.rearrange("p k c -> p (k c)"), start=True, stop=True).then_inc(p_rows, 1)

            @block.scalar
            def _(act):
                ps_e = [*ps_f, *ps_p]

                def edge_stats(s, it):
                    act.wait_ge(ea_used[s], it + 1)
                    if later(it):
                        act.wait_ge(e_stat[s], it)
                    nc.scalar.activation(h4[s], ps_e[s][0:C, :], ACT.Relu).then_inc(e_relu[s], 1)
                all_halves(act, edge_stats)
                act.wait_ge(steps, when["e_var"])
                nc.scalar.activation(sc[:, 0, 1:2], sc[:, 0, 0:1], ACT.Sqrt).then_inc(root, 1)

                def messages(it):
                    first = peeled(it)
                    for s in range(2):
                        act.wait_ge(turned[s], it * 2 + 1)
                        if not first or s:
                            act.wait_ge(pre[1 - s], it + s)
                        nc.scalar.copy(g_cols[:, 0, :], ps_t[0][0:C, :]).then_inc(src_cols[s], 1)
                        act.wait_ge(e_layer[s], it + 1)
                        nc.scalar.activation(feat[0:C, :], ps_f[0][0:C, :], ACT.Relu).then_inc(feat_set[s], 1)
                        act.wait_ge(n_layer[s], it + 1)
                        if first:
                            act.wait_ge(steps, when["e_stats"])
                        else:
                            act.wait_ge(n_stat[s], it)
                        nc.scalar.activation(h[:, s, :], ps_f[1][0:C, :], ACT.Relu).then_inc(n_relu[s], 1)
                        act.wait_ge(pre[s], it + 1)
                        nc.scalar.activation(
                            msg[:, bass.ds(it * (2 * HALF) + s * HALF, HALF), 0:C],
                            ps_p[s][:, 0:HALF * C].rearrange("p (u c) -> p u c", u=HALF), ACT.Relu).then_inc(msg_set[s], 1)
                    for s in range(2):
                        act.wait_ge(msg_set[s], it + 1)
                    act.dma_start(rows[bass.ds(it * (2 * COLS), 2 * COLS), :].rearrange("(u p) c -> p u c", p=P),
                                  msg[:, bass.ds(it * (2 * HALF), 2 * HALF), :]).then_inc(stored, 16)
                rounds(act, groups, messages)
                act.wait_ge(steps, when["pads"])
                act.dma_start(rows[n_pad:area, :].rearrange("(p w) c -> p w c", w=WINDOW), pads).then_inc(stored, 16)
                act.wait_ge(steps, when["windows"])
                with nc.allow_non_contiguous_dma(reason="a table of some hundred words"):
                    act.dma_start(lo_tab.rearrange("(b p) k -> p b k", p=P), tab_i[:, :, 2:4]).then_inc(stored, 16)
                act.wait_ge(stored, 16 * (groups + 2))
                act.dma_start(lo_i, lo_tab.rearrange("(o t) k -> o (t k)", o=1)).then_inc(stored, 16)
                act.wait_ge(steps, when["mn_var"])
                nc.scalar.activation(sc[:, 1:3, 1], sc[:, 1:3, 0], ACT.Sqrt).then_inc(root, 1)
                act.wait_ge(stored, 16 * (groups + 3))

        for layer in range(3):
            with ExitStack() as c2:
                node_layer(nc, maker(c2, f"l{layer}_"), *semaphores(c2, f"l{layer}_"), c2, layer, groups, chunks,
                           a, out, rows, area, z_tab, x1_tab, bank, iota_f, part_f, ident, base, ends_i, lo_i,
                           pool_sems.get(layer), flag_i, w_node, (w1, w2), rowp, dinv)


def before(s, it, steps):
    q = s - steps
    return q % SLOTS, it + q // SLOTS


def node_layer(nc, sb, sem, pair, ctx, layer, groups, chunks, a, out, rows, area, z_tab, x1_tab, bank, iota_f,
               part_f, ident, base, ends_i, lo_i, pool_sems, flag_i, w_node, w_conv, rowp, dinv):
    n_pad = chunks * P
    halves = 2 * groups
    assert halves % SLOTS
    slope, node_scale, msg_scale, msg_shift = (rowp[:, i, :] for i in range(2, 6))
    width = C if layer else C + 1
    slots = 3
    has_z = layer < 2
    has_ln = layer != 1
    turn_lag = 4 if has_ln else 2
    last_lag = 4 if layer == 0 else 3 if has_ln else 2
    win = sb("win", [P, SLOTS, 2, WINDOW, R])
    hot = sb("hot", [P, SLOTS, 2 * WINDOW, 2, P])
    numbers = sb("numbers", [P, 2, WINDOW, 2, P])
    acc = sb("acc", [P, SLOTS, 3, HALF, C])
    if layer == 0:
        deg = sb("deg", [P, SLOTS, HALF])
        xc = sb("xc", [C + 1, SLOTS, COLS])
    else:
        zr = sb("zr", [P, SLOTS, HALF, C])
        g_rows = sb("g_rows", [P, slots, 2 * HALF, C])
        idx = sb("idx", [P, slots, 2 * HALF], I32)
    if has_ln:
        xr = sb("xr", [P, SLOTS, HALF, C])
        ln = sb("ln", [P, SLOTS, HALF, 6])
        mv = sb("mv", [P, SLOTS, 5, HALF])
        dev = sb("dev", [P, SLOTS, 2, HALF])
        inv = sb("inv", [P, SLOTS, HALF])
        offsets = sb("offsets", [P, 2])
        lift = sb("lift", [P, SLOTS, HALF])
        o_rows = sb("o_rows", [P, SLOTS, HALF, C])
    if has_z:
        o_cols = sb("o_cols", [C, COLS])
        z_out = sb("z_out", [P, SLOTS, HALF, C])
    big = sb("big", [P, 2 * HALF, R])
    sums = sb("sums", [P, WINDOW, R])
    first_node = sb("first_node", [P, 1])

    def each(name):
        return pair(name, SLOTS)

    win_in, z_in, res_in, xc_in = each("win_in"), each("z_in"), each("res_in"), each("xc_in")
    hot_set, summed, own_x, shifts = (each(k) for k in ("hot_set", "summed", "own_x", "shifts"))
    own_relu, own_scaled, own_set = each("own_relu"), each("own_scaled"), each("own_set")
    y1, y2, y3, y4, deg_set, y_set = (each(k) for k in ("y1", "y2", "y3", "y4", "deg_set", "y_set"))
    ln_set, mv_set, var_set, roots = (each(k) for k in ("ln_set", "mv_set", "var_set", "roots"))
    deg_root, rstd_set = each("deg_root"), each("rstd_set")
    lifted, o_set, turned, cols_set, z_ps, z_set = (each(k) for k in ("lifted", "o_set", "turned", "cols_set", "z_ps", "z_set"))
    o_out, z_st, dinv_set = each("o_out"), each("z_st"), each("dinv_set")
    idx_set = [sem(f"idx_set{i}") for i in range(slots)]
    passed, act_passed, numbered = sem("passed"), sem("act_passed"), sem("numbered")
    big_in, big_hot, big_sum, big_acc, big_zero, big_key, big_out = (
        sem(k) for k in ("big_in", "big_hot", "big_sum", "big_acc", "big_zero", "big_key", "big_out"))
    if layer:
        gathered, rows_in = pool_sems[0:slots], pool_sems[slots]

    ps_a, ps_own, ps_t, ps_z = bank[0:2], (bank[2:4], bank[4:6]), bank[6], bank[7]
    z_of = z_tab[layer - 1] if layer else None
    z_to = z_tab[layer] if has_z else None

    block = ctx.enter_context(nc.Block())

    def tiles_of(table, at):
        return table[bass.ds(at, COLS), :].rearrange("(j p t) c -> p j (t c)", p=P, t=2)

    def by_pair(rows_of):
        return rows_of.rearrange("p (j t) c -> p j (t c)", t=2)

    def own_part(s, j, part):
        return ps_own[j][s % 2][:, 0:4 * C].rearrange("p (t k c) -> p t k c", t=2, k=2)[:, :, part, :]

    def tile(s, k):
        return k * (SLOTS * HALF) + s * HALF

    def exists(half):
        s, k = half
        return not peeled(k) or 0 <= k * SLOTS + s < halves

    def all_steps(eng, step, more=0):
        def body(it):
            for s in range(SLOTS):
                step(s, it)
        rounds(eng, halves // SLOTS, body, ahead=2)
        for h in range(halves // SLOTS * SLOTS, halves + more):
            step(h % SLOTS, h // SLOTS)

    def all_of(eng, signal, times):
        for s in range(SLOTS):
            eng.wait_ge(signal[s], times * ((halves - s + SLOTS - 1) // SLOTS))

    if layer:
        @block.gpsimd
        def _(pool):
            def indices(it, s):
                nc.gpsimd.tensor_copy(idx[:, s], ends_i[:, 0, bass.ds(it * (slots * 2 * HALF) + s * 2 * HALF, 2 * HALF)]).then_inc(idx_set[s], 1)

            def store(it, s):
                pool.wait_ge(gathered[s], it * (16 * 2 * HALF) + 16 * 2 * HALF)
                if later(it) or s:
                    pool.wait_ge(rows_in, it * (16 * slots) + 16 * s)
                pool.dma_start(rows[bass.ds(it * (slots * 2 * COLS) + s * 2 * COLS, 2 * COLS), 0:C].rearrange("(u p) c -> p u c", p=P),
                               g_rows[:, s]).then_inc(rows_in, 16)

            def group(it, s, last=False):
                if not last:
                    indices(it + 1 if s == slots - 1 else it, (s + 1) % slots)
                pool.wait_ge(idx_set[s], it + 1)
                if not peeled(it):
                    pool.sem_inc(passed, 1)
                for u in range(2 * HALF):
                    nc.gpsimd.indirect_dma_start(
                        g_rows[:, s, u, :], None, z_of, bass.IndirectOffsetOnAxis(idx[:, s, u:u + 1], axis=0),
                    ).then_inc(gathered[s], 16)
                if s:
                    store(it, s - 1)
                elif later(it):
                    store(it - 1, slots - 1)

            def three(it):
                for s in range(slots):
                    group(it, s)
            indices(0, 0)
            whole = (groups - 1) // slots
            rounds(pool, whole, three)
            for s in range(groups - whole * slots):
                group(whole, s, last=s == groups - whole * slots - 1)
            store(whole, groups - whole * slots - 1)
    else:
        @block.gpsimd
        def _(pool):
            def own_rows(s, k):
                A = acc[:, s]
                pool.wait_ge(own_relu[s], k * 2 + 2)
                if later(k):
                    pool.wait_ge(y_set[s], k)
                nc.gpsimd.tensor_tensor(A[:, 1], A[:, 0], rowwise(node_scale, HALF), ALU.mult).then_inc(own_scaled[s], 1)
                pool.wait_ge(deg_set[s], k + 1)
                nc.gpsimd.tensor_tensor(xr[:, s], wide(deg[:, s], C), rowwise(msg_shift, HALF), ALU.mult).then_inc(shifts[s], 1)
                pool.wait_ge(own_scaled[s], k + 1)
                pool.wait_ge(shifts[s], k + 1)
                nc.gpsimd.tensor_tensor(A[:, 1], A[:, 1], xr[:, s], ALU.add).then_inc(own_set[s], 1)

            all_steps(pool, own_rows)

    @block.sync
    def _(sp):
        flag = sp.value_load(flag_i[0:1, 0:1], min_val=0, max_val=1)
        with sp.If(flag == 1):
            if layer:
                sp.wait_ge(rows_in, 16 * groups)
            with sp.Fori(0, chunks // 2) as t:
                with sp.Fori(0, groups) as k:
                    free = sp.snap(t * groups + k + 1)
                    at = sp.snap(k * (2 * COLS))
                    sp.wait_ge(big_acc, free)
                    sp.dma_start(big[:], rows[bass.ds(at, 2 * COLS), :].rearrange("(p u) c -> p u c", p=P)).then_inc(big_in, 16)
                summed_all = sp.snap(t * groups + (groups + 1))
                to = sp.snap(t * WIN + area)
                sp.wait_ge(big_acc, summed_all)
                sp.dma_start(rows[bass.ds(to, WIN), :].rearrange("(p w) c -> p w c", w=WINDOW), sums[:]).then_inc(big_out, 16)
            sp.wait_ge(big_out, 16 * (chunks // 2))

        def loads(s, it):
            at = tile(s, it) * P
            used = it
            if not peeled(it):
                at, used = sp.snap(at), sp.snap(used)
            entry = [(tile(s, it) + 2 * j) * 2 for j in range(2)]
            lows = [sp.value_load(lo_i[0:1, bass.ds(e, 1)], min_val=0, max_val=area + (chunks // 2 - 1) * WIN) for e in entry]
            if layer:
                need = sp.value_load(lo_i[0:1, bass.ds(entry[1] + 1, 1)], min_val=16, max_val=16 * groups)
            if later(it):
                sp.wait_ge(summed[s], used)
            if layer:
                sp.wait_ge(rows_in, need)
            for j, low in enumerate(lows):
                sp.dma_start(win[:, s, j], rows[bass.ds(low, WIN), :].rearrange("(p w) c -> p w c", w=WINDOW)).then_inc(win_in[s], 16)
            if layer == 0:
                if later(it):
                    sp.wait_ge(own_x[s], used)
                sp.dma_start(xc[:, s, :], a["xT"][:, bass.ds(at, COLS)]).then_inc(xc_in[s], 16)
            else:
                sp.dma_start(by_pair(zr[:, s]), tiles_of(z_of, at)).then_inc(z_in[s], 16)
            if layer == 2:
                if later(it):
                    sp.wait_ge(y_set[s], used)
                sp.dma_start(by_pair(xr[:, s]), tiles_of(x1_tab, at)).then_inc(res_in[s], 16)
        all_steps(sp, loads)

    @block.vector
    def _(dve):
        V = nc.vector
        for v in range(2):
            V.tensor_scalar(numbers[:, 0, 0, v], iota_f[:], 2.0, float(v), ALU.mult, ALU.add).then_inc(numbered, 1)
        dve.wait_ge(numbered, 2)
        for w in range(1, WINDOW):
            V.tensor_copy(numbers[:, 0, w], numbers[:, 0, 0]).then_inc(numbered, 1)
        for w in range(WINDOW):
            V.tensor_scalar(numbers[:, 1, w], numbers[:, 0, 0], 2.0 * P, None, ALU.add).then_inc(numbered, 1)
        dve.wait_ge(numbered, 2 * WINDOW + 1)
        if has_ln:
            V.memset(offsets[:, 0:1], EPS).then_inc(numbered, 1)
            V.memset(offsets[:, 1:2], 1.0).then_inc(numbered, 1)
        flag = dve.value_load(flag_i[0:1, 0:1], min_val=0, max_val=1)
        with dve.If(flag == 1):
            every = hot[:].rearrange("p s w t m -> p (s w t m)")[:, 0:4 * HALF * P].rearrange("p (u t m) -> p u t m", t=2, m=P)
            V.memset(sums[:], 0.0).then_inc(big_zero, 1)
            V.memset(first_node[:], -2.0 * P).then_inc(big_zero, 1)
            dve.wait_ge(big_zero, 2)
            V.memset(sums[:, 2, DST:DST + 1], float(n_pad - 1)).then_inc(big_zero, 1)
            dve.wait_ge(big_zero, 3)
            V.memset(sums[:, 0, 0:1], 0.0).then_inc(big_acc, 1)
            with dve.Fori(0, chunks // 2) as t:
                dve.wait_ge(big_acc, t * groups + 1)
                V.tensor_scalar(first_node[:], first_node[:], 2.0 * P, None, ALU.add).then_inc(big_zero, 1)
                V.memset(sums[:, 0:2, 0:DST], 0.0).then_inc(big_zero, 1)
                dve.wait_ge(big_zero, t * 4 + 5)
                for v in range(2):
                    V.tensor_scalar(sums[:, v, DST:DST + 1], part_f[:], 2.0, float(v), ALU.mult, ALU.add).then_inc(big_zero, 1)
                dve.wait_ge(big_zero, t * 4 + 7)
                V.tensor_scalar(sums[:, 0:2, DST], sums[:, 0:2, DST], first_node[:, 0:1], None, ALU.add).then_inc(big_key, 1)
                with dve.Fori(0, groups) as k:
                    dve.wait_ge(big_key, t + 1)
                    dve.wait_ge(big_in, t * (16 * groups) + k * 16 + 16)
                    V.scalar_tensor_tensor(every.rearrange("p u t m -> p u (t m)"), wide(big[:, :, DST], 2 * P), first_node[:, 0:1],
                                           rowwise(numbers[:, 0, 0].rearrange("p t m -> p (t m)"), 2 * HALF),
                                           ALU.subtract, ALU.is_equal).then_inc(big_hot, 1)
                    dve.wait_ge(big_sum, t * groups + k + 1)
                    V.tensor_tensor(sums[:, 0:2, 0:DST], sums[:, 0:2, 0:DST],
                                    ps_a[0][:, 0:2 * DST].rearrange("p (t c) -> p t c", t=2), ALU.add).then_inc(big_acc, 1)
                    dve.wait_ge(big_acc, t * groups + k + 2)
                dve.wait_ge(big_out, t * 16 + 16)

        def one_hots(j, s, k):
            if later(k):
                dve.wait_ge(summed[s], k)
            dve.wait_ge(win_in[s], k * 32 + 32)
            V.scalar_tensor_tensor(hot[:, s, j * WINDOW:(j + 1) * WINDOW].rearrange("p w t m -> p w (t m)"),
                                   wide(win[:, s, j, :, DST], 2 * P),
                                   base[:, bass.ds(k * SLOTS + s, 1)], numbers[:, j].rearrange("p w t m -> p w (t m)"),
                                   ALU.subtract, ALU.is_equal).then_inc(hot_set[s], 1)

        def norm_1(s, k):
            dve.wait_ge(ln_set[s], k * HALF + HALF)
            V.tensor_tensor(mv[:, s, 0], ln[:, s, :, 1], ln[:, s, :, 4], ALU.add).then_inc(mv_set[s], 1)
            V.tensor_tensor(mv[:, s, 1], ln[:, s, :, 1], ln[:, s, :, 4], ALU.subtract).then_inc(mv_set[s], 1)
            V.tensor_tensor(mv[:, s, 2], ln[:, s, :, 2], ln[:, s, :, 5], ALU.add).then_inc(mv_set[s], 1)

        def norm_2(s, k):
            dve.wait_ge(mv_set[s], k * 4 + 3)
            V.scalar_tensor_tensor(mv[:, s, 3], mv[:, s, 1], 0.25, mv[:, s, 1], ALU.mult, ALU.mult).then_inc(mv_set[s], 1)

        def norm_3(s, k):
            if later(k):
                dve.wait_ge(roots[s], k)
            dve.wait_ge(mv_set[s], k * 4 + 4)
            V.scalar_tensor_tensor(mv[:, s, 4], mv[:, s, 2], 1.0 / C, mv[:, s, 3], ALU.mult, ALU.add).then_inc(var_set[s], 1)

        def norm_4(s, k):
            if later(k):
                dve.wait_ge(o_set[s], k * HALF)
            dve.wait_ge(roots[s], k + 1)
            V.reciprocal(inv[:, s], dev[:, s, 0]).then_inc(rstd_set[s], 1)
            if layer == 0:
                dve.wait_ge(deg_root[s], k + 1)
                V.reciprocal(dinv[:, bass.ds(tile(s, k), HALF)], dev[:, s, 1]).then_inc(dinv_set[s], 1)

        def norm_5(s, k):
            dve.wait_ge(rstd_set[s], k + 1)
            V.scalar_tensor_tensor(lift[:, s], mv[:, s, 0], -0.5, inv[:, s], ALU.mult, ALU.mult).then_inc(lifted[s], 1)

        def statistics(s, k, y):
            dve.wait_ge(y_set[s], k + 1)
            for u in range(HALF):
                V.bn_stats(ln[:, s, u], y[:, u]).then_inc(ln_set[s], 1)

        def scale_sums(s, k):
            if later(k):
                dve.wait_ge(o_set[s], k * HALF)
            dve.wait_ge(deg_set[s], k + 1)
            sums_of = ps_a[s % 2][:, 0:HALF * (C + 1)].rearrange("p (t c) -> p t c", t=HALF)
            V.tensor_tensor(acc[:, s, 2], sums_of[:, :, 0:C], rowwise(msg_scale, HALF), ALU.mult).then_inc(y1[s], 1)

        def add_x(s, k):
            dve.wait_ge(own_relu[s], k * 2 + 2)
            dve.wait_ge(y1[s], k + 1)
            for j in range(2):
                two_tiles = acc[:, s, 2, 2 * j:2 * j + 2]
                V.tensor_tensor(two_tiles, own_part(s, j, 1), two_tiles, ALU.add).then_inc(y2[s], 1)

        def add_rest(s, k):
            dve.wait_ge(own_set[s], k + 1)
            dve.wait_ge(y2[s], k * 2 + 2)
            V.tensor_tensor(acc[:, s, 2], acc[:, s, 2], acc[:, s, 1], ALU.add).then_inc(y_set[s], 1)

        def add_bias(s, k):
            dve.wait_ge(y1[s], k * HALF + HALF)
            V.tensor_tensor(acc[:, s, 0], acc[:, s, 0], rowwise(rowp[:, layer - 1, :], HALF), ALU.add).then_inc(y2[s], 1)

        def negative_part(s, k):
            if layer == 2 and later(k):
                dve.wait_ge(o_set[s], k * HALF)
            dve.wait_ge(y2[s], k + 1)
            V.scalar_tensor_tensor(acc[:, s, 1], acc[:, s, 0], 0.0, rowwise(slope, HALF), ALU.min, ALU.mult).then_inc(y3[s], 1)

        def add_positive_part(s, k):
            if layer == 1 and later(k):
                dve.wait_ge(turned[s], k)
            dve.wait_ge(y3[s], k + 1)
            V.scalar_tensor_tensor(acc[:, s, 2], acc[:, s, 0], 0.0, acc[:, s, 1], ALU.max, ALU.add).then_inc(y4[s], 1)

        def add_residual(s, k):
            dve.wait_ge(res_in[s], k * 16 + 16)
            dve.wait_ge(y4[s], k + 1)
            V.tensor_tensor(acc[:, s, 1], acc[:, s, 2], xr[:, s], ALU.add).then_inc(y_set[s], 1)

        def step(s, it):
            following, one, two = (before(s, it, j) for j in (-1, 1, 2))
            has_one, has_two, has_following = exists(one), has_ln and exists(two), exists(following)
            if has_two:
                norm_1(*two)
            if has_one:
                if layer:
                    add_bias(*one)
                else:
                    scale_sums(*one)
            if has_following:
                one_hots(0, *following)
            if has_two:
                norm_2(*two)
            if has_one:
                if layer:
                    negative_part(*one)
                else:
                    add_x(*one)
            if has_following:
                one_hots(1, *following)
            if has_two:
                norm_3(*two)
            if has_one:
                if layer:
                    add_positive_part(*one)
                else:
                    add_rest(*one)
            if has_two:
                norm_4(*two)
            if has_one and layer == 2:
                add_residual(*one)
            if has_one and has_ln:
                statistics(*one, acc[:, one[0], 1 if layer else 2])
            if has_two:
                norm_5(*two)
        for j in range(2):
            one_hots(j, 0, 0)
        all_steps(dve, step, last_lag)

    @block.tensor
    def _(pe):
        T = nc.tensor
        flag = pe.value_load(flag_i[0:1, 0:1], min_val=0, max_val=1)
        with pe.If(flag == 1):
            with pe.Fori(0, chunks // 2) as t:
                with pe.Fori(0, groups) as k:
                    pe.wait_ge(big_hot, t * groups + k + 1)
                    every = hot[:].rearrange("p s w t m -> p (s w t m)")[:, 0:4 * HALF * P].rearrange("p (u t m) -> p u t m", t=2, m=P)
                    for v in range(2):
                        for u in range(2 * HALF):
                            last = T.matmul(ps_a[0][:, v * DST:(v + 1) * DST], every[:, u, v], big[:, u, 0:DST],
                                            start=(u == 0), stop=(u == 2 * HALF - 1))
                    last.then_inc(big_sum, 1)

        def turn(s, k):
            of = acc[:, s, 2] if layer else o_rows[:, s]
            pe.wait_ge(y4[s] if layer else o_set[s], k + 1 if layer else k * HALF + HALF)
            last_one = before(s, k, 1)
            if exists(last_one):
                pe.wait_ge(cols_set[last_one[0]], last_one[1] + 1)
            for u in range(HALF):
                last = T.transpose(ps_t[0:C, u * P:(u + 1) * P], of[:, u, :], ident[:])
            last.then_inc(turned[s], 1)

        def product(s, k):
            pe.wait_ge(cols_set[s], k + 1)
            last_one = before(s, k, 1)
            if exists(last_one):
                pe.wait_ge(z_set[last_one[0]], last_one[1] * HALF + HALF)
            for u in range(HALF):
                last = T.matmul(ps_z[:, u * C:(u + 1) * C], o_cols[:, u * P:(u + 1) * P], w_conv[layer][:], start=True, stop=True)
            last.then_inc(z_ps[s], 1)

        def sum_edges(s, k):
            pe.wait_ge(hot_set[s], k * 2 + 2)
            two = before(s, k, 2)
            if exists(two):
                pe.wait_ge(y1[two[0]], two[1] * HALF + HALF if layer else two[1] + 1)
                if layer == 0:
                    pe.wait_ge(deg_set[two[0]], two[1] + 1)
            if layer:
                pe.wait_ge(z_in[s], k * 16 + 16)
                T.matmul(ps_a[s % 2][:, 0:HALF * C], ident[:], zr[:, s].rearrange("p t c -> p (t c)"), start=True, stop=False)
            for u in range(HALF):
                for w in range(WINDOW):
                    last = T.matmul(ps_a[s % 2][:, u * width:(u + 1) * width], hot[:, s, u // 2 * WINDOW + w, u % 2, :],
                                    win[:, s, u // 2, w, 0:width], start=(layer == 0 and w == 0),
                                    stop=(w == WINDOW - 1 and (layer == 0 or u == HALF - 1)))
            last.then_inc(summed[s], 1)

        def own_features(s, k):
            pe.wait_ge(xc_in[s], k * 16 + 16)
            two = before(s, k, 2)
            if exists(two):
                pe.wait_ge(own_relu[two[0]], two[1] * 2 + 2)
                pe.wait_ge(y2[two[0]], two[1] * 2 + 2)
            for u in range(HALF):
                to = ps_own[u // 2][s % 2][:, (u % 2) * 2 * C:(u % 2 + 1) * 2 * C]
                last = T.matmul(to, xc[:, s, u // 2 * 2 * P + u % 2:(u // 2 + 1) * 2 * P:2],
                                w_node[:].rearrange("p k c -> p (k c)"), start=True, stop=True)
            last.then_inc(own_x[s], 1)

        def step(s, it):
            here, old = (s, it), before(s, it, turn_lag)
            if has_z and exists(old):
                turn(*old)
            if exists(here):
                if layer == 0:
                    own_features(*here)
                sum_edges(*here)
            if has_z and exists(old):
                product(*old)
        all_steps(pe, step, last_lag)

    @block.scalar
    def _(act):
        def own_features(s, k):
            act.wait_ge(own_x[s], k + 1)
            if later(k):
                act.wait_ge(own_scaled[s], k)
            for j in range(2):
                nc.scalar.activation(acc[:, s, 0, 2 * j:2 * j + 2], own_part(s, j, 0), ACT.Relu).then_inc(own_relu[s], 1)

        def sums_out(s, k):
            act.wait_ge(summed[s], k + 1)
            if layer == 0:
                if later(k):
                    act.wait_ge(shifts[s], k)
                    act.wait_ge(deg_root[s], k)
                nc.scalar.copy(deg[:, s], ps_a[s % 2][:, 0:HALF * (C + 1)].rearrange("p (t c) -> p t c", t=HALF)[:, :, C]).then_inc(deg_set[s], 1)
                return
            if later(k):
                act.wait_ge(y4[s], k)
            for u in range(HALF):
                nc.scalar.activation(acc[:, s, 0, u], ps_a[s % 2][:, u * C:(u + 1) * C], ACT.Copy,
                                     scale=dinv[:, bass.ds(tile(s, k) + u, 1)]).then_inc(y1[s], 1)

        def square_roots(s, k):
            act.wait_ge(var_set[s], k + 1)
            if later(k):
                act.wait_ge(rstd_set[s], k)
            nc.scalar.activation(dev[:, s, 0], mv[:, s, 4], ACT.Sqrt, bias=offsets[:, 0:1]).then_inc(roots[s], 1)

        def degree_roots(s, k):
            act.wait_ge(deg_set[s], k + 1)
            if later(k):
                act.wait_ge(dinv_set[s], k)
            nc.scalar.activation(dev[:, s, 1], deg[:, s], ACT.Sqrt, bias=offsets[:, 1:2]).then_inc(deg_root[s], 1)

        def norm(s, k):
            act.wait_ge(lifted[s], k + 1)
            if later(k):
                act.wait_ge(o_out[s], k * 16)
                if layer == 0:
                    act.wait_ge(turned[s], k)
            for u in range(HALF):
                nc.scalar.activation(o_rows[:, s, u], acc[:, s, 1 if layer else 2, u], ACT.Identity,
                                     bias=lift[:, s, u:u + 1], scale=inv[:, s, u:u + 1]).then_inc(o_set[s], 1)
            act.wait_ge(o_set[s], k * HALF + HALF)
            act.dma_start(tiles_of(out if layer else x1_tab, tile(s, k) * P), by_pair(o_rows[:, s])).then_inc(o_out[s], 16)

        def columns(s, k):
            act.wait_ge(turned[s], k + 1)
            last_one = before(s, k, 1)
            if exists(last_one):
                act.wait_ge(z_ps[last_one[0]], last_one[1] + 1)
            nc.scalar.copy(o_cols[:], ps_t[0:C, :]).then_inc(cols_set[s], 1)

        def next_rows(s, k):
            act.wait_ge(z_ps[s], k + 1)
            if layer == 0:
                act.wait_ge(dinv_set[s], k + 1)
            if later(k):
                act.wait_ge(z_st[s], k * 16)
            if not peeled(k):
                act.sem_inc(act_passed, 1)
            for u in range(HALF):
                nc.scalar.activation(z_out[:, s, u], ps_z[:, u * C:(u + 1) * C], ACT.Copy,
                                     scale=dinv[:, bass.ds(tile(s, k) + u, 1)]).then_inc(z_set[s], 1)
            act.wait_ge(z_set[s], k * HALF + HALF)
            act.dma_start(tiles_of(z_to, tile(s, k) * P), by_pair(z_out[:, s])).then_inc(z_st[s], 16)

        def step(s, it):
            here, one, two, three, old = (s, it), *(before(s, it, j) for j in (1, 2, 3, turn_lag))
            if has_z and exists(old):
                columns(*old)
            if has_ln and exists(three):
                norm(*three)
            if layer == 0 and exists(one):
                degree_roots(*one)
            if layer == 0 and exists(here):
                own_features(*here)
            if has_ln and exists(two):
                square_roots(*two)
            if exists(here):
                sums_out(*here)
            if has_z and exists(old):
                next_rows(*old)
        if has_ln:
            act.wait_ge(numbered, 2 * WINDOW + 3)
        all_steps(act, step, last_lag)
        if has_ln:
            all_of(act, o_out, 16)
        if has_z:
            all_of(act, z_st, 16)


_SHAPE_ROWS = 2 * COLS


def lay_out(inputs):
    import numpy as np

    g = {k: np.asarray(v) for k, v in inputs.items()}
    n = g["x"].shape[0]
    n_pad = -(-n // _SHAPE_ROWS) * _SHAPE_ROWS
    more = n_pad - n

    def by_chunk(v):
        return np.ascontiguousarray(v.reshape(-1, P).T)

    src = np.concatenate([g["src"], np.zeros(more, np.int32)])
    dst = np.concatenate([g["dst"], np.full(more, n_pad - 1, np.int32)])
    nxt = np.concatenate([dst[1:], np.full(1, n_pad - 1, np.int32)])
    x = np.concatenate([g["x"], np.zeros((more, C), np.float32)])
    ea = np.concatenate([g["edge_attr_4"], np.zeros((more, 4), np.float32)])
    one = np.ones((1, n_pad), np.float32)
    row = lambda k: g[k].reshape(1, C)
    firsts = np.broadcast_to(dst[::2 * P], (P, n_pad // (2 * P)))
    a = {
        "x": np.concatenate([x, np.zeros((WIN, C), np.float32)]), "dst_row": dst.reshape(1, -1), "dst_first": firsts, "xT": np.concatenate([x.T, one]), "eaT": np.concatenate([ea.T, one]),
        "src": by_chunk(src), "dst": by_chunk(dst), "dst_next": by_chunk(nxt),
        "W_edge": g["L0_gnn_W_edge"], "b_edge": row("L0_gnn_b_edge"),
        "W_node": g["L0_gnn_W_node"], "b_node": row("L0_gnn_b_node"),
        "W_msg": g["L0_gnn_W_msg"], "b_msg": row("L0_gnn_b_msg"),
        "gb": np.stack([g[f"L0_gnn_{k}_{w}"] for w in ("edge", "msg", "node") for k in ("g", "beta")], 1),
        "W1": g["L1_gnn_W1"], "W2": g["L1_gnn_W2"],
        "b1": row("L1_gnn_b1"), "b2": row("L1_gnn_b2"), "prelu": row("L1_gnn_prelu_a"),
    }
    return n, n_pad, {k: np.ascontiguousarray(v) for k, v in a.items()}


def kernel(**inputs):
    import concourse.bacc as _bacc
    from concourse.bass_utils import run_bass_kernel_spmd as _run

    n, n_pad, arrays = lay_out(inputs)
    nc = _bacc.Bacc("TRN2", target_bir_lowering=False, num_devices=1)
    args = {k: nc.dram_tensor(f"in_{k}", v.shape, mybir.dt.from_np(v.dtype), kind="ExternalInput").ap()
            for k, v in arrays.items()}
    out = nc.dram_tensor("out_0", (n_pad, C), F32, kind="ExternalOutput").ap()
    build_program(nc, n, args, out)
    r = _run(nc, [{f"in_{k}": v for k, v in arrays.items()}], core_ids=[0])
    return r.results[0]["out_0"][:n]
```
